# Optimizing a Trainium2 kernel written in Bass

```python
import numpy as np
import jax
import jax.numpy as jnp

def _softmax(x, axis=-1):
    return jax.nn.softmax(x, axis=axis)

def _gelu(x):
    return jax.nn.gelu(x, approximate=True)

def _silu(x):
    return jax.nn.silu(x)

def _sigmoid(x):
    return jax.nn.sigmoid(x)

def _layernorm(x, axis=-1, eps=1e-05):
    m = jnp.mean(x, axis=axis, keepdims=True)
    v = jnp.var(x, axis=axis, keepdims=True)
    return (x - m) / jnp.sqrt(v + eps)

def _scatter_add(tgt, idx, src, axis=0):
    return tgt.at[idx].add(src)

def _segment_sum(src, seg, n):
    return jax.ops.segment_sum(src, seg, n)
kernel_name = 'mk_seq_postln_d2_jaxref_r8_5b15f9'

def setup_inputs(seed: int=0):
    np.random.seed(seed)
    _w = jnp.asarray

    def _L0_attn_setup():
        import jax, jax.numpy as jnp
        import numpy as np
        N_HEAD = 32
        ROPE_BASE = 10000.0

        def _rope_cos_sin(T, n_elem, dtype):
            theta = 1.0 / ROPE_BASE ** (jnp.arange(0, n_elem, 2, dtype=dtype) / n_elem)
            seq_idx = jnp.arange(T, dtype=dtype)
            idx_theta = jnp.outer(seq_idx, theta)
            idx_theta2 = jnp.concatenate([idx_theta, idx_theta], axis=-1)
            return (jnp.cos(idx_theta2), jnp.sin(idx_theta2))

        def _apply_rope(x, cos, sin):
            d2 = x.shape[-1] // 2
            rot = jnp.concatenate([-x[..., d2:], x[..., :d2]], axis=-1)
            return x * cos + rot * sin
        key = jax.random.key(seed)
        k1, k2, k3, k4 = jax.random.split(key, 4)
        B, T, C = (1, 256, 512)
        s_in = 1.0 / np.sqrt(C)
        return {'x': jax.random.normal(k1, (B, T, C), jnp.float32), 'w_attn': jax.random.normal(k2, (3 * C, C), jnp.float32) * s_in, 'w_proj': jax.random.normal(k3, (C, C), jnp.float32) * s_in, 'adapter_wte': jax.random.normal(k4, (10, C), jnp.float32), 'gating': jnp.ones((1,), jnp.float32)}
    _L0_attn_in = _L0_attn_setup()

    def _L0_ffn_setup():
        import jax, jax.numpy as jnp
        import numpy as np
        HID, BOT, RDIM, NSLOT, K, VB = (512, 64, 48, 128, 8, 32)
        TAU_LOW, TAU_HIGH, EARLY_EXIT = (0.5, 2.0, 0.05)

        def _uncertainty(h, Wu1, bu1, Wu2, bu2):
            var = jnp.var(h, axis=-1)
            log_var = jnp.log1p(var)
            norm_var = log_var / (jnp.mean(log_var) + 1e-06)
            learned = (jax.nn.gelu(h @ Wu1.T + bu1) @ Wu2.T + bu2)[..., 0]
            return jnp.clip(norm_var * 0.5 + jax.nn.sigmoid(learned) * 2.5, 0.0, 5.0)
        key = jax.random.key(seed)
        ks = jax.random.split(key, 12)
        B, S = (2, 256)
        return {'hidden_states': jax.random.normal(ks[0], (B, S, HID), dtype=jnp.float32), 'Wq': jax.random.normal(ks[1], (BOT, HID), dtype=jnp.float32) / np.sqrt(HID), 'Wr': jax.random.normal(ks[2], (RDIM, BOT), dtype=jnp.float32) / np.sqrt(BOT), 'aux_keys': jax.random.normal(ks[3], (NSLOT, BOT), dtype=jnp.float32) * 0.01, 'aux_values': jax.random.normal(ks[4], (NSLOT, HID), dtype=jnp.float32) * 0.02, 'Wvd': jax.random.normal(ks[5], (VB, HID), dtype=jnp.float32) * 0.1 / np.sqrt(HID), 'Wvu': jax.random.normal(ks[6], (HID, VB), dtype=jnp.float32) * 0.1 / np.sqrt(VB), 'Wu1': jax.random.normal(ks[7], (HID // 4, HID), dtype=jnp.float32) / np.sqrt(HID), 'bu1': jnp.zeros((HID // 4,), dtype=jnp.float32), 'Wu2': jax.random.normal(ks[8], (1, HID // 4), dtype=jnp.float32) * 0.01, 'bu2': jnp.zeros((1,), dtype=jnp.float32), 'gate_w1': jnp.float32(0.5), 'gate_bias': jnp.float32(-1.0), 'log_rel': jnp.zeros((NSLOT,), dtype=jnp.float32)}
    _L0_ffn_in = _L0_ffn_setup()

    def _L1_attn_setup():
        import jax, jax.numpy as jnp
        import numpy as np
        import math
        B, T, D_IN, D_OUT = (2, 256, 512, 512)
        N_HEADS, N_KV = (32, 8)
        HEAD_DIM = D_OUT // N_HEADS
        GROUP_SIZE = N_HEADS // N_KV
        ROPE_BASE = 500000.0
        CTX = 256

        def _rope_tables(head_dim, base, seq_len):
            inv_freq = 1.0 / base ** (jnp.arange(0, head_dim, 2, dtype=jnp.float32) / head_dim)
            t = jnp.arange(seq_len, dtype=jnp.float32)
            freqs = jnp.einsum('i,j->ij', t, inv_freq)
            return (jnp.cos(freqs), jnp.sin(freqs))

        def _apply_rope(x, cos, sin):
            x1, x2 = jnp.split(x, 2, axis=-1)
            c = cos[None, None]
            s = sin[None, None]
            return jnp.concatenate([x1 * c - x2 * s, x1 * s + x2 * c], axis=-1)
        key = jax.random.key(seed)
        ks = jax.random.split(key, 5)
        scale = 0.02
        return {'x': jax.random.normal(ks[0], (B, T, D_IN), dtype=jnp.float32), 'Wq': jax.random.normal(ks[1], (D_IN, D_OUT), dtype=jnp.float32) * scale, 'Wk': jax.random.normal(ks[2], (D_IN, N_KV * HEAD_DIM), dtype=jnp.float32) * scale, 'Wv': jax.random.normal(ks[3], (D_IN, N_KV * HEAD_DIM), dtype=jnp.float32) * scale, 'Wo': jax.random.normal(ks[4], (D_OUT, D_OUT), dtype=jnp.float32) * scale}
    _L1_attn_in = _L1_attn_setup()

    def _L1_ffn_setup():
        import jax, jax.numpy as jnp
        import numpy as np
        HIDDEN = 512
        INTER = 1376
        BATCH, SEQ = (2, 256)

        def _ternary(key, shape):
            return jax.random.randint(key, shape, -1, 2).astype(jnp.float32)
        key = jax.random.key(seed)
        kx, kg, ku, kd = jax.random.split(key, 4)
        x = jax.random.normal(kx, (BATCH, SEQ, HIDDEN), dtype=jnp.float32)
        gate_w = _ternary(kg, (INTER, HIDDEN))
        up_w = _ternary(ku, (INTER, HIDDEN))
        down_w = _ternary(kd, (HIDDEN, INTER))
        gate_scale = jnp.float32(0.02)
        up_scale = jnp.float32(0.02)
        down_scale = jnp.float32(0.02)
        return {'x': x, 'gate_w': gate_w, 'up_w': up_w, 'down_w': down_w, 'gate_scale': gate_scale, 'up_scale': up_scale, 'down_scale': down_scale}
    _L1_ffn_in = _L1_ffn_setup()
    _d = {'L0_attn_x': _L0_attn_in['x'], 'L0_attn_w_attn': _L0_attn_in['w_attn'], 'L0_attn_w_proj': _L0_attn_in['w_proj'], 'L0_attn_adapter_wte': _L0_attn_in['adapter_wte'], 'L0_attn_gating': _L0_attn_in['gating'], 'L0_ffn_Wq': _L0_ffn_in['Wq'], 'L0_ffn_Wr': _L0_ffn_in['Wr'], 'L0_ffn_aux_keys': _L0_ffn_in['aux_keys'], 'L0_ffn_aux_values': _L0_ffn_in['aux_values'], 'L0_ffn_Wvd': _L0_ffn_in['Wvd'], 'L0_ffn_Wvu': _L0_ffn_in['Wvu'], 'L0_ffn_Wu1': _L0_ffn_in['Wu1'], 'L0_ffn_bu1': _L0_ffn_in['bu1'], 'L0_ffn_Wu2': _L0_ffn_in['Wu2'], 'L0_ffn_bu2': _L0_ffn_in['bu2'], 'L0_ffn_gate_w1': _L0_ffn_in['gate_w1'], 'L0_ffn_gate_bias': _L0_ffn_in['gate_bias'], 'L0_ffn_log_rel': _L0_ffn_in['log_rel'], 'L1_attn_Wq': _L1_attn_in['Wq'], 'L1_attn_Wk': _L1_attn_in['Wk'], 'L1_attn_Wv': _L1_attn_in['Wv'], 'L1_attn_Wo': _L1_attn_in['Wo'], 'L1_ffn_gate_w': _L1_ffn_in['gate_w'], 'L1_ffn_up_w': _L1_ffn_in['up_w'], 'L1_ffn_down_w': _L1_ffn_in['down_w'], 'L1_ffn_gate_scale': _L1_ffn_in['gate_scale'], 'L1_ffn_up_scale': _L1_ffn_in['up_scale'], 'L1_ffn_down_scale': _L1_ffn_in['down_scale']}
    _x0 = _d['L0_attn_x']
    _d['L0_attn_x'] = jax.random.normal(jax.random.fold_in(jax.random.key(seed), 1), (1, 1024, 512), dtype=_x0.dtype)
    del _x0
    return _d

def reference(L0_attn_x, L0_attn_w_attn, L0_attn_w_proj, L0_attn_adapter_wte, L0_attn_gating, L0_ffn_Wq, L0_ffn_Wr, L0_ffn_aux_keys, L0_ffn_aux_values, L0_ffn_Wvd, L0_ffn_Wvu, L0_ffn_Wu1, L0_ffn_bu1, L0_ffn_Wu2, L0_ffn_bu2, L0_ffn_gate_w1, L0_ffn_gate_bias, L0_ffn_log_rel, L1_attn_Wq, L1_attn_Wk, L1_attn_Wv, L1_attn_Wo, L1_ffn_gate_w, L1_ffn_up_w, L1_ffn_down_w, L1_ffn_gate_scale, L1_ffn_up_scale, L1_ffn_down_scale):

    def _L0_attn_ref(x, w_attn, w_proj, adapter_wte, gating):
        import jax, jax.numpy as jnp
        import numpy as np
        N_HEAD = 32
        ROPE_BASE = 10000.0

        def _rope_cos_sin(T, n_elem, dtype):
            theta = 1.0 / ROPE_BASE ** (jnp.arange(0, n_elem, 2, dtype=dtype) / n_elem)
            seq_idx = jnp.arange(T, dtype=dtype)
            idx_theta = jnp.outer(seq_idx, theta)
            idx_theta2 = jnp.concatenate([idx_theta, idx_theta], axis=-1)
            return (jnp.cos(idx_theta2), jnp.sin(idx_theta2))

        def _apply_rope(x, cos, sin):
            d2 = x.shape[-1] // 2
            rot = jnp.concatenate([-x[..., d2:], x[..., :d2]], axis=-1)
            return x * cos + rot * sin
        B, T, C = x.shape
        H = N_HEAD
        hd = C // H
        qkv = jnp.einsum('btc,oc->bto', x, w_attn)
        q, k, v = jnp.split(qkv, 3, axis=-1)
        q = q.reshape(B, T, H, hd).transpose(0, 2, 1, 3)
        k = k.reshape(B, T, H, hd).transpose(0, 2, 1, 3)
        v = v.reshape(B, T, H, hd).transpose(0, 2, 1, 3)
        cos, sin = _rope_cos_sin(T, hd, x.dtype)
        q = _apply_rope(q, cos, sin)
        k = _apply_rope(k, cos, sin)
        scores = jnp.einsum('bhqd,bhkd->bhqk', q, k) / jnp.sqrt(jnp.asarray(hd, x.dtype))
        causal = jnp.tril(jnp.ones((T, T), bool))
        scores = jnp.where(causal, scores, jnp.asarray(-jnp.inf, x.dtype))
        attn = jax.nn.softmax(scores, axis=-1)
        y = jnp.einsum('bhqk,bhkd->bhqd', attn, v)
        aT = adapter_wte.shape[0]
        prefix = adapter_wte[None]
        aqkv = jnp.einsum('btc,oc->bto', prefix, w_attn)
        _, ak, av = jnp.split(aqkv, 3, axis=-1)
        ak = ak.reshape(1, aT, H, hd).transpose(0, 2, 1, 3)
        av = av.reshape(1, aT, H, hd).transpose(0, 2, 1, 3)
        ascores = jnp.einsum('bhqd,xhkd->bhqk', q, ak) / jnp.sqrt(jnp.asarray(C, x.dtype))
        ascores = gating[0] * jax.nn.softmax(ascores.astype(jnp.float32), axis=-1).astype(q.dtype)
        y = y + jnp.einsum('bhqk,xhkd->bhqd', ascores, av)
        y = y.transpose(0, 2, 1, 3).reshape(B, T, C)
        return jnp.einsum('btc,oc->bto', y, w_proj)

    def _L0_ffn_ref(hidden_states, Wq, Wr, aux_keys, aux_values, Wvd, Wvu, Wu1, bu1, Wu2, bu2, gate_w1, gate_bias, log_rel):
        import jax, jax.numpy as jnp
        import numpy as np
        HID, BOT, RDIM, NSLOT, K, VB = (512, 64, 48, 128, 8, 32)
        TAU_LOW, TAU_HIGH, EARLY_EXIT = (0.5, 2.0, 0.05)

        def _uncertainty(h, Wu1, bu1, Wu2, bu2):
            var = jnp.var(h, axis=-1)
            log_var = jnp.log1p(var)
            norm_var = log_var / (jnp.mean(log_var) + 1e-06)
            learned = (jax.nn.gelu(h @ Wu1.T + bu1) @ Wu2.T + bu2)[..., 0]
            return jnp.clip(norm_var * 0.5 + jax.nn.sigmoid(learned) * 2.5, 0.0, 5.0)
        query = hidden_states @ Wq.T
        rq = query @ Wr.T
        rk = aux_keys @ Wr.T
        router_scores = jnp.einsum('bsr,nr->bsn', rq, rk) / np.sqrt(RDIM) + log_rel
        top_scores, top_idx = jax.lax.top_k(router_scores, K)
        sel_keys = aux_keys[top_idx]
        attn = jnp.einsum('bsd,bskd->bsk', query, sel_keys) / np.sqrt(BOT) + log_rel[top_idx]
        w = jax.nn.softmax(attn, axis=-1)
        sel_vals = aux_values[top_idx]
        aux_out = jnp.einsum('bsk,bskh->bsh', w, sel_vals)
        aux_out = aux_out @ Wvd.T @ Wvu.T
        u = _uncertainty(hidden_states, Wu1, bu1, Wu2, bu2)
        u_norm = jnp.clip((u - TAU_LOW) / (TAU_HIGH - TAU_LOW), 0.0, 1.0)
        gate = jax.nn.sigmoid(gate_w1 * u_norm + gate_bias)
        gate = jnp.where(gate < EARLY_EXIT, 0.0, gate)
        return hidden_states + gate[..., None] * aux_out

    def _L1_attn_ref(x, Wq, Wk, Wv, Wo):
        import jax, jax.numpy as jnp
        import numpy as np
        import math
        B, T, D_IN, D_OUT = (2, 256, 512, 512)
        N_HEADS, N_KV = (32, 8)
        HEAD_DIM = D_OUT // N_HEADS
        GROUP_SIZE = N_HEADS // N_KV
        ROPE_BASE = 500000.0
        CTX = 256

        def _rope_tables(head_dim, base, seq_len):
            inv_freq = 1.0 / base ** (jnp.arange(0, head_dim, 2, dtype=jnp.float32) / head_dim)
            t = jnp.arange(seq_len, dtype=jnp.float32)
            freqs = jnp.einsum('i,j->ij', t, inv_freq)
            return (jnp.cos(freqs), jnp.sin(freqs))

        def _apply_rope(x, cos, sin):
            x1, x2 = jnp.split(x, 2, axis=-1)
            c = cos[None, None]
            s = sin[None, None]
            return jnp.concatenate([x1 * c - x2 * s, x1 * s + x2 * c], axis=-1)
        b, t, _ = x.shape
        cos, sin = _rope_tables(HEAD_DIM, ROPE_BASE, t)
        q = (x @ Wq).reshape(b, t, N_HEADS, HEAD_DIM).transpose(0, 2, 1, 3)
        k = (x @ Wk).reshape(b, t, N_KV, HEAD_DIM).transpose(0, 2, 1, 3)
        v = (x @ Wv).reshape(b, t, N_KV, HEAD_DIM).transpose(0, 2, 1, 3)
        q = _apply_rope(q, cos, sin)
        k = _apply_rope(k, cos, sin)
        k_h = jnp.repeat(k, GROUP_SIZE, axis=1)
        v_h = jnp.repeat(v, GROUP_SIZE, axis=1)
        scores = jnp.einsum('bhqd,bhkd->bhqk', q, k_h) / math.sqrt(HEAD_DIM)
        causal = jnp.triu(jnp.ones((t, t), dtype=bool), k=1)
        scores = jnp.where(causal[None, None], jnp.finfo(scores.dtype).min, scores)
        attn = jax.nn.softmax(scores, axis=-1)
        ctx = jnp.einsum('bhqk,bhkd->bhqd', attn, v_h)
        ctx = ctx.transpose(0, 2, 1, 3).reshape(b, t, D_OUT)
        return ctx @ Wo

    def _L1_ffn_ref(x, gate_w, up_w, down_w, gate_scale, up_scale, down_scale):
        import jax, jax.numpy as jnp
        import numpy as np
        HIDDEN = 512
        INTER = 1376
        BATCH, SEQ = (2, 256)

        def _ternary(key, shape):
            return jax.random.randint(key, shape, -1, 2).astype(jnp.float32)
        gate = jnp.einsum('bsh,ih->bsi', x, gate_w) * gate_scale
        up = jnp.einsum('bsh,ih->bsi', x, up_w) * up_scale
        inter = jax.nn.silu(gate) * up
        out = jnp.einsum('bsi,hi->bsh', inter, down_w) * down_scale
        return out
    x = L0_attn_x
    x = _layernorm(x + _L0_attn_ref(x, L0_attn_w_attn, L0_attn_w_proj, L0_attn_adapter_wte, L0_attn_gating), axis=-1)
    x = _layernorm(x + _L0_ffn_ref(x, L0_ffn_Wq, L0_ffn_Wr, L0_ffn_aux_keys, L0_ffn_aux_values, L0_ffn_Wvd, L0_ffn_Wvu, L0_ffn_Wu1, L0_ffn_bu1, L0_ffn_Wu2, L0_ffn_bu2, L0_ffn_gate_w1, L0_ffn_gate_bias, L0_ffn_log_rel), axis=-1)
    x = _layernorm(x + _L1_attn_ref(x, L1_attn_Wq, L1_attn_Wk, L1_attn_Wv, L1_attn_Wo), axis=-1)
    x = _layernorm(x + _L1_ffn_ref(x, L1_ffn_gate_w, L1_ffn_up_w, L1_ffn_down_w, L1_ffn_gate_scale, L1_ffn_up_scale, L1_ffn_down_scale), axis=-1)
    return x

_drawn_inputs = setup_inputs


def setup_inputs(seed=0):
    import zlib

    import numpy as np

    out = dict(_drawn_inputs(seed))
    spreads = {'L0_ffn_bu1': (0.0, 2.0), 'L0_ffn_log_rel': (0.0, 2.0)}
    factors = {'L0_ffn_Wq': 44.894,
     'L0_ffn_Wr': 52.945,
     'L0_ffn_aux_keys': 44.169,
     'L0_ffn_aux_values': 42.697,
     'L0_ffn_Wvd': 42.984,
     'L0_ffn_Wvu': 42.545,
     'L0_ffn_Wu1': 64.0,
     'L0_ffn_Wu2': 64.0,
     'L1_attn_Wq': 8.0,
     'L1_attn_Wk': 8.0}
    for name, (base, spread) in spreads.items():
        noise = np.random.default_rng([zlib.crc32(name.encode()), seed]).standard_normal(out[name].shape)
        drawn = base * np.exp(spread * noise) if base else spread * noise
        out[name] = jnp.asarray(drawn.astype(out[name].dtype))
    for name, factor in factors.items():
        out[name] = (out[name] * factor).astype(out[name].dtype)
    return out
```

```python
from contextlib import ExitStack

import numpy as np

import concourse.bass as bass
from concourse import mybir

F32 = mybir.dt.float32
BF16 = mybir.dt.bfloat16
ALU = mybir.AluOpType
ACT = mybir.ActivationFunctionType
AX = mybir.AxisListType.X

P = 128
T, C = 1024, 512
H, D = 32, 16
NT = T // P
KC = C // P
CH = T // 512
R = 4
NG = H // R
KV1 = 8
NPART = 3
PAIRS = [(0, 0), (1, 0), (2, 0), (0, 1), (1, 1), (0, 2)]
KS = len(PAIRS) * D
KM = KS + NPART
VW = 32
ADP = 10
HPT = P // D
BOT, RDIM, NSLOT, VB, HU = 64, 48, 128, 32, 128
INTER = 1376
NI = -(-INTER // P)
EPS = 1e-5
BIG = 1e30
NP_RING = 4
S2_RING = 2
AHEAD = 2


def view(arena, offset, dims, dtype=F32, parts=P):
    n = int(np.prod(dims))
    size = 4 if dtype == F32 else 2
    assert offset % 4 == 0 and (n * size) % 4 == 0
    ap = arena[0:parts, offset // 4:offset // 4 + n * size // 4]
    if dtype != F32:
        ap = ap.bitcast(dtype)
    if len(dims) > 1:
        names = "abcd"[:len(dims)]
        ap = ap.rearrange(f"p ({' '.join(names)}) -> p {' '.join(names)}",
                          **{k: int(v) for k, v in zip(names, dims)})
    return ap


class Chain:

    def __init__(self, engine, semaphore):
        self.engine, self.semaphore, self.count = engine, semaphore, 0

    def __call__(self, instruction):
        self.count += 1
        instruction.then_inc(self.semaphore, 1)
        self.engine.wait_ge(self.semaphore, self.count)


def build(nc, d, out):
    with ExitStack() as stack:
        def sb(name, shape, dtype=F32):
            return stack.enter_context(nc.sbuf_tensor(name, shape, dtype))

        x_tok = sb("x_tok", [P, NT, C])
        xT = sb("xT", [P, KC, T])
        v_tok = sb("v_tok", [P, NT, C])
        ident = sb("ident", [P, P])
        ident_b = sb("ident_b", [P, P], BF16)
        maskb = sb("maskb", [P, P], BF16)
        arena_o = sb("arena_o", [P, 8192])
        arena_s = sb("arena_s", [P, 12288])
        arena_p = sb("arena_p", [P, 4096])
        v_grp = sb("v_grp", [P, 2, NT, R, VW])
        arena_w = sb("arena_w", [P, 6144])
        arena_f = sb("arena_f", [P, 4096])
        small = sb("small", [P, 2600])
        psum = stack.enter_context(nc.psum_tensor("psum", [P, 8, 512], F32))

        q_parts = [nc.dram_tensor(f"q_parts{n}", [H, NPART, D, T], BF16, kind="Internal").ap()
                   for n in range(2)]
        k_parts = [nc.dram_tensor(f"k_parts{n}", [h, NPART, D, T], BF16, kind="Internal").ap()
                   for n, h in ((0, H), (1, KV1))]

        wq_b = view(small, 0, [KC, BOT])
        wr_b = view(small, 1024, [RDIM], parts=BOT)
        akey_b = view(small, 1216, [NSLOT], parts=BOT)
        av_b = view(small, 1728, [KC, NSLOT])
        wvd_b = view(small, 3776, [KC, VB])
        wvu_b = view(small, 4288, [C], parts=VB)
        wu1_b = view(small, 6336, [KC, HU])
        wu2_b = view(small, 8384, [1])
        bu1_b = view(small, 8388, [1])
        logrel_b = view(small, 8392, [NSLOT])
        scal = view(small, 8904, [7])
        bu2, gate_w1, gate_bias, gating, s_gate, s_up, s_down = (scal[:, n:n + 1] for n in range(7))
        ones = view(small, 8932, [P])
        eps = view(small, 9444, [1])

        load_and_project(nc, d, 0, dict(
            x_tok=x_tok, xT=xT, v_tok=v_tok, arena_o=arena_o, arena_p=arena_p, arena_w=arena_w,
            arena_f=arena_f, ident=ident, ident_b=ident_b, maskb=maskb, psum=psum, v_grp=v_grp,
            arena_s=arena_s, q_parts=q_parts[0], k_parts=k_parts[0], ones=ones, eps=eps,
            small_loads=[
                (wq_b, d["f_wqT"]), (wr_b, d["f_wrT"]), (akey_b, d["f_akeyT"]), (av_b, d["f_avT"]),
                (wvd_b, d["f_wvdT"]), (wvu_b, d["f_wvuT"]), (wu1_b, d["f_wu1T"]),
                (wu2_b, d["f_wu2T"]), (bu1_b, d["f_bu1"]), (logrel_b, d["f_logrel"]),
                *[(scal[:, n:n + 1], d[k]) for n, k in enumerate(
                    ["f_bu2", "f_gate_w1", "f_gate_bias", "gating", "s_gate", "s_up", "s_down"])],
            ]))
        adapter(nc, d, x_tok, arena_o, arena_w, arena_f, ident, gating, psum)
        attention(nc, 0, arena_o, arena_s, arena_p, v_tok, v_grp, ident_b, maskb,
                  q_parts[0], k_parts[0], psum)
        finish_attention(nc, 0, d, x_tok, xT, v_tok, arena_o, arena_s, arena_w,
                         view(arena_f, 0, [KC, C]), ident, eps, psum)
        lookup(nc, d, x_tok, xT, arena_o, arena_s, ident, ones, eps, psum,
               wq_b, wr_b, akey_b, av_b, wvd_b, wvu_b, wu1_b, wu2_b, bu1_b, logrel_b,
               bu2, gate_w1, gate_bias)
        load_and_project(nc, d, 1, dict(
            x_tok=x_tok, xT=xT, v_tok=v_tok, arena_o=arena_o, arena_p=arena_p, arena_w=arena_w,
            arena_f=arena_f, ident=ident, ident_b=ident_b, maskb=maskb, psum=psum, v_grp=v_grp,
            arena_s=arena_s, q_parts=q_parts[1], k_parts=k_parts[1], ones=ones, eps=eps, small_loads=[]))
        attention(nc, 1, arena_o, arena_s, arena_p, v_tok, v_grp, ident_b, maskb,
                  q_parts[1], k_parts[1], psum)
        finish_attention(nc, 1, d, x_tok, xT, v_tok, arena_o, arena_s, arena_w,
                         view(arena_w, 12288, [KC, C]), ident, eps, psum)
        swiglu(nc, d, x_tok, xT, arena_o, arena_s, arena_f, s_gate, s_up, s_down, eps, psum, out)


class Phase:

    def __init__(self, nc, name, recycle=False):
        self.nc, self.name, self.stack, self.sems = nc, name, ExitStack(), []
        self.recycle = recycle

    def __enter__(self):
        return self

    def sem(self, name):
        self.sems.append(self.nc.alloc_semaphore(f"{self.name}_{name}"))
        return self.sems[-1]

    def block(self):
        return self.stack.enter_context(self.nc.Block())

    def __exit__(self, *what):
        self.stack.__exit__(*what)
        if self.recycle and what[0] is None:
            self.nc.clear_and_free_semaphores(self.sems)
            self.nc.all_engine_barrier()


def load_and_project(nc, d, layer, m):
    nk = 4 if layer == 0 else 1
    n_out = C + nk * P + (C if layer == 0 else P)
    vw = C if layer == 0 else P
    w = view(m["arena_w"], 0, [KC, n_out])
    cos = view(m["arena_p"], 0, [T])
    sin = view(m["arena_p"], 4096, [T])
    parts = view(m["arena_p"], 8192, [2, NPART, 512], BF16)
    rot = view(m["arena_p"], 8192 + 6144, [P])
    q_rot = view(m["arena_o"], 0, [KC, T])
    raw = view(m["arena_o"], 16384, [2, 512])
    t_cos = view(m["arena_o"], 20480, [2, 512])
    t_sin = view(m["arena_o"], 24576, [2, 512])
    k_rot = view(m["arena_o"], 28672, [2, 512])
    psum, xT, v_tok = m["psum"], m["xT"], m["v_tok"]
    units = [("q", t, c) for t in range(KC) for c in range(CH)] \
        + [("k", t, c) for t in range(nk) for c in range(CH)]
    n_units = len(units)

    def rotated(n):
        kind, t, c = units[n]
        return q_rot[:, t, 512 * c:512 * c + 512] if kind == "q" else k_rot[:, n % 2, :]

    with Phase(nc, f"proj{layer}") as ph:
        loaded, aux_loaded, tables = ph.sem("loaded"), ph.sem("aux_loaded"), ph.sem("tables")
        proj_ready, raw_ready, rot_ready = ph.sem("proj_ready"), ph.sem("raw_ready"), ph.sem("rot_ready")
        cos_ready, sin_ready, sum_ready = ph.sem("cos_ready"), ph.sem("sin_ready"), ph.sem("sum_ready")
        hi_ready, res_ready, mid_ready = ph.sem("hi_ready"), ph.sem("res_ready"), ph.sem("mid_ready")
        lo_ready = ph.sem("lo_ready")
        stored = [ph.sem("stored0"), ph.sem("stored1")]
        v_ready, v_copied, consts = ph.sem("v_ready"), ph.sem("v_copied"), ph.sem("consts")
        block = ph.block()

        @block.sync
        def _(sp):
            n_loads = 0
            if layer == 0:
                for k in range(KC):
                    sp.dma_start(xT[:, k, :], d["xT"][P * k:P * k + P, :]).then_inc(loaded, 16)
                    sp.dma_start(w[:, k, :], d["w0"][P * k:P * k + P, :]).then_inc(loaded, 16)
                    n_loads += 2
            sp.dma_start(rot, d["rot"]).then_inc(tables, 16)
            sp.dma_start(cos, d[f"cos{layer}"]).then_inc(tables, 16)
            sp.dma_start(sin, d[f"sin{layer}"]).then_inc(tables, 16)
            if layer == 0:
                n_aux = 0
                for dst, src in ((m["ident"][:, :], d["ident"]),
                                 (view(m["arena_f"], 0, [KC, C]), d["wo0"].rearrange("(k p) n -> p k n", p=P)),
                                 *m["small_loads"]):
                    if len(dst.shape) == 3 and len(src.shape) == 2:
                        src = src.rearrange("p (k n) -> p k n", k=KC)
                    sp.dma_start(dst, src).then_inc(aux_loaded, 16)
                    n_aux += 1
            for n, (kind, t, c) in enumerate(units):
                sp.wait_ge(lo_ready, n + 1)
                dest = m["q_parts"] if kind == "q" else m["k_parts"]
                for j in range(NPART):
                    sp.dma_start(dest[HPT * t:HPT * t + HPT, j, :, 512 * c:512 * c + 512],
                                 parts[:, n % 2, j, :]).then_inc(stored[n % 2], 16)
            for side in range(2):
                sp.wait_ge(stored[side], 16 * NPART * (n_units // 2))
            if layer == 0:
                sp.wait_ge(aux_loaded, 16 * n_aux)

        @block.tensor
        def _(pe):
            if layer == 0:
                pe.wait_ge(loaded, 16 * 2 * KC)

            def rotate(n):
                pe.wait_ge(raw_ready, n + 1)
                if n == 0:
                    pe.wait_ge(tables, 48)
                if n >= 2:
                    pe.wait_ge(sin_ready, n - 1)
                pe.matmul(psum[:, 2 + n % 2, :], rot, raw[:, n % 2, :], start=True, stop=True)\
                    .then_inc(rot_ready, 1)

            for n, (kind, t, c) in enumerate(units):
                if n >= 2:
                    pe.wait_ge(raw_ready, n - 1)
                col = (0 if kind == "q" else C) + P * t
                for k in range(KC):
                    last = pe.matmul(psum[:, n % 2, :], w[:, k, col:col + P],
                                     xT[:, k, 512 * c:512 * c + 512], start=k == 0, stop=k == KC - 1)
                last.then_inc(proj_ready, 1)
                if n >= 1:
                    rotate(n - 1)
            rotate(n_units - 1)
            for t in range(NT):
                if t >= 2:
                    pe.wait_ge(v_copied, t - 1)
                for k in range(KC):
                    last = pe.matmul(psum[:, 4 + t % 2, 0:vw], xT[:, k, P * t:P * t + P],
                                     w[:, k, C + nk * P:n_out], start=k == 0, stop=k == KC - 1)
                last.then_inc(v_ready, 1)

        @block.scalar
        def _(act):
            def high(n):
                act.wait_ge(sum_ready, n + 1)
                if n >= 2:
                    act.wait_ge(stored[n % 2], 16 * NPART * (n // 2))
                act.copy(parts[:, n % 2, 0, :], rotated(n)).then_inc(hi_ready, 1)

            for n in range(n_units):
                act.wait_ge(proj_ready, n + 1)
                if n >= 2:
                    act.wait_ge(rot_ready, n - 1)
                    act.wait_ge(cos_ready, n - 1)
                act.copy(raw[:, n % 2, :], psum[:, n % 2, :]).then_inc(raw_ready, 1)
                if n >= 1:
                    high(n - 1)
            high(n_units - 1)
            for t in range(NT):
                act.wait_ge(v_ready, t + 1)
                act.copy(v_tok[:, t, 0:vw], psum[:, 4 + t % 2, 0:vw]).then_inc(v_copied, 1)

        @block.vector
        def _(dve):
            def low(n):
                dve.wait_ge(res_ready, n + 1)
                dve.tensor_copy(parts[:, n % 2, 1, :], t_cos[:, n % 2, :]).then_inc(mid_ready, 1)
                dve.wait_ge(mid_ready, n + 1)
                dve.tensor_tensor(parts[:, n % 2, 2, :], t_cos[:, n % 2, :], parts[:, n % 2, 1, :],
                                  ALU.subtract).then_inc(lo_ready, 1)

            dve.wait_ge(tables, 48)
            for n, (kind, t, c) in enumerate(units):
                dve.wait_ge(rot_ready, n + 1)
                if n >= 2:
                    dve.wait_ge(sum_ready, n - 1)
                dve.tensor_tensor(t_sin[:, n % 2, :], psum[:, 2 + n % 2, :],
                                  sin[:, 512 * c:512 * c + 512], ALU.mult).then_inc(sin_ready, 1)
                if n >= 1:
                    low(n - 1)
            low(n_units - 1)

        @block.gpsimd
        def _(pool):
            if layer == 0:
                pool.memset(m["v_grp"][:, :, :, :, D:VW], 1.0).then_inc(consts, 1)
                pool.memset(m["ones"], 1.0).then_inc(consts, 1)
                pool.memset(m["eps"], EPS).then_inc(consts, 1)
                pool.memset(m["maskb"][:, :], 0.0).then_inc(consts, 1)
                pool.memset(m["ident_b"][:, :], 0.0).then_inc(consts, 1)
                pool.wait_ge(consts, 5)
                pool.affine_select(out=m["maskb"][:, :], in_=m["maskb"][:, :], compare_op=ALU.is_ge,
                                   fill=-BIG, base=0, pattern=[[-1, P]], channel_multiplier=1)\
                    .then_inc(consts, 1)
                pool.affine_select(out=m["ident_b"][:, :], in_=m["ident_b"][:, :],
                                   compare_op=ALU.not_equal, fill=1.0, base=0, pattern=[[-1, P]],
                                   channel_multiplier=1).then_inc(consts, 1)
                pool.wait_ge(consts, 7)
            pool.wait_ge(tables, 48)
            for n, (kind, t, c) in enumerate(units):
                s = n % 2
                pool.wait_ge(raw_ready, n + 1)
                if n >= 2:
                    pool.wait_ge(lo_ready, n - 1)
                pool.tensor_tensor(t_cos[:, s, :], raw[:, s, :], cos[:, 512 * c:512 * c + 512],
                                   ALU.mult).then_inc(cos_ready, 1)
                pool.wait_ge(cos_ready, n + 1)
                pool.wait_ge(sin_ready, n + 1)
                if kind == "k" and n >= 2:
                    pool.wait_ge(hi_ready, n - 1)
                pool.tensor_tensor(rotated(n), t_cos[:, s, :], t_sin[:, s, :], ALU.add)\
                    .then_inc(sum_ready, 1)
                pool.wait_ge(sum_ready, n + 1)
                pool.wait_ge(hi_ready, n + 1)
                pool.tensor_tensor(t_cos[:, s, :], rotated(n), parts[:, s, 0, :], ALU.subtract)\
                    .then_inc(res_ready, 1)


def adapter(nc, d, y_ad, arena_o, arena_w, arena_f, ident, gating, psum):
    q_rot = view(arena_o, 0, [KC, T])
    w = view(arena_w, 0, [KC, 3 * C])
    AW = HPT * ADP
    HT = NT // 2
    a_rep = view(arena_f, 8192, [KC, AW])
    ak_bd = view(arena_f, 9472, [KC, AW])
    av_bd = view(arena_f, 10752, [KC, P], parts=AW)
    hm_k = view(arena_f, 12800, [HPT])
    hm_v = view(arena_f, 12832, [HPT], parts=AW)
    mx = view(arena_f, 12864, [HT, H])
    sc = view(arena_o, 16384, [HT, H * ADP])
    prob = view(arena_o, 16384 + 5120, [HT, H * ADP])
    pT = view(arena_o, 16384 + 10240, [2, KC, P], parts=AW)

    def heads(a):
        return a.rearrange("p t (h a) -> p t h a", a=ADP)

    with Phase(nc, "adapter") as ph:
        loaded, chain_s = ph.sem("loaded"), ph.sem("chain")
        kv_ready, bd_ready = ph.sem("kv_ready"), ph.sem("bd_ready")
        scores_ready, shifted, exped, prob_ready = (ph.sem(n) for n in
                                                    ("scores_ready", "shifted", "exped", "prob_ready"))
        pT_ready, pT_copied, y_ready, y_copied = (ph.sem(n) for n in
                                                  ("pT_ready", "pT_copied", "y_ready", "y_copied"))
        block = ph.block()

        @block.sync
        def _(sp):
            sp.dma_start(a_rep, d["a_repT"].rearrange("(k p) n -> p k n", p=P)).then_inc(loaded, 16)
            sp.dma_start(hm_k, d["hm_k"]).then_inc(loaded, 16)
            sp.dma_start(hm_v, d["hm_v"]).then_inc(loaded, 16)
            sp.wait_ge(loaded, 48)

        @block.tensor
        def _(pe):
            pe.wait_ge(loaded, 48)
            for t in range(KC):
                for k in range(KC):
                    pe.matmul(psum[:, 6, ADP * t:ADP * t + ADP], w[:, k, C + P * t:C + P * t + P],
                              a_rep[:, k, 0:ADP], start=k == 0, stop=k == KC - 1)
            for k in range(KC):
                last = pe.matmul(psum[0:AW, 7, :], a_rep[:, k, :], w[:, k, 2 * C:3 * C],
                                 start=k == 0, stop=k == KC - 1)
            last.then_inc(kv_ready, 1)
            pe.wait_ge(bd_ready, 1)
            for half in range(2):
                if half:
                    pe.wait_ge(shifted, 1)
                for i in range(HT):
                    tok = P * (HT * half + i)
                    for t in range(KC):
                        last = pe.matmul(psum[:, i, AW * t:AW * t + AW], q_rot[:, t, tok:tok + P],
                                         ak_bd[:, t, :], start=True, stop=True)
                last.then_inc(scores_ready, 1)
                pe.wait_ge(prob_ready, half + 1)
                for i in range(HT):
                    n = HT * half + i
                    if n >= 2:
                        pe.wait_ge(pT_copied, n - 1)
                    for t in range(KC):
                        last = pe.transpose(psum[0:AW, 4 + n % 2, P * t:P * t + P],
                                            prob[:, i, AW * t:AW * t + AW], ident[:, :])
                    last.then_inc(pT_ready, 1)
                    pe.wait_ge(pT_copied, n + 1)
                    if n >= 2:
                        pe.wait_ge(y_copied, n - 1)
                    for t in range(KC):
                        last = pe.matmul(psum[:, 6 + n % 2, P * t:P * t + P], pT[:, n % 2, t, :],
                                         av_bd[:, t, :], start=True, stop=True)
                    last.then_inc(y_ready, 1)

        @block.scalar
        def _(act):
            for half in range(2):
                act.wait_ge(shifted, half + 1)
                if half:
                    act.wait_ge(pT_ready, HT)
                act.activation(prob, sc, ACT.Exp, scale=float(C) ** -0.5).then_inc(exped, 1)
                for i in range(HT):
                    n = HT * half + i
                    act.wait_ge(pT_ready, n + 1)
                    if n >= 2:
                        act.wait_ge(y_ready, n - 1)
                    act.copy(pT[:, n % 2, :, :], psum[0:AW, 4 + n % 2, :].rearrange(
                        "p (t q) -> p t q", q=P)).then_inc(pT_copied, 1)
                    act.wait_ge(y_ready, n + 1)
                    act.copy(y_ad[:, n, :], psum[:, 6 + n % 2, :]).then_inc(y_copied, 1)

        @block.vector
        def _(dve):
            link = Chain(dve, chain_s)
            dve.wait_ge(kv_ready, 1)
            dve.wait_ge(loaded, 48)
            link(dve.tensor_tensor(
                ak_bd.rearrange("p t (h a) -> p t h a", a=ADP),
                psum[:, 6, 0:KC * ADP].rearrange("p (t o a) -> p t o a", o=1, a=ADP)
                .broadcast_to([P, KC, HPT, ADP]),
                hm_k.rearrange("p (t h a) -> p t h a", t=1, a=1).broadcast_to([P, KC, HPT, ADP]),
                ALU.mult))
            dve.tensor_tensor(
                av_bd.rearrange("p t (h f) -> p t h f", f=D),
                psum[0:AW, 7, :].rearrange("p (t h f) -> p t h f", h=HPT, f=D),
                hm_v.rearrange("p (t h f) -> p t h f", t=1, f=1).broadcast_to([AW, KC, HPT, D]),
                ALU.mult).then_inc(bd_ready, 1)
            for half in range(2):
                dve.wait_ge(scores_ready, half + 1)
                if half:
                    dve.wait_ge(exped, 1)
                ps = heads(psum[:, 0:HT, 0:H * ADP])
                wide = [P, HT, H, ADP]
                link(dve.tensor_reduce(mx, ps, AX, ALU.max))
                dve.tensor_tensor(heads(sc), ps, mx.rearrange("p t (h o) -> p t h o", o=1)
                                  .broadcast_to(wide), ALU.subtract).then_inc(shifted, 1)
                dve.wait_ge(exped, half + 1)
                dve.wait_ge(shifted, half + 1)
                link(dve.tensor_reduce(mx, heads(prob), AX, ALU.add))
                link(dve.reciprocal(mx, mx))
                link(dve.tensor_scalar(mx, mx, gating, None, ALU.mult))
                dve.tensor_tensor(heads(prob), heads(prob), mx.rearrange("p t (h o) -> p t h o", o=1)
                                  .broadcast_to(wide), ALU.mult).then_inc(prob_ready, 1)


def attention(nc, layer, arena_o, arena_s, arena_p, v_tok, v_grp, ident_b, maskb,
              q_parts, k_parts, psum):
    kr = R if layer == 0 else 1
    scale = float(D) ** -0.5
    q_st = view(arena_s, 0, [2, CH, R * 512], BF16)
    k_max = view(arena_s, 16384, [2, R * T], BF16)
    k_exp = view(arena_s, 32768, [2, R * T], BF16)
    pr = view(arena_p, 0, [NP_RING, 2, 512])
    o_raw = view(arena_o, 0, [NG, T])

    with Phase(nc, f"att{layer}", recycle=layer == 0) as ph, ExitStack() as own:
        mx = own.enter_context(nc.sbuf_tensor(f"mx{layer}", [P, CH, R * 4], F32))
        md = own.enter_context(nc.sbuf_tensor(f"md{layer}", [P, R * 4], F32))
        mst = own.enter_context(nc.sbuf_tensor(f"mst{layer}", [P, 2, NPART, R * 4], BF16))
        mT = own.enter_context(nc.sbuf_tensor(f"mT{layer}", [NPART * R * 4, 2, P], BF16))
        q_loaded = [[ph.sem(f"q_loaded{s}{c}") for c in range(CH)] for s in range(2)]
        max_loaded = [[ph.sem(f"max_loaded{s}{c}") for c in range(CH)] for s in range(2)]
        km_loaded = [ph.sem(f"km_loaded{s}") for s in range(2)]
        ke_loaded = [ph.sem(f"ke_loaded{s}") for s in range(2)]
        qk_ready, qk_taken = ph.sem("qk_ready"), ph.sem("qk_taken")
        max_ready, maxT_ready, maxT_copied = ph.sem("max_ready"), ph.sem("maxT_ready"), ph.sem("maxT_copied")
        scores_ready, exp_ready = ph.sem("scores_ready"), ph.sem("exp_ready")
        masked, pv_done = ph.sem("masked"), ph.sem("pv_done")
        o_copied, vg_ready, rows = ph.sem("o_copied"), ph.sem("vg_ready"), ph.sem("rows")
        dve_link, passed = ph.sem("dve_link"), ph.sem("passed")
        block = ph.block()

        n_blocks = [2 * 4 * (c + 1) for c in range(CH)]
        BG = sum(n_blocks)
        first_block = [0, n_blocks[0]]
        n_pieces = [4 * R * (c + 1) for c in range(CH)]
        PG = sum(n_pieces)
        first_piece = [0, n_pieces[0]]
        DG = 2 * 4 * CH
        LINKS = 4
        assert BG % NP_RING == 0 and BG % S2_RING == 0 and PG % 2 == 0

        def piece(c, j):
            per = c + 1
            i, r, kc = j // (R * per), j // per % R, j % per
            return i, r, kc, (512 if kc < c else P * (i + 1))

        def shape(c, b):
            kt, hp = b // 2, b % 2
            return kt, hp, max(0, P * kt - 512 * c)

        def pairs(engine, body):
            body(0, False)
            with engine.Fori(1, NG // 2 - 1) as pair:
                body(pair, False)
            body(NG // 2 - 1, True)

        @block.sync
        def _(sp):
            def load_q(g, s, c):
                for j0, n in ((0, 3), (3, 2), (5, 1)):
                    sp.dma_start(
                        q_st[D * j0:D * (j0 + n), s, c, :].rearrange("p (h t) -> p h t", h=R),
                        q_parts[bass.ds(R * g, R), 0:n, :, 512 * c:512 * c + 512]
                        .rearrange("h j d t -> j d h t")).then_inc(q_loaded[s][c], 16)

            def load_k(g, s, dst, sem):
                for j, (_, kp) in enumerate(PAIRS):
                    sp.dma_start(
                        dst[D * j:D * j + D, s, 0:kr * T].rearrange("p (h t) -> p h t", h=kr),
                        k_parts[bass.ds(kr * g, kr), kp, :, :].rearrange("h d t -> d h t"))\
                        .then_inc(sem[s], 16)

            def load_max(unit, s, c):
                sp.wait_ge(maxT_copied, unit + 1)
                for j in range(NPART):
                    sp.dma_start(q_st[KS + j:KS + j + 1, s, c, :].rearrange("p (i t) -> p i t", t=P),
                                 mT[R * 4 * j:R * 4 * (j + 1), c, :])\
                        .then_inc(max_loaded[s][c], 16)

            load_q(0, 0, 0)
            load_k(0, 0, k_max, km_loaded)
            load_q(0, 0, 1)
            load_k(0, 0, k_exp, ke_loaded)
            load_q(1, 1, 0)
            load_k(1, 1, k_max, km_loaded)
            load_max(0, 0, 0)

            def body(pair, last):
                for a in range(2):
                    g = 2 * pair + a
                    load_max(2 * g + 1, a, 1)
                    if last and a == 1:
                        break
                    if not (isinstance(pair, int) and g == 0):
                        sp.wait_ge(scores_ready, BG * g)
                    load_q(g + 1, 1 - a, 1)
                    load_k(g + 1, 1 - a, k_exp, ke_loaded)
                    load_max(2 * g + 2, 1 - a, 0)
                    if last:
                        continue
                    sp.wait_ge(scores_ready, BG * g + n_blocks[0])
                    load_q(g + 2, a, 0)
                    sp.wait_ge(qk_ready, PG * g + PG)
                    load_k(g + 2, a, k_max, km_loaded)

            pairs(sp, body)

        @block.tensor
        def _(pe):
            def max_piece(pair, s, c, j):
                G = 2 * pair + s
                i, r, kc, width = piece(c, j)
                n = first_piece[c] + j
                if j == 0:
                    pe.wait_ge(q_loaded[s][c], 48 * pair + 48)
                    if c == 0:
                        pe.wait_ge(km_loaded[s], 96 * pair + 96)
                if not (isinstance(G, int) and PG * G + n < 2):
                    pe.wait_ge(qk_taken, PG * G + n - 1)
                bank = psum[:, 4 + n % 2, :]
                kh = r if layer == 0 else 0
                diagonal = kc == c
                last = pe.matmul(bank[:, 0:width], q_st[0:KS, s, c, 512 * r + P * i:512 * r + P * i + P],
                                 k_max[0:KS, s, T * kh + 512 * kc:T * kh + 512 * kc + width],
                                 start=True, stop=not diagonal)
                if diagonal:
                    last = pe.matmul(bank[:, width - P:width], ident_b[:, :], maskb[:, :],
                                     start=False, stop=True)
                last.then_inc(qk_ready, 1)

            def max_transpose(unit, c):
                pe.wait_ge(max_ready, unit + 1)
                if not (isinstance(unit, int) and unit == 0):
                    pe.wait_ge(maxT_copied, unit)
                pe.sem_inc(passed, 1)
                pe.transpose(psum[0:NPART * R * 4, 7, 0:P // 2].bitcast(BF16),
                             mst[:, c, :, :].rearrange("p j i -> p (j i)"), ident_b[:, :])\
                    .then_inc(maxT_ready, 1)

            def scores(pair, s, c, b):
                g = 2 * pair + s
                kt, hp, o = shape(c, b)
                n = first_block[c] + b
                if b == 0:
                    pe.wait_ge(max_loaded[s][c], 48 * pair + 48)
                    if c == 0:
                        pe.wait_ge(ke_loaded[s], 96 * pair + 96)
                if not (isinstance(g, int) and BG * g + n < S2_RING):
                    pe.wait_ge(exp_ready, BG * g + n - S2_RING + 1)
                for h in range(2):
                    r = 2 * hp + h
                    kh = r if layer == 0 else 0
                    last = pe.matmul(psum[:, 2 * (n % S2_RING) + h, o:512],
                                     k_exp[0:KM, s, T * kh + P * kt:T * kh + P * kt + P],
                                     q_st[0:KM, s, c, 512 * r + o:512 * r + 512],
                                     start=True, stop=True)
                last.then_inc(scores_ready, 1)

            def values(g, s, c, b):
                kt, hp, o = shape(c, b)
                n = first_block[c] + b
                if kt >= 4 * c:
                    pe.wait_ge(masked, DG * g + b + 1)
                else:
                    pe.wait_ge(exp_ready, BG * g + n + 1)
                if b == 0:
                    if c == 0:
                        pe.wait_ge(vg_ready, g + 1)
                    if not (isinstance(g, int) and 2 * g + c == 0):
                        pe.wait_ge(o_copied, 2 * g + c)
                for h in range(2):
                    r = 2 * hp + h
                    last = pe.matmul(psum[32 * r:32 * r + VW, 6, o:512],
                                     v_grp[:, s, kt, r if layer == 0 else 0, :],
                                     pr[:, n % NP_RING, h, o:512],
                                     start=kt == 0, stop=kt == 4 * c + 3, tile_position=(0, 32 * r))
                last.then_inc(pv_done, 1)

            pe.wait_ge(rows, 2)
            for j in range(n_pieces[0]):
                max_piece(0, 0, 0, j)
            max_transpose(0, 0)
            for j in range(n_pieces[1]):
                max_piece(0, 0, 1, j)
            for b in range(AHEAD):
                scores(0, 0, 0, b)

            def body(pair, last):
                for a in range(2):
                    g = 2 * pair + a
                    ahead = not (last and a == 1)
                    nxt = (pair, 1) if a == 0 else (pair + 1, 0)
                    for c in range(CH):
                        nb = n_blocks[c]
                        for b in range(nb):
                            if b + AHEAD < nb:
                                scores(pair, a, c, b + AHEAD)
                            elif c == 0:
                                scores(pair, a, 1, b + AHEAD - nb)
                            elif ahead:
                                scores(*nxt, 0, b + AHEAD - nb)
                            if ahead:
                                for j in (2 * b, 2 * b + 1):
                                    max_piece(*nxt, c, j)
                            values(g, a, c, b)
                            if b == 3:
                                if c == 0:
                                    max_transpose(2 * g + 1, 1)
                                elif ahead:
                                    max_transpose(2 * g + 2, 0)

            pairs(pe, body)

        @block.scalar
        def _(act):
            def exp(g, c, b):
                kt, hp, o = shape(c, b)
                n = first_block[c] + b
                act.wait_ge(scores_ready, BG * g + n + 1)
                if not (isinstance(g, int) and BG * g + n < NP_RING):
                    act.wait_ge(pv_done, BG * g + n - NP_RING + 1)
                act.activation(pr[:, n % NP_RING, :, o:512],
                               psum[:, 2 * (n % S2_RING):2 * (n % S2_RING) + 2, o:512],
                               ACT.Exp, scale=scale).then_inc(exp_ready, 1)

            def copy_o(g, c):
                act.wait_ge(pv_done, BG * g + first_block[c] + n_blocks[c])
                act.copy(o_raw[:, bass.ds(g, 1), 512 * c:512 * c + 512] if not isinstance(g, int)
                         else o_raw[:, g, 512 * c:512 * c + 512], psum[:, 6, :]).then_inc(o_copied, 1)

            def copy_max(unit, c):
                act.wait_ge(maxT_ready, unit + 1)
                act.copy(mT[:, c, :], psum[0:NPART * R * 4, 7, 0:P // 2].bitcast(BF16))\
                    .then_inc(maxT_copied, 1)

            copy_max(0, 0)

            def body(pair, last):
                for a in range(2):
                    g = 2 * pair + a
                    for c in range(CH):
                        for b in range(n_blocks[c]):
                            exp(g, c, b)
                            if b == 0:
                                if c == 1:
                                    copy_o(g, 0)
                                elif not (isinstance(g, int) and g == 0):
                                    copy_o(g - 1, 1)
                            if b == 5:
                                if c == 0:
                                    copy_max(2 * g + 1, 1)
                                elif not (last and a == 1):
                                    copy_max(2 * g + 2, 0)
                if last:
                    copy_o(NG - 1, 1)

            pairs(act, body)

        @block.vector
        def _(dve):
            def maxima(G, c):
                for j in range(n_pieces[c]):
                    i, r, kc, width = piece(c, j)
                    n = first_piece[c] + j
                    dve.wait_ge(qk_ready, PG * G + n + 1)
                    if j == 0 and not (isinstance(G, int) and G == 0 and c == 0):
                        dve.wait_ge(max_ready, 2 * G + c)
                    dve.tensor_reduce(mx[:, kc, 4 * r + i:4 * r + i + 1], psum[:, 4 + n % 2, 0:width],
                                      AX, ALU.max).then_inc(qk_taken, 1)
                at = LINKS * (2 * G + c)
                dve.wait_ge(qk_taken, PG * G + first_piece[c] + n_pieces[c])
                if c == 1:
                    dve.tensor_tensor(mx[:, 0, :], mx[:, 0, :], mx[:, 1, :], ALU.max)\
                        .then_inc(dve_link, 1)
                else:
                    dve.sem_inc(dve_link, 1)
                dve.wait_ge(dve_link, at + 1)
                if not (isinstance(G, int) and G == 0):
                    dve.wait_ge(maxT_ready, 2 * G + c - 1)
                dve.tensor_copy(mst[:, c, 0, :], mx[:, 0, :]).then_inc(dve_link, 1)
                dve.wait_ge(dve_link, at + 2)
                dve.tensor_tensor(md[:, :], mx[:, 0, :], mst[:, c, 0, :], ALU.subtract)\
                    .then_inc(dve_link, 1)
                dve.wait_ge(dve_link, at + 3)
                dve.tensor_copy(mst[:, c, 1, :], md[:, :]).then_inc(dve_link, 1)
                dve.wait_ge(dve_link, at + 4)
                dve.tensor_tensor(mst[:, c, 2, :], md[:, :], mst[:, c, 1, :], ALU.subtract)\
                    .then_inc(max_ready, 1)

            maxima(0, 0)
            maxima(0, 1)

            def body(pair, last):
                for a in range(2):
                    if not (last and a == 1):
                        for c in range(CH):
                            maxima(2 * pair + a + 1, c)

            pairs(dve, body)

        @block.gpsimd
        def _(pool):
            pool.memset(k_exp[KS:KM, 0, :], -1.0).then_inc(rows, 1)
            pool.memset(k_exp[KS:KM, 1, :], -1.0).then_inc(rows, 1)
            vgw = kr * D

            def load_v(g, s):
                if not (isinstance(g, int) and g < 2):
                    pool.wait_ge(pv_done, BG * g - BG)
                src = v_tok[:, :, bass.ds(vgw * g, vgw)] if not isinstance(g, int) \
                    else v_tok[:, :, vgw * g:vgw * g + vgw]
                pool.tensor_copy(v_grp[:, s, :, 0:kr, 0:D],
                                 src.rearrange("p t (r f) -> p t r f", f=D)).then_inc(vg_ready, 1)

            pool.wait_ge(rows, 2)
            load_v(0, 0)

            def body(pair, last):
                for a in range(2):
                    g = 2 * pair + a
                    for c in range(CH):
                        for b in range(n_blocks[c]):
                            kt, hp, o = shape(c, b)
                            n = first_block[c] + b
                            if kt < 4 * c:
                                continue
                            pool.wait_ge(exp_ready, BG * g + n + 1)
                            pool.sem_inc(passed, 1)
                            tri = pr[:, n % NP_RING, :, o:o + P]
                            pool.affine_select(out=tri, in_=tri, compare_op=ALU.is_ge, fill=0.0,
                                               base=0, pattern=[[0, 2], [1, P]],
                                               channel_multiplier=-1).then_inc(masked, 1)
                        if c == 0 and not (last and a == 1):
                            load_v(g + 1, 1 - a)

            pairs(pool, body)


def norm_stats(dve, link, src, stats):
    link(dve.bn_stats(stats[:, 0:6], src))
    return dve.bn_aggr(stats[:, 6:8], stats[:, 0:6])


def norm_root(act, stats, eps):
    return act.activation(stats[:, 8:9], stats[:, 7:8], ACT.Sqrt, bias=eps)


def norm_apply(dve, link, dst, src, stats):
    link(dve.reciprocal(stats[:, 8:9], stats[:, 8:9]))
    return dve.tensor_scalar(dst, src, stats[:, 6:7], stats[:, 8:9], ALU.subtract, ALU.mult)


def finish_attention(nc, layer, d, x_tok, xT, v_tok, arena_o, arena_s, arena_w, w_out, ident, eps, psum):
    o_raw = view(arena_o, 0, [NG, T])
    y = view(arena_s, 0, [2, C])
    yT = view(arena_s, 4096, [2, KC, P])
    h = view(arena_s, 8192, [2, C])
    rec = view(arena_s, 12288, [H])
    stats = view(arena_s, 12416, [2, 9])
    with Phase(nc, f"fin{layer}") as ph:
        x_loaded, chain_s = ph.sem("x_loaded"), ph.sem("chain")
        oT_ready, y_ready, yT_ready, yT_copied = (ph.sem(n) for n in
                                                  ("oT_ready", "y_ready", "yT_ready", "yT_copied"))
        z_ready, x_ready, xT_ready, xT_copied = (ph.sem(n) for n in
                                                 ("z_ready", "x_ready", "xT_ready", "xT_copied"))
        z_added, var_ready, dev_ready = ph.sem("z_added"), ph.sem("var_ready"), ph.sem("dev_ready")
        block = ph.block()

        @block.sync
        def _(sp):
            if layer == 0:
                sp.dma_start(v_tok[:, :, :], d["x"].rearrange("(t p) c -> p t c", p=P))\
                    .then_inc(x_loaded, 16)
                w_next = view(arena_w, 0, [KC, C + 2 * P])
                sp.dma_start(w_next, d["w1"].rearrange("(k p) n -> p k n", p=P)).then_inc(x_loaded, 16)
                sp.dma_start(view(arena_w, 12288, [KC, C]), d["wo1"].rearrange("(k p) n -> p k n", p=P))\
                    .then_inc(x_loaded, 16)
                sp.wait_ge(x_loaded, 48)

        @block.tensor
        def _(pe):
            for s in range(NT + 4):
                if s < NT:
                    t = s
                    if t >= 2:
                        pe.wait_ge(y_ready, t - 1)
                    for g in range(NG):
                        last = pe.transpose(psum[:, 2 * (t % 2) + g // 4, P * (g % 4):P * (g % 4) + P],
                                            o_raw[:, g, P * t:P * t + P], ident[:, :])
                    last.then_inc(oT_ready, 1)
                if 0 <= s - 1 < NT:
                    t = s - 1
                    pe.wait_ge(y_ready, t + 1)
                    if t >= 1:
                        pe.wait_ge(yT_copied, t)
                    for k in range(KC):
                        last = pe.transpose(psum[:, 4, P * k:P * k + P],
                                            y[:, t % 2, P * k:P * k + P], ident[:, :])
                    last.then_inc(yT_ready, 1)
                if 0 <= s - 2 < NT:
                    t = s - 2
                    pe.wait_ge(yT_copied, t + 1)
                    if t >= 1:
                        pe.wait_ge(z_added, t)
                    for k in range(KC):
                        last = pe.matmul(psum[:, 5, :], yT[:, t % 2, k, :], w_out[:, k, :],
                                         start=k == 0, stop=k == KC - 1)
                    last.then_inc(z_ready, 1)
                if 0 <= s - 4 < NT:
                    t = s - 4
                    pe.wait_ge(x_ready, t + 1)
                    if t >= 1:
                        pe.wait_ge(xT_copied, t)
                    for k in range(KC):
                        last = pe.transpose(psum[:, 6, P * k:P * k + P],
                                            x_tok[:, t, P * k:P * k + P], ident[:, :])
                    last.then_inc(xT_ready, 1)

        @block.scalar
        def _(act):
            for s in range(NT + 4):
                if 0 <= s - 1 < NT:
                    t = s - 1
                    act.wait_ge(yT_ready, t + 1)
                    if t >= 2:
                        act.wait_ge(z_ready, t - 1)
                    act.copy(yT[:, t % 2, :, :], psum[:, 4, :].rearrange("p (k q) -> p k q", q=P))\
                        .then_inc(yT_copied, 1)
                if 0 <= s - 2 < NT:
                    t = s - 2
                    act.wait_ge(var_ready, t + 1)
                    norm_root(act, stats[:, t % 2, :], eps).then_inc(dev_ready, 1)
                if 0 <= s - 4 < NT:
                    t = s - 4
                    act.wait_ge(xT_ready, t + 1)
                    act.copy(xT[:, :, P * t:P * t + P], psum[:, 6, :].rearrange("p (k q) -> p k q", q=P))\
                        .then_inc(xT_copied, 1)

        @block.vector
        def _(dve):
            link = Chain(dve, chain_s)
            if layer == 0:
                dve.wait_ge(x_loaded, 48)
            for s in range(NT + 3):
                if s < NT:
                    t = s
                    dve.wait_ge(oT_ready, t + 1)
                    if t >= 2:
                        dve.wait_ge(yT_ready, t - 1)
                    o = psum[:, 2 * (t % 2):2 * (t % 2) + 2, :].rearrange("p b (h f) -> p (b h) f", f=VW)
                    if t >= 1:
                        dve.wait_ge(y_ready, t)
                    link(dve.reciprocal(rec, o[:, :, D]))
                    out_y = y[:, t % 2, :].rearrange("p (h f) -> p h f", f=D)
                    mul = dve.tensor_tensor(out_y, o[:, :, 0:D], rec.rearrange("p (h o) -> p h o", o=1)
                                            .broadcast_to([P, H, D]), ALU.mult)
                    if layer == 0:
                        link(mul)
                        mul = dve.tensor_tensor(y[:, t % 2, :], y[:, t % 2, :], x_tok[:, t, :], ALU.add)
                    mul.then_inc(y_ready, 1)
                if 0 <= s - 2 < NT:
                    t = s - 2
                    dve.wait_ge(z_ready, t + 1)
                    dve.wait_ge(y_ready, t + 1)
                    if t >= 2:
                        dve.wait_ge(x_ready, t - 1)
                    res = v_tok[:, t, :] if layer == 0 else x_tok[:, t, :]
                    dve.tensor_tensor(h[:, t % 2, :], psum[:, 5, :], res, ALU.add).then_inc(z_added, 1)
                    dve.wait_ge(z_added, t + 1)
                    norm_stats(dve, link, h[:, t % 2, :], stats[:, t % 2, :]).then_inc(var_ready, 1)
                if 0 <= s - 3 < NT:
                    t = s - 3
                    dve.wait_ge(dev_ready, t + 1)
                    norm_apply(dve, link, x_tok[:, t, :], h[:, t % 2, :], stats[:, t % 2, :])\
                        .then_inc(x_ready, 1)


def lookup(nc, d, x_tok, xT, arena_o, arena_s, ident, ones, eps, psum, wq, wr, akey, av, wvd, wvu,
           wu1, wu2, bu1, logrel, bu2, gate_w1, gate_bias):
    hid = view(arena_o, 0, [T])
    query = view(arena_o, 4096, [T], parts=BOT)
    rq = view(arena_o, 8192, [T], parts=RDIM)
    rs = view(arena_o, 12288, [NT, NSLOT])
    at = view(arena_o, 16384, [NT, NSLOT])
    rest = view(arena_o, 20480, [NT, NSLOT])
    wT = view(arena_o, 24576, [T])
    aux = view(arena_o, 28672, [2, C])
    rk = view(arena_s, 0, [NSLOT], parts=RDIM)
    dn = view(arena_s, 512, [NSLOT], parts=VB)
    vals = view(arena_s, 1024, [C])
    top = view(arena_s, 3072, [NT, 8])
    n8 = [view(arena_s, 3328 + 32 * n, [NT]) for n in range(8)]
    mxs, sums, var, lv, learned, gate, tmp, tmp2 = n8
    lvs = view(arena_s, 3584, [1])
    stats2 = view(arena_s, 3712, [2, 9])
    stats = stats2[:, 0, :]
    var2 = view(arena_s, 3648, [NT, 2])
    h = view(arena_s, 4096, [2, C])
    last_exp = float(BOT) ** -0.5
    with Phase(nc, "lookup") as ph:
        pre, pre_copied = ph.sem("pre"), ph.sem("pre_copied")
        qh_ready, qh_copied, s_ready, s_read = (ph.sem(n) for n in
                                                ("qh_ready", "qh_copied", "s_ready", "s_read"))
        shifted, exped, wT_ready, wT_copied = (ph.sem(n) for n in
                                               ("shifted", "exped", "wT_ready", "wT_copied"))
        lv_done, lvs_ready, mean_ready, lin_ready = (ph.sem(n) for n in
                                                     ("lv_done", "lvs_ready", "mean_ready", "lin_ready"))
        var_ready, sig_in, sig_out, gate_ready = (ph.sem(n) for n in
                                                  ("var_ready", "sig_in", "sig_out", "gate_ready"))
        z_ready, aux_ready, x_ready, xT_ready, xT_copied = (ph.sem(n) for n in
                                                            ("z_ready", "aux_ready", "x_ready", "xT_ready", "xT_copied"))
        chain_s, g_in, g_out = ph.sem("chain"), ph.sem("g_in"), ph.sem("g_out")
        row_var, dev_ready = ph.sem("row_var"), ph.sem("dev_ready")
        block = ph.block()

        @block.tensor
        def _(pe):
            for c in range(CH):
                for k in range(KC):
                    last = pe.matmul(psum[:, c, :], wu1[:, k, :], xT[:, k, 512 * c:512 * c + 512],
                                     start=k == 0, stop=k == KC - 1)
                last.then_inc(qh_ready, 1)
            for c in range(CH):
                for k in range(KC):
                    last = pe.matmul(psum[0:BOT, 2 + c, :], wq[:, k, :], xT[:, k, 512 * c:512 * c + 512],
                                     start=k == 0, stop=k == KC - 1)
                last.then_inc(qh_ready, 1)
            pe.matmul(psum[0:RDIM, 4, 0:NSLOT], wr, akey, start=True, stop=True)
            for k in range(KC):
                last = pe.matmul(psum[0:VB, 5, 0:NSLOT], wvd[:, k, :], av[:, k, :],
                                 start=k == 0, stop=k == KC - 1)
            last.then_inc(pre, 1)
            pe.wait_ge(pre_copied, 2)
            pe.matmul(psum[:, 6, :], dn, wvu, start=True, stop=True).then_inc(pre, 1)
            pe.wait_ge(qh_copied, 4)
            for c in range(CH):
                last = pe.matmul(psum[0:RDIM, 4 + c, :], wr, query[:, 512 * c:512 * c + 512],
                                 start=True, stop=True)
            last.then_inc(qh_ready, 1)
            pe.wait_ge(qh_copied, 5)
            for t in range(NT):
                pe.matmul(psum[:, t // 4, P * (t % 4):P * (t % 4) + NSLOT], rq[:, P * t:P * t + P], rk,
                          start=True, stop=True)
                last = pe.matmul(psum[:, 2 + t // 4, P * (t % 4):P * (t % 4) + NSLOT],
                                 query[:, P * t:P * t + P], akey, start=True, stop=True)
            last.then_inc(s_ready, 1)
            pe.wait_ge(pre_copied, 3)
            for t in range(NT):
                last = pe.matmul(psum[:, 4, t:t + 1], hid[:, P * t:P * t + P], wu2, start=True, stop=True)
            last.then_inc(lin_ready, 1)
            pe.wait_ge(lvs_ready, 1)
            pe.matmul(psum[:, 5, 0:1], ones, lvs, start=True, stop=True).then_inc(mean_ready, 1)
            pe.wait_ge(exped, 1)
            pe.wait_ge(s_read, 1)
            for t in range(NT):
                last = pe.transpose(psum[:, t // 4, P * (t % 4):P * (t % 4) + P], at[:, t, :], ident[:, :])
            last.then_inc(wT_ready, 1)
            pe.wait_ge(wT_copied, 1)
            for s in range(NT + 3):
                if s < NT:
                    t = s
                    if t >= 2:
                        pe.wait_ge(aux_ready, t - 1)
                    pe.matmul(psum[:, 2 + t % 2, :], wT[:, P * t:P * t + P], vals, start=True, stop=True)\
                        .then_inc(z_ready, 1)
                if s >= 3:
                    t = s - 3
                    pe.wait_ge(x_ready, t + 1)
                    if t >= 2:
                        pe.wait_ge(xT_copied, t - 1)
                    for k in range(KC):
                        last = pe.transpose(psum[:, 6 + t % 2, P * k:P * k + P],
                                            x_tok[:, t, P * k:P * k + P], ident[:, :])
                    last.then_inc(xT_ready, 1)

        @block.scalar
        def _(act):
            for c in range(CH):
                act.wait_ge(qh_ready, c + 1)
                act.activation(hid[:, 512 * c:512 * c + 512], psum[:, c, :], ACT.Gelu_apprx_tanh,
                               bias=bu1[:, :]).then_inc(qh_copied, 1)
            for c in range(CH):
                act.wait_ge(qh_ready, 3 + c)
                act.copy(query[:, 512 * c:512 * c + 512], psum[0:BOT, 2 + c, :]).then_inc(qh_copied, 1)
            act.wait_ge(pre, 1)
            act.copy(rk, psum[0:RDIM, 4, 0:NSLOT]).then_inc(pre_copied, 1)
            act.copy(dn, psum[0:VB, 5, 0:NSLOT]).then_inc(pre_copied, 1)
            act.wait_ge(pre, 2)
            act.copy(vals, psum[:, 6, :]).then_inc(pre_copied, 1)
            act.wait_ge(qh_ready, 5)
            act.copy(rq.rearrange("p (c t) -> p c t", c=CH), psum[0:RDIM, 4:6, :]).then_inc(qh_copied, 1)
            act.wait_ge(var_ready, 1)
            act.activation(lv, var, ACT.Ln, bias=1.0).then_inc(lv_done, 1)
            act.wait_ge(sig_in, 1)
            act.activation(learned, tmp, ACT.Sigmoid).then_inc(sig_out, 1)
            act.wait_ge(g_in, 1)
            act.activation(tmp, gate, ACT.Sigmoid).then_inc(g_out, 1)
            act.wait_ge(shifted, 1)
            act.activation(at, rest, ACT.Exp).then_inc(exped, 1)
            act.wait_ge(wT_ready, 1)
            act.copy(wT.rearrange("p (c t) -> p c t", c=CH), psum[:, 0:2, :]).then_inc(wT_copied, 1)
            act.wait_ge(gate_ready, 1)
            for s in range(NT + 3):
                if s < NT:
                    t = s
                    act.wait_ge(z_ready, t + 1)
                    if t >= 2:
                        act.wait_ge(row_var, t - 1)
                    act.activation(aux[:, t % 2, :], psum[:, 2 + t % 2, :], ACT.Copy,
                                   scale=gate[:, t:t + 1]).then_inc(aux_ready, 1)
                if 1 <= s <= NT:
                    t = s - 1
                    act.wait_ge(row_var, t + 1)
                    norm_root(act, stats2[:, t % 2, :], eps).then_inc(dev_ready, 1)
                if s >= 3:
                    t = s - 3
                    act.wait_ge(xT_ready, t + 1)
                    act.copy(xT[:, :, P * t:P * t + P], psum[:, 6 + t % 2, :]
                             .rearrange("p (k q) -> p k q", q=P)).then_inc(xT_copied, 1)

        @block.vector
        def _(dve):
            link = Chain(dve, chain_s)
            for t in range(NT):
                link(dve.bn_stats(stats[:, 0:6], x_tok[:, t, :]))
                link(dve.bn_aggr(var2[:, t, :], stats[:, 0:6]))
            dve.tensor_copy(var, var2[:, :, 1]).then_inc(var_ready, 1)
            dve.wait_ge(lv_done, 1)
            dve.tensor_reduce(lvs, lv, AX, ALU.add).then_inc(lvs_ready, 1)
            dve.wait_ge(mean_ready, 1)
            link(dve.tensor_scalar(lvs, psum[:, 5, 0:1], 1.0 / T, 1e-6, ALU.mult, ALU.add))
            link(dve.reciprocal(lvs, lvs))
            link(dve.tensor_scalar(tmp2, lv, lvs, 0.5, ALU.mult, ALU.mult))
            dve.wait_ge(lin_ready, 1)
            dve.tensor_scalar(tmp, psum[:, 4, 0:NT], bu2, None, ALU.add).then_inc(sig_in, 1)
            dve.wait_ge(sig_out, 1)
            link(dve.scalar_tensor_tensor(out=gate, in0=learned, scalar=2.5, in1=tmp2,
                                          op0=ALU.mult, op1=ALU.add))
            link(dve.tensor_scalar(gate, gate, 0.0, 5.0, ALU.max, ALU.min))
            link(dve.tensor_scalar(gate, gate, 0.5, 1.0 / 1.5, ALU.subtract, ALU.mult))
            link(dve.tensor_scalar(gate, gate, 0.0, 1.0, ALU.max, ALU.min))
            dve.tensor_scalar(gate, gate, gate_w1, gate_bias, ALU.mult, ALU.add).then_inc(g_in, 1)
            dve.wait_ge(g_out, 1)
            link(dve.tensor_scalar(learned, tmp, 0.05, None, ALU.is_ge))
            link(dve.tensor_tensor(gate, tmp, learned, ALU.mult))
            dve.wait_ge(s_ready, 1)
            lr = logrel.rearrange("p (o n) -> p o n", o=1).broadcast_to([P, NT, NSLOT])
            ps = [psum[:, 2 * n:2 * n + 2, :].rearrange("p b (t n) -> p (b t) n", n=NSLOT) for n in range(2)]
            link(dve.scalar_tensor_tensor(out=rs, in0=ps[0], scalar=float(1 / np.sqrt(RDIM)), in1=lr,
                                          op0=ALU.mult, op1=ALU.add))
            dve.scalar_tensor_tensor(out=at, in0=ps[1], scalar=last_exp, in1=lr,
                                     op0=ALU.mult, op1=ALU.add).then_inc(s_read, 1)
            dve.wait_ge(s_read, 1)
            for t in range(NT):
                link(dve.max(top[:, t, :], rs[:, t, :]))
            for t in range(NT):
                link(dve.match_replace(out=rest[:, t, :], in_to_replace=top[:, t, :],
                                       in_values=rs[:, t, :], imm_value=-3e38))
            link(dve.tensor_tensor(rs, rs, rest, ALU.is_equal))
            link(dve.scalar_tensor_tensor(out=at, in0=rs, scalar=-BIG, in1=at,
                                          op0=ALU.mult, op1=ALU.add))
            link(dve.tensor_reduce(mxs, at, AX, ALU.max))
            dve.tensor_tensor(rest, at, mxs.rearrange("p (t o) -> p t o", o=1)
                              .broadcast_to([P, NT, NSLOT]), ALU.subtract).then_inc(shifted, 1)
            dve.wait_ge(exped, 1)
            link(dve.tensor_reduce(sums, at, AX, ALU.add))
            link(dve.reciprocal(sums, sums))
            dve.tensor_tensor(gate, gate, sums, ALU.mult).then_inc(gate_ready, 1)
            for s in range(NT + 1):
                if s < NT:
                    t = s
                    dve.wait_ge(aux_ready, t + 1)
                    if t >= 2:
                        dve.wait_ge(x_ready, t - 1)
                    link(dve.scalar_tensor_tensor(out=h[:, t % 2, :], in0=x_tok[:, t, :], scalar=2.0,
                                                  in1=aux[:, t % 2, :], op0=ALU.mult, op1=ALU.add))
                    norm_stats(dve, link, h[:, t % 2, :], stats2[:, t % 2, :]).then_inc(row_var, 1)
                if s >= 1:
                    t = s - 1
                    dve.wait_ge(dev_ready, t + 1)
                    norm_apply(dve, link, x_tok[:, t, :], h[:, t % 2, :], stats2[:, t % 2, :])\
                        .then_inc(x_ready, 1)


def swiglu(nc, d, x_tok, xT, arena_o, arena_s, arena_f, s_gate, s_up, s_down, eps, psum, out):
    w_in = view(arena_f, 0, [4, 2, KC, P])
    w_down = view(arena_o, 0, [NI, C])
    act_g = view(arena_o, NI * C * 4, [2, 512])
    h = view(arena_o, NI * C * 4 + 4096, [2, C])
    inter = view(arena_s, 0, [NI, T])
    stats = view(arena_s, NI * T * 4, [2, 9])
    with Phase(nc, "swiglu") as ph:
        w_loaded = [ph.sem(f"w_loaded{n}") for n in range(4)]
        wd_loaded, chain_s, stored = ph.sem("wd_loaded"), ph.sem("chain"), ph.sem("stored")
        gu_ready, silu_ready, inter_ready = ph.sem("gu_ready"), ph.sem("silu_ready"), ph.sem("inter_ready")
        z_ready, z_scaled, x_ready = ph.sem("z_ready"), ph.sem("z_scaled"), ph.sem("x_ready")
        var_ready, dev_ready = ph.sem("var_ready"), ph.sem("dev_ready")
        block = ph.block()
        rows = [min(P, INTER - P * i) for i in range(NI)]

        @block.sync
        def _(sp):
            for i in range(NI):
                if i >= 4:
                    sp.wait_ge(gu_ready, 2 * (i - 4) + 2)
                sp.dma_start(w_in[:, i % 4, :, :, :], d["w_in"][i]
                             .rearrange("p (u k n) -> p u k n", u=2, k=KC)).then_inc(w_loaded[i % 4], 16)
                if i == 3:
                    sp.dma_start(w_down[:, 0:NI - 1, :], d["w_down"][0:P * (NI - 1), :]
                                 .rearrange("(i p) n -> p i n", p=P)).then_inc(wd_loaded, 16)
                    sp.dma_start(w_down[0:rows[-1], NI - 1, :], d["w_down"][P * (NI - 1):, :])\
                        .then_inc(wd_loaded, 16)
            for t in range(NT):
                sp.wait_ge(x_ready, t + 1)
                sp.dma_start(out[P * t:P * t + P, :], x_tok[:, t, :]).then_inc(stored, 16)
            sp.wait_ge(stored, 16 * NT)

        @block.tensor
        def _(pe):
            for i in range(NI):
                pe.wait_ge(w_loaded[i % 4], 16 * (i // 4 + 1))
                for c in range(CH):
                    n = CH * i + c
                    if n >= 2:
                        pe.wait_ge(inter_ready, n - 1)
                    for u in range(2):
                        for k in range(KC):
                            last = pe.matmul(psum[0:rows[i], 2 * (n % 2) + u, :],
                                             w_in[:, i % 4, u, k, 0:rows[i]],
                                             xT[:, k, 512 * c:512 * c + 512],
                                             start=k == 0, stop=k == KC - 1)
                    last.then_inc(gu_ready, 1)
            pe.wait_ge(wd_loaded, 32)
            pe.wait_ge(inter_ready, CH * NI)
            for t in range(NT):
                if t >= 2:
                    pe.wait_ge(z_scaled, t - 1)
                for i in range(NI):
                    last = pe.matmul(psum[:, 4 + t % 2, :], inter[0:rows[i], i, P * t:P * t + P],
                                     w_down[0:rows[i], i, :], start=i == 0, stop=i == NI - 1)
                last.then_inc(z_ready, 1)

        @block.scalar
        def _(act):
            for i in range(NI):
                for c in range(CH):
                    n = CH * i + c
                    act.wait_ge(gu_ready, n + 1)
                    if n >= 2:
                        act.wait_ge(inter_ready, n - 1)
                    act.activation(act_g[0:rows[i], n % 2, :], psum[0:rows[i], 2 * (n % 2), :], ACT.Silu,
                                   scale=s_gate[0:rows[i], :]).then_inc(silu_ready, 1)
            for t in range(NT):
                act.wait_ge(var_ready, t + 1)
                norm_root(act, stats[:, t % 2, :], eps).then_inc(dev_ready, 1)

        @block.vector
        def _(dve):
            link = Chain(dve, chain_s)
            for i in range(NI):
                for c in range(CH):
                    n = CH * i + c
                    dve.wait_ge(silu_ready, n + 1)
                    dve.scalar_tensor_tensor(out=inter[0:rows[i], i, 512 * c:512 * c + 512],
                                             in0=psum[0:rows[i], 2 * (n % 2) + 1, :],
                                             scalar=s_up[0:rows[i], :], in1=act_g[0:rows[i], n % 2, :],
                                             op0=ALU.mult, op1=ALU.mult).then_inc(inter_ready, 1)
            for t in range(NT):
                dve.wait_ge(z_ready, t + 1)
                if t >= 2:
                    dve.wait_ge(x_ready, t - 1)
                dve.scalar_tensor_tensor(out=h[:, t % 2, :], in0=psum[:, 4 + t % 2, :], scalar=s_down,
                                         in1=x_tok[:, t, :], op0=ALU.mult, op1=ALU.add)\
                    .then_inc(z_scaled, 1)
                dve.wait_ge(z_scaled, t + 1)
                norm_stats(dve, link, h[:, t % 2, :], stats[:, t % 2, :]).then_inc(var_ready, 1)
                dve.wait_ge(dev_ready, t + 1)
                norm_apply(dve, link, x_tok[:, t, :], h[:, t % 2, :], stats[:, t % 2, :])\
                    .then_inc(x_ready, 1)


def _rope(base):
    theta = (1.0 / np.float32(base) ** (np.arange(0, D, 2, dtype=np.float32) / np.float32(D))).astype(np.float32)
    angle = np.outer(np.arange(T, dtype=np.float32), theta).astype(np.float32)
    angle = np.concatenate([angle, angle], axis=1).T
    return (np.tile(np.cos(angle), (HPT, 1)).astype(np.float32),
            np.tile(np.sin(angle), (HPT, 1)).astype(np.float32))


def _constants():
    cos0, sin0 = _rope(10000.0)
    cos1, sin1 = _rope(500000.0)
    rot = np.zeros((P, P), np.float32)
    for h in range(HPT):
        for i in range(D // 2):
            rot[D * h + D // 2 + i, D * h + i] = -1.0
            rot[D * h + i, D * h + D // 2 + i] = 1.0
    eye = np.eye(P, dtype=np.float32)
    hm_k = (np.arange(P)[:, None] // D == np.arange(HPT)[None]).astype(np.float32)
    hm_v = (np.arange(HPT * ADP)[:, None] // ADP == np.arange(HPT)[None]).astype(np.float32)
    return dict(cos0=cos0, sin0=sin0, cos1=cos1, sin1=sin1, rot=rot, ident=eye, hm_k=hm_k, hm_v=hm_v)


def kernel(**inputs):
    import concourse.bacc as bacc
    from concourse.bass_utils import run_bass_kernel_spmd as run

    a = {k: np.asarray(v) for k, v in inputs.items()}
    tiles = lambda w: np.ascontiguousarray(w.reshape(KC, P, -1).transpose(1, 0, 2).reshape(P, -1))
    col = lambda v: np.broadcast_to(np.asarray(v).reshape(1, -1), (P, np.asarray(v).size)).copy()
    w_in = np.zeros((NI, P, 2, KC, P), np.float32)
    for u, name in enumerate(["L1_ffn_gate_w", "L1_ffn_up_w"]):
        wT = a[name].T.reshape(KC, P, INTER)
        for i in range(NI):
            n = min(P, INTER - P * i)
            w_in[i, :, u, :, 0:n] = wT[:, :, P * i:P * i + n].transpose(1, 0, 2)
    x0 = a["L0_attn_x"][0]
    d = dict(
        x=x0, xT=x0.T, w0=a["L0_attn_w_attn"].T, wo0=a["L0_attn_w_proj"].T,
        a_repT=np.tile(a["L0_attn_adapter_wte"].T, (1, HPT)), gating=col(a["L0_attn_gating"]),
        f_wqT=tiles(a["L0_ffn_Wq"].T), f_wrT=a["L0_ffn_Wr"].T, f_akeyT=a["L0_ffn_aux_keys"].T,
        f_avT=tiles(a["L0_ffn_aux_values"].T), f_wvdT=tiles(a["L0_ffn_Wvd"].T),
        f_wvuT=a["L0_ffn_Wvu"].T, f_wu1T=tiles(a["L0_ffn_Wu1"].T), f_wu2T=a["L0_ffn_Wu2"].T,
        f_bu1=a["L0_ffn_bu1"].reshape(HU, 1), f_logrel=col(a["L0_ffn_log_rel"]),
        f_bu2=col(a["L0_ffn_bu2"]), f_gate_w1=col(a["L0_ffn_gate_w1"]),
        f_gate_bias=col(a["L0_ffn_gate_bias"]),
        w1=np.concatenate([a["L1_attn_Wq"], a["L1_attn_Wk"], a["L1_attn_Wv"]], axis=1),
        wo1=a["L1_attn_Wo"], w_in=w_in.reshape(NI, P, -1), w_down=a["L1_ffn_down_w"].T,
        s_gate=col(a["L1_ffn_gate_scale"]), s_up=col(a["L1_ffn_up_scale"]),
        s_down=col(a["L1_ffn_down_scale"]), **_constants())
    nc = bacc.Bacc("TRN2", target_bir_lowering=False, num_devices=1)
    arrays, aps = {}, {}
    for name, v in d.items():
        v = np.ascontiguousarray(v)
        arrays[f"in_{name}"] = v
        aps[name] = nc.dram_tensor(f"in_{name}", v.shape, mybir.dt.from_np(v.dtype),
                                   kind="ExternalInput").ap()
    out = nc.dram_tensor("out", [T, C], F32, kind="ExternalOutput").ap()
    build(nc, aps, out)
    r = run(nc, [arrays], core_ids=[0])
    return np.asarray(r.results[0]["out"]).reshape(1, T, C)
```

```python
from contextlib import ExitStack

import numpy as np

import concourse.bass as bass
from concourse import mybir

F32 = mybir.dt.float32
BF16 = mybir.dt.bfloat16
F32R = mybir.dt.float32r
ALU = mybir.AluOpType
ACT = mybir.ActivationFunctionType
AX = mybir.AxisListType.X

P = 128
T, C = 1024, 512
H, D = 32, 16
NT = T // P
KC = C // P
CH = T // 512
R = 4
NG = H // R
KV1 = 8
NPART = 3
PAIRS = [(0, 0), (1, 0), (2, 0), (0, 1), (1, 1), (0, 2)]
KS = len(PAIRS) * D
KM = KS + NPART
VW = 32
ADP = 10
HPT = P // D
BOT, RDIM, NSLOT, VB, HU = 64, 48, 128, 32, 128
INTER = 1376
NI = -(-INTER // P)
EPS = 1e-5
BIG = 1e30
NP_RING = 4


M_X, M_XT, M_V, M_O, M_S = 0, 16384, 32768, 49152, 81920
M_P, M_VG, M_W, M_F, M_SMALL, M_ID = 131072, 147456, 155648, 180224, 196608, 207040
MAP_END = 208064
M_WIN, M_GH, M_WD, M_RAW, M_GL, M_TMP = 49152, 65536, 110592, 133120, 141312, 186368


def view(arena, offset, dims, dtype=F32, parts=P):
    n = int(np.prod(dims))
    size = 4 if dtype == F32 else 2
    assert offset % 4 == 0 and (n * size) % 4 == 0
    ap = arena[0:parts, offset // 4:offset // 4 + n * size // 4]
    if dtype != F32:
        ap = ap.bitcast(dtype)
    if len(dims) > 1:
        names = "abcd"[:len(dims)]
        ap = ap.rearrange(f"p ({' '.join(names)}) -> p {' '.join(names)}",
                          **{k: int(v) for k, v in zip(names, dims)})
    return ap


class Chain:

    def __init__(self, engine, semaphore):
        self.engine, self.semaphore, self.count = engine, semaphore, 0

    def __call__(self, instruction):
        self.count += 1
        instruction.then_inc(self.semaphore, 1)
        self.engine.wait_ge(self.semaphore, self.count)


def build(nc, d, out):
    with ExitStack() as stack:
        base = -(-nc.sbuf_base // 32) * 32
        stack.enter_context(nc.sbuf_tensor("fence", [P, MAP_END // 4], F32))

        def at(name, offset, shape, dtype=F32):
            return nc.alloc_sbuf_tensor_at(name, shape, dtype, offset=base + offset)

        x_tok = at("x_tok", M_X, [P, NT, C])
        xT = at("xT", M_XT, [P, KC, T])
        v_tok = at("v_tok", M_V, [P, NT, C])
        arena_o = at("arena_o", M_O, [P, 8192])
        arena_s = at("arena_s", M_S, [P, 12288])
        arena_p = at("arena_p", M_P, [P, 4096])
        v_grp = at("v_grp", M_VG, [P, 2, NT, R, VW])
        arena_w = at("arena_w", M_W, [P, 6144])
        arena_f = at("arena_f", M_F, [P, 4096])
        small = at("small", M_SMALL, [P, 2600])
        ident = at("ident", M_ID, [P, P])
        ident_b = at("ident_b", M_ID + 512, [P, P], BF16)
        maskb = at("maskb", M_ID + 768, [P, P], BF16)
        w0_hl = [at(f"w0_{n}", M_S + 24576 * n, [P, KC, 3 * C], F32R) for n in range(2)]
        x0_hl = [at("x0_h", M_XT, [P, KC, T], F32R), at("x0_l", M_X, [P, KC, T], F32R)]
        w1_hl = [at(f"w1_{n}", M_S + 8192 + 12288 * n, [P, KC, C + 2 * P], F32R) for n in range(2)]
        x1_hl = [at("x1_h", M_XT, [P, KC, T], F32R), at("x1_l", M_S + 32768, [P, KC, T], F32R)]
        x2_hl = [at("x2_h", M_XT, [P, KC, T], F32R), at("x2_l", M_V, [P, KC, T], F32R)]
        psum = stack.enter_context(nc.psum_tensor("psum", [P, 8, 512], F32))

        q_parts = [nc.dram_tensor(f"q_parts{n}", [H, NPART, D, T], BF16, kind="Internal").ap()
                   for n in range(2)]
        k_parts = [nc.dram_tensor(f"k_parts{n}", [h, NPART, D, T], BF16, kind="Internal").ap()
                   for n, h in ((0, H), (1, KV1))]

        wq_b = view(small, 0, [KC, BOT])
        wr_b = view(small, 1024, [RDIM], parts=BOT)
        akey_b = view(small, 1216, [NSLOT], parts=BOT)
        av_b = view(small, 1728, [KC, NSLOT])
        wvd_b = view(small, 3776, [KC, VB])
        wvu_b = view(small, 4288, [C], parts=VB)
        wu1_b = view(small, 6336, [KC, HU])
        wu2_b = view(small, 8384, [1])
        bu1_b = view(small, 8388, [1])
        logrel_b = view(small, 8392, [NSLOT])
        scal = view(small, 8904, [7])
        bu2, gate_w1, gate_bias, gating, s_gate, s_up, s_down = (scal[:, n:n + 1] for n in range(7))
        ones = view(small, 8932, [P])
        eps = view(small, 9444, [1])

        load_and_project(nc, d, 0, dict(
            x_tok=x_tok, v_tok=v_tok, arena_o=arena_o, arena_p=arena_p, arena_w=arena_w,
            arena_f=arena_f, ident=ident, ident_b=ident_b, maskb=maskb, psum=psum, v_grp=v_grp,
            w_hl=w0_hl, x_hl=x0_hl, q_parts=q_parts[0], k_parts=k_parts[0], ones=ones, eps=eps,
            small_loads=[
                (wq_b, d["f_wqT"]), (wr_b, d["f_wrT"]), (akey_b, d["f_akeyT"]), (av_b, d["f_avT"]),
                (wvd_b, d["f_wvdT"]), (wvu_b, d["f_wvuT"]), (wu1_b, d["f_wu1T"]),
                (wu2_b, d["f_wu2T"]), (bu1_b, d["f_bu1"]), (logrel_b, d["f_logrel"]),
                *[(scal[:, n:n + 1], d[k]) for n, k in enumerate(
                    ["f_bu2", "f_gate_w1", "f_gate_bias", "gating", "s_gate", "s_up", "s_down"])],
            ]))
        adapter(nc, d, x_tok, arena_o, arena_w, arena_f, ident, gating, psum)
        attention(nc, 0, arena_o, arena_s, arena_p, v_tok, v_grp, ident_b, maskb,
                  q_parts[0], k_parts[0], psum)
        finish_attention(nc, 0, d, x_tok, xT, v_tok, arena_o, arena_s, arena_w,
                         view(arena_f, 0, [KC, C]), ident, eps, psum, None, None)
        lookup(nc, d, x_tok, xT, arena_o, arena_s, arena_w, w1_hl, x1_hl, ident, ones, eps, psum,
               wq_b, wr_b, akey_b, av_b, wvd_b, wvu_b, wu1_b, wu2_b, bu1_b, logrel_b,
               bu2, gate_w1, gate_bias)
        load_and_project(nc, d, 1, dict(
            x_tok=x_tok, v_tok=v_tok, arena_o=arena_o, arena_p=arena_p, arena_w=arena_w,
            arena_f=arena_f, ident=ident, ident_b=ident_b, maskb=maskb, psum=psum, v_grp=v_grp,
            w_hl=w1_hl, x_hl=x1_hl, q_parts=q_parts[1], k_parts=k_parts[1], ones=ones, eps=eps, small_loads=[]))
        ff = SwigluArrays(nc, at)
        attention(nc, 1, arena_o, arena_s, arena_p, v_tok, v_grp, ident_b, maskb,
                  q_parts[1], k_parts[1], psum)
        finish_attention(nc, 1, d, x_tok, xT, v_tok, arena_o, arena_s, arena_w,
                         view(arena_w, 12288, [KC, C]), ident, eps, psum, x2_hl, ff)
        swiglu(nc, d, x_tok, x2_hl, ff, s_gate, s_up, s_down, eps, psum, out)


class Phase:

    def __init__(self, nc, name, recycle=False):
        self.nc, self.name, self.stack, self.sems = nc, name, ExitStack(), []
        self.recycle = recycle

    def __enter__(self):
        return self

    def sem(self, name):
        self.sems.append(self.nc.alloc_semaphore(f"{self.name}_{name}"))
        return self.sems[-1]

    def block(self):
        return self.stack.enter_context(self.nc.Block())

    def __exit__(self, *what):
        self.stack.__exit__(*what)
        if self.recycle and what[0] is None:
            self.nc.clear_and_free_semaphores(self.sems)
            self.nc.all_engine_barrier()


def load_and_project(nc, d, layer, m):
    nk = 4 if layer == 0 else 1
    n_out = C + nk * P + (C if layer == 0 else P)
    vw = C if layer == 0 else P
    w = view(m["arena_w"], 0, [KC, n_out])
    cos = view(m["arena_p"], 0, [T])
    sin = view(m["arena_p"], 4096, [T])
    parts = view(m["arena_p"], 8192, [2, NPART, 512], BF16)
    rot = view(m["arena_p"], 8192 + 6144, [P])
    q_rot = view(m["arena_o"], 0, [KC, T])
    raw = view(m["arena_o"], 16384, [2, 512])
    t_cos = view(m["arena_o"], 20480, [2, 512])
    t_sin = view(m["arena_o"], 24576, [2, 512])
    k_rot = view(m["arena_o"], 28672, [2, 512])
    psum, v_tok, (wh, wl), (xh, xl) = m["psum"], m["v_tok"], m["w_hl"], m["x_hl"]
    x_raw = v_tok[:, :, :].rearrange("p t c -> p (t c)").rearrange("p (k n) -> p k n", k=KC)
    units = [("q", t, c) for c in range(CH) for t in range(KC)] \
        + [("k", t, c) for c in range(CH) for t in range(nk)]
    pieces = []
    if layer == 0:
        for kind, n0 in (("x", 0), ("w", 0), ("x", 512), ("w", C), ("w", 2 * C)):
            pieces += [(kind, k, n0) for k in range(KC)]

    def cut_of(piece):
        kind, k, n0 = piece
        return [a[:, k, n0:n0 + 512] for a in ((x_raw, xh, xl) if kind == "x" else (w, wh, wl))]

    def products(pe, out, lhs, rhs):
        for k in range(KC):
            for n, (i, j) in enumerate(((0, 0), (0, 1), (1, 0))):
                last = pe.matmul(out, lhs[i](k), rhs[j](k), start=k + n == 0, stop=k == KC - 1 and n == 2)
        return last
    n_units = len(units)

    def rotated(n):
        kind, t, c = units[n]
        return q_rot[:, t, 512 * c:512 * c + 512] if kind == "q" else k_rot[:, n % 2, :]

    with Phase(nc, f"proj{layer}") as ph:
        aux_loaded, tables = ph.sem("aux_loaded"), ph.sem("tables")
        proj_ready, raw_ready, rot_ready = ph.sem("proj_ready"), ph.sem("raw_ready"), ph.sem("rot_ready")
        cos_ready, sin_ready, sum_ready = ph.sem("cos_ready"), ph.sem("sin_ready"), ph.sem("sum_ready")
        hi_ready, res_ready, mid_ready = ph.sem("hi_ready"), ph.sem("res_ready"), ph.sem("mid_ready")
        lo_ready = ph.sem("lo_ready")
        stored = [ph.sem("stored0"), ph.sem("stored1")]
        v_ready, v_copied, consts = ph.sem("v_ready"), ph.sem("v_copied"), ph.sem("consts")
        arrived = [ph.sem(f"arrived{n}") for n in range(len(pieces) // KC)]
        cut_h, cut_l = ph.sem("cut_h"), ph.sem("cut_l")
        block = ph.block()

        @block.sync
        def _(sp):
            for n, (kind, k, n0) in enumerate(pieces):
                src = d["xT"] if kind == "x" else d["w0"]
                sp.dma_start(cut_of(pieces[n])[0], src[P * k:P * k + P, n0:n0 + 512])\
                    .then_inc(arrived[n // KC], 16)
            sp.dma_start(rot, d["rot"]).then_inc(tables, 16)
            sp.dma_start(cos, d[f"cos{layer}"]).then_inc(tables, 16)
            sp.dma_start(sin, d[f"sin{layer}"]).then_inc(tables, 16)
            if layer == 0:
                n_aux = 0
                for dst, src in ((m["ident"][:, :], d["ident"]),
                                 (view(m["arena_f"], 0, [KC, C]), d["wo0"].rearrange("(k p) n -> p k n", p=P)),
                                 *m["small_loads"]):
                    if len(dst.shape) == 3 and len(src.shape) == 2:
                        src = src.rearrange("p (k n) -> p k n", k=KC)
                    sp.dma_start(dst, src).then_inc(aux_loaded, 16)
                    n_aux += 1
            for n, (kind, t, c) in enumerate(units):
                sp.wait_ge(lo_ready, n + 1)
                dest = m["q_parts"] if kind == "q" else m["k_parts"]
                for j in range(NPART):
                    sp.dma_start(dest[HPT * t:HPT * t + HPT, j, :, 512 * c:512 * c + 512],
                                 parts[:, n % 2, j, :]).then_inc(stored[n % 2], 16)
            for side in range(2):
                sp.wait_ge(stored[side], 16 * NPART * (n_units // 2))
            if layer == 0:
                sp.wait_ge(aux_loaded, 16 * n_aux)

        @block.tensor
        def _(pe):
            def rotate(n):
                pe.wait_ge(raw_ready, n + 1)
                if n == 0:
                    pe.wait_ge(tables, 48)
                if n >= 2:
                    pe.wait_ge(sin_ready, n - 1)
                pe.matmul(psum[:, 2 + n % 2, :], rot, raw[:, n % 2, :], start=True, stop=True)\
                    .then_inc(rot_ready, 1)

            for n, (kind, t, c) in enumerate(units):
                if n >= 2:
                    pe.wait_ge(raw_ready, n - 1)
                if layer == 0:
                    pe.wait_ge(cut_l, KC * ((2 if c == 0 else 3) if kind == "q" else 4))
                col = (0 if kind == "q" else C) + P * t
                products(pe, psum[:, n % 2, :],
                         [lambda k, a=a: a[:, k, col:col + P] for a in (wh, wl)],
                         [lambda k, a=a: a[:, k, 512 * c:512 * c + 512] for a in (xh, xl)])\
                    .then_inc(proj_ready, 1)
                if n >= 1:
                    rotate(n - 1)
            rotate(n_units - 1)
            for t in range(NT):
                if t >= 2:
                    pe.wait_ge(v_copied, t - 1)
                if layer == 0:
                    pe.wait_ge(cut_l, len(pieces))
                products(pe, psum[:, 4 + t % 2, 0:vw],
                         [lambda k, a=a: a[:, k, P * t:P * t + P] for a in (xh, xl)],
                         [lambda k, a=a: a[:, k, C + nk * P:n_out] for a in (wh, wl)])\
                    .then_inc(v_ready, 1)

        @block.scalar
        def _(act):
            def high(n):
                act.wait_ge(sum_ready, n + 1)
                if n >= 2:
                    act.wait_ge(stored[n % 2], 16 * NPART * (n // 2))
                act.copy(parts[:, n % 2, 0, :], rotated(n)).then_inc(hi_ready, 1)

            def cut_high(n):
                act.wait_ge(arrived[n // KC], 16 * KC)
                raw_piece, h, _ = cut_of(pieces[n])
                act.copy(h, raw_piece).then_inc(cut_h, 1)

            for n in range(min(len(pieces), 2 * KC)):
                cut_high(n)
            for n in range(n_units):
                if 2 * KC + 2 * n < len(pieces):
                    cut_high(2 * KC + 2 * n)
                    cut_high(2 * KC + 2 * n + 1)
                act.wait_ge(proj_ready, n + 1)
                if n >= 2:
                    act.wait_ge(rot_ready, n - 1)
                    act.wait_ge(cos_ready, n - 1)
                act.copy(raw[:, n % 2, :], psum[:, n % 2, :]).then_inc(raw_ready, 1)
                if n >= 1:
                    high(n - 1)
            high(n_units - 1)
            for t in range(NT):
                act.wait_ge(v_ready, t + 1)
                act.copy(v_tok[:, t, 0:vw], psum[:, 4 + t % 2, 0:vw]).then_inc(v_copied, 1)

        @block.vector
        def _(dve):
            def low(n):
                dve.wait_ge(res_ready, n + 1)
                dve.tensor_copy(parts[:, n % 2, 1, :], t_cos[:, n % 2, :]).then_inc(mid_ready, 1)
                dve.wait_ge(mid_ready, n + 1)
                dve.tensor_tensor(parts[:, n % 2, 2, :], t_cos[:, n % 2, :], parts[:, n % 2, 1, :],
                                  ALU.subtract).then_inc(lo_ready, 1)

            def cut_low(n):
                dve.wait_ge(cut_h, n + 1)
                raw_piece, h, lo = cut_of(pieces[n])
                dve.tensor_tensor(lo, raw_piece, h.bitcast(F32), ALU.subtract).then_inc(cut_l, 1)

            for n in range(min(len(pieces), 2 * KC)):
                cut_low(n)
            dve.wait_ge(tables, 48)
            for n, (kind, t, c) in enumerate(units):
                if 2 * KC + 2 * n < len(pieces):
                    cut_low(2 * KC + 2 * n)
                    cut_low(2 * KC + 2 * n + 1)
                dve.wait_ge(raw_ready, n + 1)
                if n >= 2:
                    dve.wait_ge(lo_ready, n - 1)
                dve.tensor_tensor(t_cos[:, n % 2, :], raw[:, n % 2, :],
                                  cos[:, 512 * c:512 * c + 512], ALU.mult).then_inc(cos_ready, 1)
                dve.wait_ge(rot_ready, n + 1)
                if n >= 2:
                    dve.wait_ge(sum_ready, n - 1)
                dve.tensor_tensor(t_sin[:, n % 2, :], psum[:, 2 + n % 2, :],
                                  sin[:, 512 * c:512 * c + 512], ALU.mult).then_inc(sin_ready, 1)
                if n >= 1:
                    low(n - 1)
            low(n_units - 1)

        @block.gpsimd
        def _(pool):
            if layer == 0:
                pool.memset(m["v_grp"][:, :, :, :, D:VW], 1.0).then_inc(consts, 1)
                pool.memset(m["ones"], 1.0).then_inc(consts, 1)
                pool.memset(m["eps"], EPS).then_inc(consts, 1)
                pool.memset(m["maskb"][:, :], 0.0).then_inc(consts, 1)
                pool.memset(m["ident_b"][:, :], 0.0).then_inc(consts, 1)
                pool.wait_ge(consts, 5)
                pool.affine_select(out=m["maskb"][:, :], in_=m["maskb"][:, :], compare_op=ALU.is_ge,
                                   fill=-BIG, base=0, pattern=[[-1, P]], channel_multiplier=1)\
                    .then_inc(consts, 1)
                pool.affine_select(out=m["ident_b"][:, :], in_=m["ident_b"][:, :],
                                   compare_op=ALU.not_equal, fill=1.0, base=0, pattern=[[-1, P]],
                                   channel_multiplier=1).then_inc(consts, 1)
                pool.wait_ge(consts, 7)
            for n, (kind, t, c) in enumerate(units):
                s = n % 2
                pool.wait_ge(cos_ready, n + 1)
                pool.wait_ge(sin_ready, n + 1)
                if kind == "k" and n >= 2:
                    pool.wait_ge(hi_ready, n - 1)
                pool.tensor_tensor(rotated(n), t_cos[:, s, :], t_sin[:, s, :], ALU.add)\
                    .then_inc(sum_ready, 1)
                pool.wait_ge(sum_ready, n + 1)
                pool.wait_ge(hi_ready, n + 1)
                pool.tensor_tensor(t_cos[:, s, :], rotated(n), parts[:, s, 0, :], ALU.subtract)\
                    .then_inc(res_ready, 1)


def adapter(nc, d, y_ad, arena_o, arena_w, arena_f, ident, gating, psum):
    q_rot = view(arena_o, 0, [KC, T])
    w = view(arena_w, 0, [KC, 3 * C])
    AW = HPT * ADP
    HT = NT // 2
    a_rep = view(arena_f, 8192, [KC, AW])
    ak_bd = view(arena_f, 9472, [KC, AW])
    av_bd = view(arena_f, 10752, [KC, P], parts=AW)
    hm_k = view(arena_f, 12800, [HPT])
    hm_v = view(arena_f, 12832, [HPT], parts=AW)
    mx = view(arena_f, 12864, [HT, H])
    sc = view(arena_o, 16384, [HT, H * ADP])
    prob = view(arena_o, 16384 + 5120, [HT, H * ADP])
    pT = view(arena_o, 16384 + 10240, [2, KC, P], parts=AW)

    def heads(a):
        return a.rearrange("p t (h a) -> p t h a", a=ADP)

    with Phase(nc, "adapter") as ph:
        loaded, chain_s = ph.sem("loaded"), ph.sem("chain")
        kv_ready, bd_ready = ph.sem("kv_ready"), ph.sem("bd_ready")
        scores_ready, shifted, exped, prob_ready = (ph.sem(n) for n in
                                                    ("scores_ready", "shifted", "exped", "prob_ready"))
        pT_ready, pT_copied, y_ready, y_copied = (ph.sem(n) for n in
                                                  ("pT_ready", "pT_copied", "y_ready", "y_copied"))
        block = ph.block()

        @block.sync
        def _(sp):
            sp.dma_start(a_rep, d["a_repT"].rearrange("(k p) n -> p k n", p=P)).then_inc(loaded, 16)
            sp.dma_start(hm_k, d["hm_k"]).then_inc(loaded, 16)
            sp.dma_start(hm_v, d["hm_v"]).then_inc(loaded, 16)
            sp.wait_ge(loaded, 48)

        @block.tensor
        def _(pe):
            pe.wait_ge(loaded, 48)
            for t in range(KC):
                for k in range(KC):
                    pe.matmul(psum[:, 6, ADP * t:ADP * t + ADP], w[:, k, C + P * t:C + P * t + P],
                              a_rep[:, k, 0:ADP], start=k == 0, stop=k == KC - 1)
            for k in range(KC):
                last = pe.matmul(psum[0:AW, 7, :], a_rep[:, k, :], w[:, k, 2 * C:3 * C],
                                 start=k == 0, stop=k == KC - 1)
            last.then_inc(kv_ready, 1)
            pe.wait_ge(bd_ready, 1)
            for half in range(2):
                if half:
                    pe.wait_ge(shifted, 1)
                for i in range(HT):
                    tok = P * (HT * half + i)
                    for t in range(KC):
                        last = pe.matmul(psum[:, i, AW * t:AW * t + AW], q_rot[:, t, tok:tok + P],
                                         ak_bd[:, t, :], start=True, stop=True)
                last.then_inc(scores_ready, 1)
                pe.wait_ge(prob_ready, half + 1)
                for i in range(HT):
                    n = HT * half + i
                    if n >= 2:
                        pe.wait_ge(pT_copied, n - 1)
                    for t in range(KC):
                        last = pe.transpose(psum[0:AW, 4 + n % 2, P * t:P * t + P],
                                            prob[:, i, AW * t:AW * t + AW], ident[:, :])
                    last.then_inc(pT_ready, 1)
                    pe.wait_ge(pT_copied, n + 1)
                    if n >= 2:
                        pe.wait_ge(y_copied, n - 1)
                    for t in range(KC):
                        last = pe.matmul(psum[:, 6 + n % 2, P * t:P * t + P], pT[:, n % 2, t, :],
                                         av_bd[:, t, :], start=True, stop=True)
                    last.then_inc(y_ready, 1)

        @block.scalar
        def _(act):
            for half in range(2):
                act.wait_ge(shifted, half + 1)
                if half:
                    act.wait_ge(pT_ready, HT)
                act.activation(prob, sc, ACT.Exp, scale=float(C) ** -0.5).then_inc(exped, 1)
                for i in range(HT):
                    n = HT * half + i
                    act.wait_ge(pT_ready, n + 1)
                    if n >= 2:
                        act.wait_ge(y_ready, n - 1)
                    act.copy(pT[:, n % 2, :, :], psum[0:AW, 4 + n % 2, :].rearrange(
                        "p (t q) -> p t q", q=P)).then_inc(pT_copied, 1)
                    act.wait_ge(y_ready, n + 1)
                    act.copy(y_ad[:, n, :], psum[:, 6 + n % 2, :]).then_inc(y_copied, 1)

        @block.vector
        def _(dve):
            link = Chain(dve, chain_s)
            dve.wait_ge(kv_ready, 1)
            dve.wait_ge(loaded, 48)
            link(dve.tensor_tensor(
                ak_bd.rearrange("p t (h a) -> p t h a", a=ADP),
                psum[:, 6, 0:KC * ADP].rearrange("p (t o a) -> p t o a", o=1, a=ADP)
                .broadcast_to([P, KC, HPT, ADP]),
                hm_k.rearrange("p (t h a) -> p t h a", t=1, a=1).broadcast_to([P, KC, HPT, ADP]),
                ALU.mult))
            dve.tensor_tensor(
                av_bd.rearrange("p t (h f) -> p t h f", f=D),
                psum[0:AW, 7, :].rearrange("p (t h f) -> p t h f", h=HPT, f=D),
                hm_v.rearrange("p (t h f) -> p t h f", t=1, f=1).broadcast_to([AW, KC, HPT, D]),
                ALU.mult).then_inc(bd_ready, 1)
            for half in range(2):
                dve.wait_ge(scores_ready, half + 1)
                if half:
                    dve.wait_ge(exped, 1)
                ps = heads(psum[:, 0:HT, 0:H * ADP])
                wide = [P, HT, H, ADP]
                link(dve.tensor_reduce(mx, ps, AX, ALU.max))
                dve.tensor_tensor(heads(sc), ps, mx.rearrange("p t (h o) -> p t h o", o=1)
                                  .broadcast_to(wide), ALU.subtract).then_inc(shifted, 1)
                dve.wait_ge(exped, half + 1)
                dve.wait_ge(shifted, half + 1)
                link(dve.tensor_reduce(mx, heads(prob), AX, ALU.add))
                link(dve.reciprocal(mx, mx))
                link(dve.tensor_scalar(mx, mx, gating, None, ALU.mult))
                dve.tensor_tensor(heads(prob), heads(prob), mx.rearrange("p t (h o) -> p t h o", o=1)
                                  .broadcast_to(wide), ALU.mult).then_inc(prob_ready, 1)


def attention(nc, layer, arena_o, arena_s, arena_p, v_tok, v_grp, ident_b, maskb,
              q_parts, k_parts, psum):
    kr = R if layer == 0 else 1
    scale = float(D) ** -0.5
    q_st = view(arena_s, 0, [2, CH, R * 512], BF16)
    k_max = view(arena_s, 16384, [2, R * T], BF16)
    k_exp = view(arena_s, 32768, [2, R * T], BF16)
    pr = view(arena_p, 0, [NP_RING, 2, 512])
    o_raw = view(arena_o, 0, [NG, T])

    with Phase(nc, f"att{layer}", recycle=layer == 0) as ph, ExitStack() as own:
        mx = own.enter_context(nc.sbuf_tensor(f"mx{layer}", [P, CH, R * 4], F32))
        md = own.enter_context(nc.sbuf_tensor(f"md{layer}", [P, R * 4], F32))
        mst = own.enter_context(nc.sbuf_tensor(f"mst{layer}", [P, 2, NPART, R * 4], BF16))
        mT = own.enter_context(nc.sbuf_tensor(f"mT{layer}", [NPART * R * 4, 2, P], BF16))
        q_loaded = [[ph.sem(f"q_loaded{s}{c}") for c in range(CH)] for s in range(2)]
        max_loaded = [[ph.sem(f"max_loaded{s}{c}") for c in range(CH)] for s in range(2)]
        km_loaded = [ph.sem(f"km_loaded{s}") for s in range(2)]
        ke_loaded = [ph.sem(f"ke_loaded{s}") for s in range(2)]
        qk_ready, qk_taken = ph.sem("qk_ready"), ph.sem("qk_taken")
        max_ready, dve_link = ph.sem("max_ready"), ph.sem("dve_link")
        scores_ready, exp_ready = ph.sem("scores_ready"), ph.sem("exp_ready")
        masked, pv_done = ph.sem("masked"), ph.sem("pv_done")
        o_copied, vg_ready, rows = ph.sem("o_copied"), ph.sem("vg_ready"), ph.sem("rows")
        passed_pe, passed_pool = ph.sem("passed_pe"), ph.sem("passed_pool")
        block = ph.block()

        n_tiles = [4 * (c + 1) for c in range(CH)]
        first_half = [0, 2 * n_tiles[0]]
        BG = 2 * sum(n_tiles)
        DG = 2 * 4 * CH
        assert BG % NP_RING == 0

        def pieces(c):
            out = []
            for i in range(4):
                for kc in range(c):
                    out += [(i, (r,), kc, 512) for r in range(R)]
                heads = [(0, 1), (2, 3)] if i < 2 else [(r,) for r in range(R)]
                out += [(i, hs, c, P * (i + 1)) for hs in heads]
            return out

        def entries(c, with_pieces=True, with_t=True):
            out = list(pieces(c)) if with_pieces else []
            if with_t:
                out.insert(min(2, len(out)), "T")
            return out

        RING = (4, 5, 7)
        first0 = len(entries(0, with_t=False))
        start = first0 + len(entries(1))
        n_entries = [len(entries(c)) for c in range(CH)]
        EG = sum(n_entries)
        assert EG % len(RING) == 0

        def first_entry(g, c):
            at = start + (n_entries[0] if c else 0)
            return EG * g + at, at

        def first_column(c, kt):
            return max(0, P * kt - 512 * c)

        def pairs(engine, body):
            with engine.Fori(0, NG // 2 - 1) as pair:
                body(pair, False)
            body(NG // 2 - 1, True)

        @block.sync
        def _(sp):
            def load_q(g, s, c):
                for j0, n in ((0, 3), (3, 2), (5, 1)):
                    sp.dma_start(
                        q_st[D * j0:D * (j0 + n), s, c, :].rearrange("p (h t) -> p h t", h=R),
                        q_parts[bass.ds(R * g, R), 0:n, :, 512 * c:512 * c + 512]
                        .rearrange("h j d t -> j d h t")).then_inc(q_loaded[s][c], 16)

            def load_k(g, s, dst, sem):
                for j, (_, kp) in enumerate(PAIRS):
                    sp.dma_start(
                        dst[D * j:D * j + D, s, 0:kr * T].rearrange("p (h t) -> p h t", h=kr),
                        k_parts[bass.ds(kr * g, kr), kp, :, :].rearrange("h d t -> d h t"))\
                        .then_inc(sem[s], 16)

            def load_max(entry, s, c):
                sp.wait_ge(qk_taken, entry + 1)
                for j in range(NPART):
                    sp.dma_start(q_st[KS + j:KS + j + 1, s, c, :].rearrange("p (i t) -> p i t", t=P),
                                 mT[R * 4 * j:R * 4 * (j + 1), c, :]).then_inc(max_loaded[s][c], 16)

            load_q(0, 0, 0)
            load_k(0, 0, k_max, km_loaded)
            load_q(0, 0, 1)
            load_k(0, 0, k_exp, ke_loaded)
            load_q(1, 1, 0)
            load_k(1, 1, k_max, km_loaded)
            load_max(first0 + 2, 0, 0)

            def body(pair, last):
                for a in range(2):
                    g = 2 * pair + a
                    alone = last and a == 1
                    load_max(first_entry(g, 0)[0] + (0 if alone else 2), a, 1)
                    if alone:
                        break
                    sp.wait_ge(scores_ready, BG * g + 1)
                    load_q(g + 1, 1 - a, 1)
                    load_k(g + 1, 1 - a, k_exp, ke_loaded)
                    load_max(first_entry(g, 1)[0] + 2, 1 - a, 0)
                    if last:
                        continue
                    sp.wait_ge(scores_ready, BG * g + first_half[1])
                    load_q(g + 2, a, 0)
                    sp.wait_ge(qk_ready, first_entry(g, 0)[0])
                    load_k(g + 2, a, k_max, km_loaded)

            pairs(sp, body)

        @block.tensor
        def _(pe):
            def entry(number, at, what, pair, s, c, first):
                if at >= len(RING):
                    pe.wait_ge(qk_taken, number - len(RING) + 1)
                bank = RING[at % len(RING)]
                if what == "T":
                    tc = 1 - c
                    pe.wait_ge(max_ready, 2 * (2 * pair + s) + c)
                    pe.sem_inc(passed_pe, 1)
                    pe.transpose(psum[0:NPART * R * 4, bank, 0:P // 2].bitcast(BF16),
                                 mst[:, tc, :, :].rearrange("p j i -> p (j i)"), ident_b[:, :])\
                        .then_inc(qk_ready, 1)
                    return
                i, heads, kc, width = what
                if first:
                    pe.wait_ge(q_loaded[s][c], 48 * pair + 48)
                    if c == 0:
                        pe.wait_ge(km_loaded[s], 96 * pair + 96)
                for n, r in enumerate(heads):
                    kh = r if layer == 0 else 0
                    last = pe.matmul(psum[:, bank, width * n:width * n + width],
                                     q_st[0:KS, s, c, 512 * r + P * i:512 * r + P * i + P],
                                     k_max[0:KS, s, T * kh + 512 * kc:T * kh + 512 * kc + width],
                                     start=True, stop=kc < c)
                    if kc == c:
                        last = pe.matmul(psum[:, bank, width * (n + 1) - P:width * (n + 1)],
                                         ident_b[:, :], maskb[:, :], start=False, stop=True)
                last.then_inc(qk_ready, 1)

            def scores(pair, s, c, kt, hp):
                n = first_half[c] + 2 * kt + hp
                o = first_column(c, kt)
                if kt == 0 and hp == 0:
                    pe.wait_ge(max_loaded[s][c], 48 * pair + 48)
                    if c == 0:
                        pe.wait_ge(ke_loaded[s], 96 * pair + 96)
                if not (isinstance(pair, int) and pair == 0 and n < 2):
                    pe.wait_ge(exp_ready, BG * (2 * pair + s) + n - 1)
                for h in range(2):
                    r = 2 * hp + h
                    kh = r if layer == 0 else 0
                    last = pe.matmul(psum[:, 2 * hp + h, o:512],
                                     k_exp[0:KM, s, T * kh + P * kt:T * kh + P * kt + P],
                                     q_st[0:KM, s, c, 512 * r + o:512 * r + 512],
                                     start=True, stop=True)
                last.then_inc(scores_ready, 1)

            def values(pair, s, c, kt):
                g = 2 * pair + s
                n = first_half[c] + 2 * kt
                o = first_column(c, kt)
                if kt >= 4 * c:
                    pe.wait_ge(masked, DG * g + 2 * kt + 2)
                else:
                    pe.wait_ge(exp_ready, BG * g + n + 2)
                if kt == 0:
                    if c == 0:
                        pe.wait_ge(vg_ready, g + 1)
                    pe.wait_ge(o_copied, 2 * g + c + 1)
                for r in range(R):
                    last = pe.matmul(psum[32 * r:32 * r + VW, 6, o:512],
                                     v_grp[:, s, kt, r if layer == 0 else 0, :],
                                     pr[:, (n + r // 2) % NP_RING, r % 2, o:512],
                                     start=kt == 0, stop=kt == 4 * c + 3, tile_position=(0, 32 * r))
                last.then_inc(pv_done, 2)

            pe.sem_inc(pv_done, NP_RING)
            pe.wait_ge(rows, 2)
            for n, what in enumerate(entries(0, with_t=False)):
                entry(n, n, what, 0, 0, 0, n == 0)
            for n, what in enumerate(entries(1)):
                entry(first0 + n, first0 + n, what, 0, 0, 1, n == 0)
            scores(0, 0, 0, 0, 0)
            scores(0, 0, 0, 0, 1)

            def body(pair, last):
                for a in range(2):
                    alone = last and a == 1
                    nxt = (pair, 1) if a == 0 else (pair + 1, 0)
                    for c in range(CH):
                        todo = entries(c, not alone, not (alone and c == 1))
                        number, at = first_entry(2 * pair + a, c)
                        done = [0, 0]

                        def slot():
                            done[0] += 1
                            n_slots = 1 if alone else 4 * n_tiles[c]
                            while done[1] < min(len(todo), len(todo) * done[0] // n_slots):
                                entry(number + done[1], at + done[1], todo[done[1]], *nxt, c,
                                      done[1] == 0)
                                done[1] += 1

                        for kt in range(n_tiles[c]):
                            if kt + 1 < n_tiles[c]:
                                ahead = (pair, a, c, kt + 1)
                            elif c == 0:
                                ahead = (pair, a, 1, 0)
                            else:
                                ahead = None if alone else (*nxt, 0, 0)
                            for hp in range(2):
                                if ahead:
                                    scores(*ahead, hp)
                                slot()
                            slot()
                            values(pair, a, c, kt)
                            slot()

            pairs(pe, body)

        @block.scalar
        def _(act):
            def exp(g, c, b):
                n = first_half[c] + b
                o = first_column(c, b // 2)
                act.wait_ge(scores_ready, BG * g + n + 1)
                act.wait_ge(pv_done, BG * g + n + 1)
                act.activation(pr[:, n % NP_RING, :, o:512],
                               psum[:, 2 * (b % 2):2 * (b % 2) + 2, o:512],
                               ACT.Exp, scale=scale).then_inc(exp_ready, 1)

            def copy_o(g, c):
                act.wait_ge(pv_done, NP_RING + BG * g + first_half[c] + 2 * n_tiles[c])
                act.copy(o_raw[:, bass.ds(g, 1), 512 * c:512 * c + 512], psum[:, 6, :])\
                    .then_inc(o_copied, 1)

            act.sem_inc(o_copied, 1)
            exp(0, 0, 0)

            def body(pair, last):
                for a in range(2):
                    g = 2 * pair + a
                    for b in range(1, 2 * n_tiles[0]):
                        exp(g, 0, b)
                    exp(g, 1, 0)
                    copy_o(g, 0)
                    for b in range(1, 2 * n_tiles[1]):
                        exp(g, 1, b)
                    if not (last and a == 1):
                        exp(g + 1, 0, 0)
                    copy_o(g, 1)

            pairs(act, body)

        @block.vector
        def _(dve):
            LINKS = [3, 4]

            def unit(number, at, todo, G, c):
                for n, what in enumerate(todo):
                    bank = RING[(at + n) % len(RING)]
                    dve.wait_ge(qk_ready, number + n + 1)
                    if what == "T":
                        dve.tensor_copy(mT[:, 1 - c, :],
                                        psum[0:NPART * R * 4, bank, 0:P // 2].bitcast(BF16))\
                            .then_inc(qk_taken, 1)
                        continue
                    i, heads, kc, width = what
                    if n == 0 and not (isinstance(G, int) and G == 0 and c == 0):
                        dve.wait_ge(max_ready, 2 * G + c)
                    src = psum[:, bank, 0:width * len(heads)]
                    if len(heads) > 1:
                        src = src.rearrange("p (h k) -> p h k", h=len(heads))
                    col = 4 * heads[0] + i
                    dve.tensor_reduce(mx[:, kc, col:col + 4 * len(heads) - 3:4], src, AX, ALU.max)\
                        .then_inc(qk_taken, 1)
                if len(todo) == 1:
                    return
                base = sum(LINKS) * G + (LINKS[0] if c else 0)
                dve.wait_ge(qk_taken, number + len(todo))
                if c == 1:
                    dve.tensor_tensor(mx[:, 0, :], mx[:, 0, :], mx[:, 1, :], ALU.max)\
                        .then_inc(dve_link, 1)
                    dve.wait_ge(dve_link, base + 1)
                    base = base + 1
                dve.tensor_copy(mst[:, c, 0, :], mx[:, 0, :]).then_inc(dve_link, 1)
                dve.wait_ge(dve_link, base + 1)
                dve.tensor_tensor(md[:, :], mx[:, 0, :], mst[:, c, 0, :], ALU.subtract)\
                    .then_inc(dve_link, 1)
                dve.wait_ge(dve_link, base + 2)
                dve.tensor_copy(mst[:, c, 1, :], md[:, :]).then_inc(dve_link, 1)
                dve.wait_ge(dve_link, base + 3)
                dve.tensor_tensor(mst[:, c, 2, :], md[:, :], mst[:, c, 1, :], ALU.subtract)\
                    .then_inc(max_ready, 1)

            unit(0, 0, entries(0, with_t=False), 0, 0)
            unit(first0, first0, entries(1), 0, 1)

            def body(pair, last):
                for a in range(2):
                    alone = last and a == 1
                    for c in range(CH):
                        if not (alone and c == 1):
                            unit(*first_entry(2 * pair + a, c), entries(c, not alone),
                                 2 * pair + a + 1, c)

            pairs(dve, body)

        @block.gpsimd
        def _(pool):
            pool.memset(k_exp[KS:KM, 0, :], -1.0).then_inc(rows, 1)
            pool.memset(k_exp[KS:KM, 1, :], -1.0).then_inc(rows, 1)
            vgw = kr * D

            def load_v(g, s):
                pool.wait_ge(pv_done, NP_RING + BG * g - BG)
                pool.tensor_copy(v_grp[:, s, :, 0:kr, 0:D],
                                 v_tok[:, :, bass.ds(vgw * g, vgw)]
                                 .rearrange("p t (r f) -> p t r f", f=D)).then_inc(vg_ready, 1)

            pool.wait_ge(rows, 2)
            pool.tensor_copy(v_grp[:, 0, :, 0:kr, 0:D],
                             v_tok[:, :, 0:vgw].rearrange("p t (r f) -> p t r f", f=D))\
                .then_inc(vg_ready, 1)

            def body(pair, last):
                for a in range(2):
                    g = 2 * pair + a
                    for c in range(CH):
                        for b in range(8 * c, 8 * c + 8):
                            n = first_half[c] + b
                            o = first_column(c, b // 2)
                            pool.wait_ge(exp_ready, BG * g + n + 1)
                            pool.sem_inc(passed_pool, 1)
                            tri = pr[:, n % NP_RING, :, o:o + P]
                            pool.affine_select(out=tri, in_=tri, compare_op=ALU.is_ge, fill=0.0,
                                               base=0, pattern=[[0, 2], [1, P]],
                                               channel_multiplier=-1).then_inc(masked, 1)
                        if c == 0 and not (last and a == 1):
                            load_v(g + 1, 1 - a)

            pairs(pool, body)


def norm_stats(dve, link, src, stats):
    link(dve.bn_stats(stats[:, 0:6], src))
    return dve.bn_aggr(stats[:, 6:8], stats[:, 0:6])


def norm_root(act, stats, eps):
    return act.activation(stats[:, 8:9], stats[:, 7:8], ACT.Sqrt, bias=eps)


def norm_apply(dve, link, dst, src, stats):
    link(dve.reciprocal(stats[:, 8:9], stats[:, 8:9]))
    return dve.tensor_scalar(dst, src, stats[:, 6:7], stats[:, 8:9], ALU.subtract, ALU.mult)


def finish_attention(nc, layer, d, x_tok, xT, v_tok, arena_o, arena_s, arena_w, w_out, ident, eps, psum, x_hl, ff):
    o_raw = view(arena_o, 0, [NG, T])
    y = view(arena_s, 0, [2, C])
    yT = view(arena_s, 4096, [2, KC, P])
    h = view(arena_s, 8192, [2, C])
    rec = view(arena_s, 12288, [H])
    stats = view(arena_s, 12416, [2, 9])
    with Phase(nc, f"fin{layer}") as ph:
        x_loaded, chain_s = ph.sem("x_loaded"), ph.sem("chain")
        oT_ready, y_ready, yT_ready, yT_copied = (ph.sem(n) for n in
                                                  ("oT_ready", "y_ready", "yT_ready", "yT_copied"))
        z_ready, x_ready, xT_ready, xT_copied = (ph.sem(n) for n in
                                                 ("z_ready", "x_ready", "xT_ready", "xT_copied"))
        xT_cut = ph.sem("xT_cut")
        z_added, var_ready, dev_ready = ph.sem("z_added"), ph.sem("var_ready"), ph.sem("dev_ready")
        block = ph.block()

        @block.sync
        def _(sp):
            if layer == 1:
                ff.prefetch(sp, d)
            if layer == 0:
                sp.dma_start(v_tok[:, :, :], d["x"].rearrange("(t p) c -> p t c", p=P))\
                    .then_inc(x_loaded, 16)
                w_next = view(arena_w, 0, [KC, C + 2 * P])
                sp.dma_start(w_next, d["w1"].rearrange("(k p) n -> p k n", p=P)).then_inc(x_loaded, 16)
                sp.dma_start(view(arena_w, 12288, [KC, C]), d["wo1"].rearrange("(k p) n -> p k n", p=P))\
                    .then_inc(x_loaded, 16)
                sp.wait_ge(x_loaded, 48)

        @block.tensor
        def _(pe):
            for s in range(NT + 4):
                if s < NT:
                    t = s
                    if t >= 2:
                        pe.wait_ge(y_ready, t - 1)
                    for g in range(NG):
                        last = pe.transpose(psum[:, 2 * (t % 2) + g // 4, P * (g % 4):P * (g % 4) + P],
                                            o_raw[:, g, P * t:P * t + P], ident[:, :])
                    last.then_inc(oT_ready, 1)
                if 0 <= s - 1 < NT:
                    t = s - 1
                    pe.wait_ge(y_ready, t + 1)
                    if t >= 1:
                        pe.wait_ge(yT_copied, t)
                    for k in range(KC):
                        last = pe.transpose(psum[:, 4, P * k:P * k + P],
                                            y[:, t % 2, P * k:P * k + P], ident[:, :])
                    last.then_inc(yT_ready, 1)
                if 0 <= s - 2 < NT:
                    t = s - 2
                    pe.wait_ge(yT_copied, t + 1)
                    if t >= 1:
                        pe.wait_ge(z_added, t)
                    for k in range(KC):
                        last = pe.matmul(psum[:, 5, :], yT[:, t % 2, k, :], w_out[:, k, :],
                                         start=k == 0, stop=k == KC - 1)
                    last.then_inc(z_ready, 1)
                if 0 <= s - 4 < NT:
                    t = s - 4
                    pe.wait_ge(x_ready, t + 1)
                    if t >= 1:
                        pe.wait_ge(xT_copied if layer == 0 else xT_cut, t)
                    for k in range(KC):
                        last = pe.transpose(psum[:, 6, P * k:P * k + P],
                                            x_tok[:, t, P * k:P * k + P], ident[:, :])
                    last.then_inc(xT_ready, 1)

        @block.scalar
        def _(act):
            for s in range(NT + 4):
                if 0 <= s - 1 < NT:
                    t = s - 1
                    act.wait_ge(yT_ready, t + 1)
                    if t >= 2:
                        act.wait_ge(z_ready, t - 1)
                    act.copy(yT[:, t % 2, :, :], psum[:, 4, :].rearrange("p (k q) -> p k q", q=P))\
                        .then_inc(yT_copied, 1)
                if 0 <= s - 2 < NT:
                    t = s - 2
                    act.wait_ge(var_ready, t + 1)
                    norm_root(act, stats[:, t % 2, :], eps).then_inc(dev_ready, 1)
                if 0 <= s - 4 < NT:
                    t = s - 4
                    act.wait_ge(xT_ready, t + 1)
                    dst = xT if layer == 0 else x_hl[0]
                    act.copy(dst[:, :, P * t:P * t + P], psum[:, 6, :].rearrange("p (k q) -> p k q", q=P))\
                        .then_inc(xT_copied, 1)

        @block.vector
        def _(dve):
            link = Chain(dve, chain_s)
            if layer == 0:
                dve.wait_ge(x_loaded, 48)
            for s in range(NT + (3 if layer == 0 else 5)):
                if s < NT:
                    t = s
                    dve.wait_ge(oT_ready, t + 1)
                    if t >= 2:
                        dve.wait_ge(yT_ready, t - 1)
                    o = psum[:, 2 * (t % 2):2 * (t % 2) + 2, :].rearrange("p b (h f) -> p (b h) f", f=VW)
                    if t >= 1:
                        dve.wait_ge(y_ready, t)
                    link(dve.reciprocal(rec, o[:, :, D]))
                    out_y = y[:, t % 2, :].rearrange("p (h f) -> p h f", f=D)
                    mul = dve.tensor_tensor(out_y, o[:, :, 0:D], rec.rearrange("p (h o) -> p h o", o=1)
                                            .broadcast_to([P, H, D]), ALU.mult)
                    if layer == 0:
                        link(mul)
                        mul = dve.tensor_tensor(y[:, t % 2, :], y[:, t % 2, :], x_tok[:, t, :], ALU.add)
                    mul.then_inc(y_ready, 1)
                if 0 <= s - 2 < NT:
                    t = s - 2
                    dve.wait_ge(z_ready, t + 1)
                    dve.wait_ge(y_ready, t + 1)
                    if t >= 2:
                        dve.wait_ge(x_ready, t - 1)
                    res = v_tok[:, t, :] if layer == 0 else x_tok[:, t, :]
                    dve.tensor_tensor(h[:, t % 2, :], psum[:, 5, :], res, ALU.add).then_inc(z_added, 1)
                    dve.wait_ge(z_added, t + 1)
                    norm_stats(dve, link, h[:, t % 2, :], stats[:, t % 2, :]).then_inc(var_ready, 1)
                if 0 <= s - 3 < NT:
                    t = s - 3
                    dve.wait_ge(dev_ready, t + 1)
                    norm_apply(dve, link, x_tok[:, t, :], h[:, t % 2, :], stats[:, t % 2, :])\
                        .then_inc(x_ready, 1)
                if layer == 1 and 0 <= s - 5 < NT:
                    t = s - 5
                    dve.wait_ge(xT_copied, t + 1)
                    dve.tensor_tensor(x_hl[1][:, :, P * t:P * t + P],
                                      psum[:, 6, :].rearrange("p (k q) -> p k q", q=P),
                                      x_hl[0][:, :, P * t:P * t + P].bitcast(F32), ALU.subtract)\
                        .then_inc(xT_cut, 1)


def lookup(nc, d, x_tok, xT, arena_o, arena_s, arena_w, w_hl, x_hl, ident, ones, eps, psum, wq, wr, akey, av, wvd, wvu,
           wu1, wu2, bu1, logrel, bu2, gate_w1, gate_bias):
    hid = view(arena_o, 0, [T])
    query = view(arena_o, 4096, [T], parts=BOT)
    rq = view(arena_o, 8192, [T], parts=RDIM)
    rs = view(arena_o, 12288, [NT, NSLOT])
    at = view(arena_o, 16384, [NT, NSLOT])
    rest = view(arena_o, 20480, [NT, NSLOT])
    wT = view(arena_o, 24576, [T])
    aux = view(arena_o, 28672, [2, C])
    rk = view(arena_s, 0, [NSLOT], parts=RDIM)
    dn = view(arena_s, 512, [NSLOT], parts=VB)
    vals = view(arena_s, 1024, [C])
    top = view(arena_s, 3072, [NT, 8])
    n8 = [view(arena_s, 3328 + 32 * n, [NT]) for n in range(8)]
    mxs, sums, var, lv, learned, gate, tmp, tmp2 = n8
    lvs = view(arena_s, 3584, [1])
    stats2 = view(arena_s, 3712, [2, 9])
    stats = stats2[:, 0, :]
    var2 = view(arena_s, 3648, [NT, 2])
    h = view(arena_s, 4096, [2, C])
    last_exp = float(BOT) ** -0.5
    with Phase(nc, "lookup") as ph:
        pre, pre_copied = ph.sem("pre"), ph.sem("pre_copied")
        qh_ready, qh_copied, s_ready, s_read = (ph.sem(n) for n in
                                                ("qh_ready", "qh_copied", "s_ready", "s_read"))
        shifted, exped, wT_ready, wT_copied = (ph.sem(n) for n in
                                               ("shifted", "exped", "wT_ready", "wT_copied"))
        lv_done, lvs_ready, mean_ready, lin_ready = (ph.sem(n) for n in
                                                     ("lv_done", "lvs_ready", "mean_ready", "lin_ready"))
        var_ready, sig_in, sig_out, gate_ready = (ph.sem(n) for n in
                                                  ("var_ready", "sig_in", "sig_out", "gate_ready"))
        z_ready, aux_ready, x_ready, xT_ready, xT_copied = (ph.sem(n) for n in
                                                            ("z_ready", "aux_ready", "x_ready", "xT_ready", "xT_copied"))
        chain_s, g_in, g_out = ph.sem("chain"), ph.sem("g_in"), ph.sem("g_out")
        row_var, dev_ready = ph.sem("row_var"), ph.sem("dev_ready")
        xT_cut, w_cut = ph.sem("xT_cut"), ph.sem("w_cut")
        block = ph.block()

        @block.gpsimd
        def _(pool):
            w_raw = view(arena_w, 0, [KC, C + 2 * P])
            for k in range(KC):
                pool.tensor_copy(w_hl[0][:, k, :], w_raw[:, k, :]).then_inc(w_cut, 1)
                pool.wait_ge(w_cut, 2 * k + 1)
                pool.tensor_tensor(w_hl[1][:, k, :], w_raw[:, k, :], w_hl[0][:, k, :].bitcast(F32),
                                   ALU.subtract).then_inc(w_cut, 1)

        @block.tensor
        def _(pe):
            for c in range(CH):
                for k in range(KC):
                    last = pe.matmul(psum[:, c, :], wu1[:, k, :], xT[:, k, 512 * c:512 * c + 512],
                                     start=k == 0, stop=k == KC - 1)
                last.then_inc(qh_ready, 1)
            for c in range(CH):
                for k in range(KC):
                    last = pe.matmul(psum[0:BOT, 2 + c, :], wq[:, k, :], xT[:, k, 512 * c:512 * c + 512],
                                     start=k == 0, stop=k == KC - 1)
                last.then_inc(qh_ready, 1)
            pe.matmul(psum[0:RDIM, 4, 0:NSLOT], wr, akey, start=True, stop=True)
            for k in range(KC):
                last = pe.matmul(psum[0:VB, 5, 0:NSLOT], wvd[:, k, :], av[:, k, :],
                                 start=k == 0, stop=k == KC - 1)
            last.then_inc(pre, 1)
            pe.wait_ge(pre_copied, 2)
            pe.matmul(psum[:, 6, :], dn, wvu, start=True, stop=True).then_inc(pre, 1)
            pe.wait_ge(qh_copied, 4)
            for c in range(CH):
                last = pe.matmul(psum[0:RDIM, 4 + c, :], wr, query[:, 512 * c:512 * c + 512],
                                 start=True, stop=True)
            last.then_inc(qh_ready, 1)
            pe.wait_ge(qh_copied, 5)
            for t in range(NT):
                pe.matmul(psum[:, t // 4, P * (t % 4):P * (t % 4) + NSLOT], rq[:, P * t:P * t + P], rk,
                          start=True, stop=True)
                last = pe.matmul(psum[:, 2 + t // 4, P * (t % 4):P * (t % 4) + NSLOT],
                                 query[:, P * t:P * t + P], akey, start=True, stop=True)
            last.then_inc(s_ready, 1)
            pe.wait_ge(pre_copied, 3)
            for t in range(NT):
                last = pe.matmul(psum[:, 4, t:t + 1], hid[:, P * t:P * t + P], wu2, start=True, stop=True)
            last.then_inc(lin_ready, 1)
            pe.wait_ge(lvs_ready, 1)
            pe.matmul(psum[:, 5, 0:1], ones, lvs, start=True, stop=True).then_inc(mean_ready, 1)
            pe.wait_ge(exped, 1)
            pe.wait_ge(s_read, 1)
            for t in range(NT):
                last = pe.transpose(psum[:, t // 4, P * (t % 4):P * (t % 4) + P], at[:, t, :], ident[:, :])
            last.then_inc(wT_ready, 1)
            pe.wait_ge(wT_copied, 1)
            for s in range(NT + 3):
                if s < NT:
                    t = s
                    if t >= 2:
                        pe.wait_ge(aux_ready, t - 1)
                    pe.matmul(psum[:, 2 + t % 2, :], wT[:, P * t:P * t + P], vals, start=True, stop=True)\
                        .then_inc(z_ready, 1)
                if s >= 3:
                    t = s - 3
                    pe.wait_ge(x_ready, t + 1)
                    if t >= 2:
                        pe.wait_ge(xT_cut, t - 1)
                    for k in range(KC):
                        last = pe.transpose(psum[:, 6 + t % 2, P * k:P * k + P],
                                            x_tok[:, t, P * k:P * k + P], ident[:, :])
                    last.then_inc(xT_ready, 1)

        @block.scalar
        def _(act):
            for c in range(CH):
                act.wait_ge(qh_ready, c + 1)
                act.activation(hid[:, 512 * c:512 * c + 512], psum[:, c, :], ACT.Gelu_apprx_tanh,
                               bias=bu1[:, :]).then_inc(qh_copied, 1)
            for c in range(CH):
                act.wait_ge(qh_ready, 3 + c)
                act.copy(query[:, 512 * c:512 * c + 512], psum[0:BOT, 2 + c, :]).then_inc(qh_copied, 1)
            act.wait_ge(pre, 1)
            act.copy(rk, psum[0:RDIM, 4, 0:NSLOT]).then_inc(pre_copied, 1)
            act.copy(dn, psum[0:VB, 5, 0:NSLOT]).then_inc(pre_copied, 1)
            act.wait_ge(pre, 2)
            act.copy(vals, psum[:, 6, :]).then_inc(pre_copied, 1)
            act.wait_ge(qh_ready, 5)
            act.copy(rq.rearrange("p (c t) -> p c t", c=CH), psum[0:RDIM, 4:6, :]).then_inc(qh_copied, 1)
            act.wait_ge(var_ready, 1)
            act.activation(lv, var, ACT.Ln, bias=1.0).then_inc(lv_done, 1)
            act.wait_ge(sig_in, 1)
            act.activation(learned, tmp, ACT.Sigmoid).then_inc(sig_out, 1)
            act.wait_ge(g_in, 1)
            act.activation(tmp, gate, ACT.Sigmoid).then_inc(g_out, 1)
            act.wait_ge(shifted, 1)
            act.activation(at, rest, ACT.Exp).then_inc(exped, 1)
            act.wait_ge(wT_ready, 1)
            act.copy(wT.rearrange("p (c t) -> p c t", c=CH), psum[:, 0:2, :]).then_inc(wT_copied, 1)
            act.wait_ge(gate_ready, 1)
            for s in range(NT + 3):
                if s < NT:
                    t = s
                    act.wait_ge(z_ready, t + 1)
                    if t >= 2:
                        act.wait_ge(row_var, t - 1)
                    act.activation(aux[:, t % 2, :], psum[:, 2 + t % 2, :], ACT.Copy,
                                   scale=gate[:, t:t + 1]).then_inc(aux_ready, 1)
                if 1 <= s <= NT:
                    t = s - 1
                    act.wait_ge(row_var, t + 1)
                    norm_root(act, stats2[:, t % 2, :], eps).then_inc(dev_ready, 1)
                if s >= 3:
                    t = s - 3
                    act.wait_ge(xT_ready, t + 1)
                    act.copy(x_hl[0][:, :, P * t:P * t + P], psum[:, 6 + t % 2, :]
                             .rearrange("p (k q) -> p k q", q=P)).then_inc(xT_copied, 1)

        @block.vector
        def _(dve):
            link = Chain(dve, chain_s)
            for t in range(NT):
                link(dve.bn_stats(stats[:, 0:6], x_tok[:, t, :]))
                link(dve.bn_aggr(var2[:, t, :], stats[:, 0:6]))
            dve.tensor_copy(var, var2[:, :, 1]).then_inc(var_ready, 1)
            dve.wait_ge(lv_done, 1)
            dve.tensor_reduce(lvs, lv, AX, ALU.add).then_inc(lvs_ready, 1)
            dve.wait_ge(mean_ready, 1)
            link(dve.tensor_scalar(lvs, psum[:, 5, 0:1], 1.0 / T, 1e-6, ALU.mult, ALU.add))
            link(dve.reciprocal(lvs, lvs))
            link(dve.tensor_scalar(tmp2, lv, lvs, 0.5, ALU.mult, ALU.mult))
            dve.wait_ge(lin_ready, 1)
            dve.tensor_scalar(tmp, psum[:, 4, 0:NT], bu2, None, ALU.add).then_inc(sig_in, 1)
            dve.wait_ge(sig_out, 1)
            link(dve.scalar_tensor_tensor(out=gate, in0=learned, scalar=2.5, in1=tmp2,
                                          op0=ALU.mult, op1=ALU.add))
            link(dve.tensor_scalar(gate, gate, 0.0, 5.0, ALU.max, ALU.min))
            link(dve.tensor_scalar(gate, gate, 0.5, 1.0 / 1.5, ALU.subtract, ALU.mult))
            link(dve.tensor_scalar(gate, gate, 0.0, 1.0, ALU.max, ALU.min))
            dve.tensor_scalar(gate, gate, gate_w1, gate_bias, ALU.mult, ALU.add).then_inc(g_in, 1)
            dve.wait_ge(g_out, 1)
            link(dve.tensor_scalar(learned, tmp, 0.05, None, ALU.is_ge))
            link(dve.tensor_tensor(gate, tmp, learned, ALU.mult))
            dve.wait_ge(s_ready, 1)
            lr = logrel.rearrange("p (o n) -> p o n", o=1).broadcast_to([P, NT, NSLOT])
            ps = [psum[:, 2 * n:2 * n + 2, :].rearrange("p b (t n) -> p (b t) n", n=NSLOT) for n in range(2)]
            link(dve.scalar_tensor_tensor(out=rs, in0=ps[0], scalar=float(1 / np.sqrt(RDIM)), in1=lr,
                                          op0=ALU.mult, op1=ALU.add))
            dve.scalar_tensor_tensor(out=at, in0=ps[1], scalar=last_exp, in1=lr,
                                     op0=ALU.mult, op1=ALU.add).then_inc(s_read, 1)
            dve.wait_ge(s_read, 1)
            for t in range(NT):
                link(dve.max(top[:, t, :], rs[:, t, :]))
            for t in range(NT):
                link(dve.match_replace(out=rest[:, t, :], in_to_replace=top[:, t, :],
                                       in_values=rs[:, t, :], imm_value=-3e38))
            link(dve.tensor_tensor(rs, rs, rest, ALU.is_equal))
            link(dve.scalar_tensor_tensor(out=at, in0=rs, scalar=-BIG, in1=at,
                                          op0=ALU.mult, op1=ALU.add))
            link(dve.tensor_reduce(mxs, at, AX, ALU.max))
            dve.tensor_tensor(rest, at, mxs.rearrange("p (t o) -> p t o", o=1)
                              .broadcast_to([P, NT, NSLOT]), ALU.subtract).then_inc(shifted, 1)
            dve.wait_ge(exped, 1)
            link(dve.tensor_reduce(sums, at, AX, ALU.add))
            link(dve.reciprocal(sums, sums))
            dve.tensor_tensor(gate, gate, sums, ALU.mult).then_inc(gate_ready, 1)
            for s in range(NT + 4):
                if s >= 4:
                    t = s - 4
                    dve.wait_ge(xT_copied, t + 1)
                    dve.tensor_tensor(x_hl[1][:, :, P * t:P * t + P],
                                      psum[:, 6 + t % 2, :].rearrange("p (k q) -> p k q", q=P),
                                      x_hl[0][:, :, P * t:P * t + P].bitcast(F32), ALU.subtract)\
                        .then_inc(xT_cut, 1)
                if s < NT:
                    t = s
                    dve.wait_ge(aux_ready, t + 1)
                    if t >= 2:
                        dve.wait_ge(x_ready, t - 1)
                    link(dve.scalar_tensor_tensor(out=h[:, t % 2, :], in0=x_tok[:, t, :], scalar=2.0,
                                                  in1=aux[:, t % 2, :], op0=ALU.mult, op1=ALU.add))
                    norm_stats(dve, link, h[:, t % 2, :], stats2[:, t % 2, :]).then_inc(row_var, 1)
                if 1 <= s <= NT:
                    t = s - 1
                    dve.wait_ge(dev_ready, t + 1)
                    norm_apply(dve, link, x_tok[:, t, :], h[:, t % 2, :], stats2[:, t % 2, :])\
                        .then_inc(x_ready, 1)


class SwigluArrays:

    def __init__(self, nc, at):
        self.nc = nc
        self.raw = at("ff_raw", M_RAW, [P, 2, 2 * KC * P])
        self.w_hl = [at(f"ff_w{n}", M_WIN + 8192 * n, [P, 2, 2 * KC * P], F32R) for n in range(2)]
        self.g_hl = [at(f"ff_g{n}", m, [P, NI, T], F32R) for n, m in enumerate((M_GH, M_GL))]
        self.wd_raw = at("ff_wd_raw", M_WD, [P, NI, C])
        self.wd_hl = [at(f"ff_wd{n}", M_XT + NI * C * 4 * n, [P, NI, C], F32R) for n in range(2)]
        self.silu = at("ff_silu", M_TMP, [P, 2, 512])
        self.h = at("ff_h", M_TMP, [P, 2, C])
        self.prod = at("ff_prod", M_TMP + 4096, [P, 2, 512])
        self.stats = at("ff_stats", M_TMP + 8192, [P, 2, 9])
        self.arrived = [nc.alloc_semaphore(f"ff_arrived{n}") for n in range(2)]
        self.wd_arrived = nc.alloc_semaphore("ff_wd_arrived")

    def load_in(self, sp, d, i):
        sp.dma_start(self.raw[:, i % 2, :], d["w_in"][i]).then_inc(self.arrived[i % 2], 16)

    def prefetch(self, sp, d):
        self.load_in(sp, d, 0)
        self.load_in(sp, d, 1)
        full = P * (NI - 1)
        sp.dma_start(self.wd_raw[:, 0:NI - 1, :], d["w_down"][0:full, :]
                     .rearrange("(i p) n -> p i n", p=P)).then_inc(self.wd_arrived, 16)
        sp.dma_start(self.wd_raw[0:INTER - full, NI - 1, :], d["w_down"][full:, :])\
            .then_inc(self.wd_arrived, 16)


def swiglu(nc, d, x_tok, x_hl, ff, s_gate, s_up, s_down, eps, psum, out):
    TERMS = ((0, 0), (0, 1), (1, 0))
    rows = [min(P, INTER - P * i) for i in range(NI)]
    with Phase(nc, "swiglu") as ph:
        chain_s, stored = ph.sem("chain"), ph.sem("stored")
        w_high, w_low = ph.sem("w_high"), ph.sem("w_low")
        gu_ready, silu_ready, prod_ready = ph.sem("gu_ready"), ph.sem("silu_ready"), ph.sem("prod_ready")
        g_high, g_low = ph.sem("g_high"), ph.sem("g_low")
        wd_high, wd_low = ph.sem("wd_high"), ph.sem("wd_low")
        z_ready, z_scaled, x_ready = ph.sem("z_ready"), ph.sem("z_scaled"), ph.sem("x_ready")
        var_ready, dev_ready = ph.sem("var_ready"), ph.sem("dev_ready")
        block = ph.block()

        @block.sync
        def _(sp):
            for i in range(2, NI):
                sp.wait_ge(w_low, i - 1)
                ff.load_in(sp, d, i)
            for t in range(NT):
                sp.wait_ge(x_ready, t + 1)
                sp.dma_start(out[P * t:P * t + P, :], x_tok[:, t, :]).then_inc(stored, 16)
            sp.wait_ge(stored, 16 * NT)

        @block.tensor
        def _(pe):
            for i in range(NI):
                pe.wait_ge(w_low, i + 1)
                for c in range(CH):
                    n = CH * i + c
                    if n >= 2:
                        pe.wait_ge(prod_ready, n - 1)
                    for u in range(2):
                        for k in range(KC):
                            col = P * (KC * u + k)
                            for m, (a, b) in enumerate(TERMS):
                                last = pe.matmul(psum[0:rows[i], 2 * (n % 2) + u, :],
                                                 ff.w_hl[a][:, i % 2, col:col + rows[i]],
                                                 x_hl[b][:, k, 512 * c:512 * c + 512],
                                                 start=k + m == 0, stop=k == KC - 1 and m == 2)
                    last.then_inc(gu_ready, 1)
            for t in range(NT):
                if t >= 2:
                    pe.wait_ge(z_scaled, t - 1)
                for i in range(NI):
                    if t == 0:
                        pe.wait_ge(wd_low, i + 1)
                        if i == 0:
                            pe.wait_ge(g_low, CH * NI)
                    for m, (a, b) in enumerate(TERMS):
                        last = pe.matmul(psum[:, 4 + t % 2, :],
                                         ff.g_hl[a][0:rows[i], i, P * t:P * t + P],
                                         ff.wd_hl[b][0:rows[i], i, :],
                                         start=i + m == 0, stop=i == NI - 1 and m == 2)
                last.then_inc(z_ready, 1)

        def product(n):
            i, c = n // CH, n % CH
            return (ff.prod[0:rows[i], n % 2, :],
                    *[a[0:rows[i], i, 512 * c:512 * c + 512] for a in ff.g_hl])

        @block.scalar
        def _(act):
            def high(n):
                act.wait_ge(prod_ready, n + 1)
                src, h, _ = product(n)
                act.copy(h, src).then_inc(g_high, 1)

            for n in range(CH * NI):
                i = n // CH
                act.wait_ge(gu_ready, n + 1)
                if n >= 2:
                    act.wait_ge(prod_ready, n - 1)
                act.activation(ff.silu[0:rows[i], n % 2, :], psum[0:rows[i], 2 * (n % 2), :], ACT.Silu,
                               scale=s_gate[0:rows[i], :]).then_inc(silu_ready, 1)
                high(n)
            act.wait_ge(ff.wd_arrived, 32)
            for i in range(NI):
                act.copy(ff.wd_hl[0][0:rows[i], i, :], ff.wd_raw[0:rows[i], i, :]).then_inc(wd_high, 1)
            for t in range(NT):
                act.wait_ge(var_ready, t + 1)
                norm_root(act, ff.stats[:, t % 2, :], eps).then_inc(dev_ready, 1)

        @block.vector
        def _(dve):
            link = Chain(dve, chain_s)
            for n in range(CH * NI):
                i = n // CH
                dve.wait_ge(silu_ready, n + 1)
                if n >= 2:
                    dve.wait_ge(g_low, n - 1)
                src, h, lo = product(n)
                dve.scalar_tensor_tensor(out=src, in0=psum[0:rows[i], 2 * (n % 2) + 1, :],
                                         scalar=s_up[0:rows[i], :], in1=ff.silu[0:rows[i], n % 2, :],
                                         op0=ALU.mult, op1=ALU.mult).then_inc(prod_ready, 1)
                dve.wait_ge(g_high, n + 1)
                dve.tensor_tensor(lo, src, h.bitcast(F32), ALU.subtract).then_inc(g_low, 1)
            dve.wait_ge(gu_ready, CH * NI)
            for i in range(NI):
                dve.wait_ge(wd_high, i + 1)
                dve.tensor_tensor(ff.wd_hl[1][0:rows[i], i, :], ff.wd_raw[0:rows[i], i, :],
                                  ff.wd_hl[0][0:rows[i], i, :].bitcast(F32), ALU.subtract)\
                    .then_inc(wd_low, 1)
            for t in range(NT):
                dve.wait_ge(z_ready, t + 1)
                if t >= 2:
                    dve.wait_ge(x_ready, t - 1)
                dve.scalar_tensor_tensor(out=ff.h[:, t % 2, :], in0=psum[:, 4 + t % 2, :],
                                         scalar=s_down, in1=x_tok[:, t, :], op0=ALU.mult,
                                         op1=ALU.add).then_inc(z_scaled, 1)
                dve.wait_ge(z_scaled, t + 1)
                norm_stats(dve, link, ff.h[:, t % 2, :], ff.stats[:, t % 2, :]).then_inc(var_ready, 1)
                dve.wait_ge(dev_ready, t + 1)
                norm_apply(dve, link, x_tok[:, t, :], ff.h[:, t % 2, :], ff.stats[:, t % 2, :])\
                    .then_inc(x_ready, 1)

        @block.gpsimd
        def _(pool):
            for i in range(NI):
                pool.wait_ge(ff.arrived[i % 2], 16 * (i // 2 + 1))
                if i >= 2:
                    pool.wait_ge(gu_ready, CH * (i - 1))
                pool.tensor_copy(ff.w_hl[0][:, i % 2, :], ff.raw[:, i % 2, :]).then_inc(w_high, 1)
                pool.wait_ge(w_high, i + 1)
                pool.tensor_tensor(ff.w_hl[1][:, i % 2, :], ff.raw[:, i % 2, :],
                                   ff.w_hl[0][:, i % 2, :].bitcast(F32), ALU.subtract)\
                    .then_inc(w_low, 1)


def _rope(base):
    theta = (1.0 / np.float32(base) ** (np.arange(0, D, 2, dtype=np.float32) / np.float32(D))).astype(np.float32)
    angle = np.outer(np.arange(T, dtype=np.float32), theta).astype(np.float32)
    angle = np.concatenate([angle, angle], axis=1).T
    return (np.tile(np.cos(angle), (HPT, 1)).astype(np.float32),
            np.tile(np.sin(angle), (HPT, 1)).astype(np.float32))


def _constants():
    cos0, sin0 = _rope(10000.0)
    cos1, sin1 = _rope(500000.0)
    rot = np.zeros((P, P), np.float32)
    for h in range(HPT):
        for i in range(D // 2):
            rot[D * h + D // 2 + i, D * h + i] = -1.0
            rot[D * h + i, D * h + D // 2 + i] = 1.0
    eye = np.eye(P, dtype=np.float32)
    hm_k = (np.arange(P)[:, None] // D == np.arange(HPT)[None]).astype(np.float32)
    hm_v = (np.arange(HPT * ADP)[:, None] // ADP == np.arange(HPT)[None]).astype(np.float32)
    return dict(cos0=cos0, sin0=sin0, cos1=cos1, sin1=sin1, rot=rot, ident=eye, hm_k=hm_k, hm_v=hm_v)


def kernel(**inputs):
    import concourse.bacc as bacc
    from concourse.bass_utils import run_bass_kernel_spmd as run

    a = {k: np.asarray(v) for k, v in inputs.items()}
    tiles = lambda w: np.ascontiguousarray(w.reshape(KC, P, -1).transpose(1, 0, 2).reshape(P, -1))
    col = lambda v: np.broadcast_to(np.asarray(v).reshape(1, -1), (P, np.asarray(v).size)).copy()
    w_in = np.zeros((NI, P, 2, KC, P), np.float32)
    for u, name in enumerate(["L1_ffn_gate_w", "L1_ffn_up_w"]):
        wT = a[name].T.reshape(KC, P, INTER)
        for i in range(NI):
            n = min(P, INTER - P * i)
            w_in[i, :, u, :, 0:n] = wT[:, :, P * i:P * i + n].transpose(1, 0, 2)
    x0 = a["L0_attn_x"][0]
    d = dict(
        x=x0, xT=x0.T, w0=a["L0_attn_w_attn"].T, wo0=a["L0_attn_w_proj"].T,
        a_repT=np.tile(a["L0_attn_adapter_wte"].T, (1, HPT)), gating=col(a["L0_attn_gating"]),
        f_wqT=tiles(a["L0_ffn_Wq"].T), f_wrT=a["L0_ffn_Wr"].T, f_akeyT=a["L0_ffn_aux_keys"].T,
        f_avT=tiles(a["L0_ffn_aux_values"].T), f_wvdT=tiles(a["L0_ffn_Wvd"].T),
        f_wvuT=a["L0_ffn_Wvu"].T, f_wu1T=tiles(a["L0_ffn_Wu1"].T), f_wu2T=a["L0_ffn_Wu2"].T,
        f_bu1=a["L0_ffn_bu1"].reshape(HU, 1), f_logrel=col(a["L0_ffn_log_rel"]),
        f_bu2=col(a["L0_ffn_bu2"]), f_gate_w1=col(a["L0_ffn_gate_w1"]),
        f_gate_bias=col(a["L0_ffn_gate_bias"]),
        w1=np.concatenate([a["L1_attn_Wq"], a["L1_attn_Wk"], a["L1_attn_Wv"]], axis=1),
        wo1=a["L1_attn_Wo"], w_in=w_in.reshape(NI, P, -1), w_down=a["L1_ffn_down_w"].T,
        s_gate=col(a["L1_ffn_gate_scale"]), s_up=col(a["L1_ffn_up_scale"]),
        s_down=col(a["L1_ffn_down_scale"]), **_constants())
    nc = bacc.Bacc("TRN2", target_bir_lowering=False, num_devices=1)
    arrays, aps = {}, {}
    for name, v in d.items():
        v = np.ascontiguousarray(v)
        arrays[f"in_{name}"] = v
        aps[name] = nc.dram_tensor(f"in_{name}", v.shape, mybir.dt.from_np(v.dtype),
                                   kind="ExternalInput").ap()
    out = nc.dram_tensor("out", [T, C], F32, kind="ExternalOutput").ap()
    build(nc, aps, out)
    r = run(nc, [arrays], core_ids=[0])
    return np.asarray(r.results[0]["out"]).reshape(1, T, C)
```

```python
from contextlib import ExitStack

import numpy as np

import concourse.bass as bass
from concourse import mybir

F32 = mybir.dt.float32
BF16 = mybir.dt.bfloat16
F32R = mybir.dt.float32r
ALU = mybir.AluOpType
ACT = mybir.ActivationFunctionType
AX = mybir.AxisListType.X

P = 128
T, C = 1024, 512
H, D = 32, 16
NT = T // P
KC = C // P
CH = T // 512
R = 4
NG = H // R
KV1 = 8
NPART = 3
PAIRS = [(0, 0), (1, 0), (2, 0), (0, 1), (1, 1), (0, 2)]
KS = len(PAIRS) * D
KM = KS + NPART
VW = 32
ADP = 10
HPT = P // D
AW = HPT * ADP
BOT, RDIM, NSLOT, VB, HU = 64, 48, 128, 32, 128
INTER = 1376
NI = -(-INTER // P)
EPS = 1e-5
BIG = 1e30
NP_RING = 4


M_X, M_XT, M_V, M_O, M_S = 0, 16384, 32768, 49152, 81920
M_P, M_VG, M_W, M_F, M_SMALL, M_ID = 131072, 147456, 155648, 180224, 196608, 207040
MAP_END = 208064
M_TMP, M_WD, M_GH, M_RAW, M_WIN, M_GL = 49152, 61440, 83968, 129024, 137216, 153600
M_ROWS = 198656


def view(arena, offset, dims, dtype=F32, parts=P):
    n = int(np.prod(dims))
    size = 4 if dtype == F32 else 2
    assert offset % 4 == 0 and (n * size) % 4 == 0
    ap = arena[0:parts, offset // 4:offset // 4 + n * size // 4]
    if dtype != F32:
        ap = ap.bitcast(dtype)
    if len(dims) > 1:
        names = "abcd"[:len(dims)]
        ap = ap.rearrange(f"p ({' '.join(names)}) -> p {' '.join(names)}",
                          **{k: int(v) for k, v in zip(names, dims)})
    return ap


class Chain:

    def __init__(self, engine, semaphore):
        self.engine, self.semaphore, self.count = engine, semaphore, 0

    def __call__(self, instruction):
        self.later(instruction)
        self.all()

    def later(self, instruction):
        self.count += 1
        instruction.then_inc(self.semaphore, 1)

    def all(self):
        self.engine.wait_ge(self.semaphore, self.count)


def build(nc, d, out):
    with ExitStack() as stack:
        base = -(-nc.sbuf_base // 32) * 32
        stack.enter_context(nc.sbuf_tensor("fence", [P, MAP_END // 4], F32))

        def at(name, offset, shape, dtype=F32):
            return nc.alloc_sbuf_tensor_at(name, shape, dtype, offset=base + offset)

        x_tok = at("x_tok", M_X, [P, NT, C])
        xT = at("xT", M_XT, [P, KC, T])
        v_tok = at("v_tok", M_V, [P, NT, C])
        arena_o = at("arena_o", M_O, [P, 8192])
        arena_s = at("arena_s", M_S, [P, 12288])
        arena_p = at("arena_p", M_P, [P, 4096])
        v_grp = at("v_grp", M_VG, [P, 2, NT, R, VW])
        arena_w = at("arena_w", M_W, [P, 6144])
        arena_f = at("arena_f", M_F, [P, 4096])
        small = at("small", M_SMALL, [P, 2600])
        ident = at("ident", M_ID, [P, P])
        ident_b = at("ident_b", M_ID + 512, [P, P], BF16)
        maskb = at("maskb", M_ID + 768, [P, P], BF16)
        w0_hl = [at(f"w0_{n}", M_S + 24576 * n, [P, KC, 3 * C], F32R) for n in range(2)]
        x0_hl = [at("x0_h", M_XT, [P, KC, T], F32R), at("x0_l", M_X, [P, KC, T], F32R)]
        w1_hl = [at(f"w1_{n}", m, [P, KC, C + 2 * P], F32R) for n, m in
                 enumerate((M_S + 20480, M_W + 4096))]
        x1_hl = [at("x1_h", M_XT, [P, KC, T], F32R), at("x1_l", M_S + 32768, [P, KC, T], F32R)]
        wo_hl = [[at(f"wo{n}_h", M_W + 16384, [P, KC, C], F32R),
                  at(f"wo{n}_l", M_F + 8192 * n, [P, KC, C], F32R)] for n in range(2)]
        yT_hl = [at(f"yT_{n}", M_S + 16384 + 4096 * n, [P, 2, KC, P], F32R) for n in range(2)]
        x2_hl = [at("x2_h", M_XT, [P, KC, T], F32R), at("x2_l", M_V, [P, KC, T], F32R)]
        psum = stack.enter_context(nc.psum_tensor("psum", [P, 8, 512], F32))

        q_parts = [nc.dram_tensor(f"q_parts{n}", [H, NPART, D, T], BF16, kind="Internal").ap()
                   for n in range(2)]
        k_parts = [nc.dram_tensor(f"k_parts{n}", [NPART, D, h, T], BF16, kind="Internal").ap()
                   for n, h in ((0, H), (1, KV1))]

        wq_b = view(small, 0, [KC, BOT])
        wr_b = view(small, 1024, [RDIM], parts=BOT)
        akey_b = view(small, 1216, [NSLOT], parts=BOT)
        av_b = view(small, 1728, [KC, NSLOT])
        wvd_b = view(small, 3776, [KC, VB])
        wvu_b = view(small, 4288, [C], parts=VB)
        wu1_b = view(small, 6336, [KC, HU])
        wu2_b = view(small, 8384, [1])
        bu1_b = view(small, 8388, [1])
        logrel_b = view(small, 8392, [NSLOT])
        scal = view(small, 8904, [7])
        bu2, gate_w1, gate_bias, gating, s_gate, s_up, s_down = (scal[:, n:n + 1] for n in range(7))
        ones = view(small, 8932, [P])
        eps = view(small, 9444, [1])

        ad = dict(
            a_rep=view(arena_f, 8192, [KC, AW]),
            ak_bd=view(arena_f, 9472, [KC, AW]),
            av_bd=view(arena_f, 10752, [KC, P], parts=AW),
            hm_k=view(arena_f, 12800, [HPT]),
            hm_v=view(arena_f, 12832, [HPT], parts=AW),
            mx=view(arena_f, 12864, [NT // 2, H]),
            y=view(arena_w, 0, [NT, C]))
        att = Phase(nc, "att0", recycle=True)
        stacked = StackedOperands(att, 0, arena_s, q_parts[0], k_parts[0])
        load_and_project(nc, d, 0, dict(
            ad=ad, stacked=stacked,
            x_tok=x_tok, v_tok=v_tok, arena_o=arena_o, arena_p=arena_p, arena_w=arena_w,
            arena_f=arena_f, ident=ident, ident_b=ident_b, maskb=maskb, psum=psum, v_grp=v_grp,
            w_hl=w0_hl, x_hl=x0_hl, q_parts=q_parts[0], k_parts=k_parts[0], ones=ones, eps=eps,
            small_loads=[
                (wq_b, d["f_wqT"]), (wr_b, d["f_wrT"]), (akey_b, d["f_akeyT"]), (av_b, d["f_avT"]),
                (wvd_b, d["f_wvdT"]), (wvu_b, d["f_wvuT"]), (wu1_b, d["f_wu1T"]),
                (wu2_b, d["f_wu2T"]), (bu1_b, d["f_bu1"]), (logrel_b, d["f_logrel"]),
                *[(scal[:, n:n + 1], d[k]) for n, k in enumerate(
                    ["f_bu2", "f_gate_w1", "f_gate_bias", "gating", "s_gate", "s_up", "s_down"])],
            ]))
        x_loaded = nc.alloc_semaphore("x_loaded")
        wo = [view(arena_f, 8192 * n, [KC, C]) for n in range(2)]
        adapter(nc, d, ad, x_loaded, x_tok, v_tok, w0_hl, x0_hl, arena_o, ident, gating, psum, stacked,
                wo[0], wo_hl[0])
        attention(nc, 0, att, stacked, arena_o, arena_p, v_tok, v_grp, ident_b, maskb, psum)
        w1_raw = view(v_tok[:, :, :].rearrange("p t c -> p (t c)"), 0, [KC, C + 2 * P])
        finish_attention(nc, 0, d, x_loaded, x_tok, xT, ad["y"], arena_o, arena_s, w1_raw, wo[1],
                         wo_hl[0], yT_hl, ident, eps, psum, None, None)
        lookup(nc, x_tok, xT, arena_o, arena_s, arena_p, w1_raw, w1_hl, x1_hl, ident, ones, eps, psum,
               wq_b, wr_b, akey_b, av_b, wvd_b, wvu_b, wu1_b, wu2_b, bu1_b, logrel_b,
               bu2, gate_w1, gate_bias, wo[1], wo_hl[1])
        att = Phase(nc, "att1", recycle=True)
        stacked = StackedOperands(att, 1, arena_s, q_parts[1], k_parts[1])
        load_and_project(nc, d, 1, dict(
            stacked=stacked,
            x_tok=x_tok, v_tok=v_tok, arena_o=arena_o, arena_p=arena_p, arena_w=arena_w,
            arena_f=arena_f, ident=ident, ident_b=ident_b, maskb=maskb, psum=psum, v_grp=v_grp,
            w_hl=w1_hl, x_hl=x1_hl, q_parts=q_parts[1], k_parts=k_parts[1], ones=ones, eps=eps,
            small_loads=[]))
        ff = SwigluArrays(nc, at)
        attention(nc, 1, att, stacked, arena_o, arena_p, v_tok, v_grp, ident_b, maskb, psum)
        finish_attention(nc, 1, d, None, x_tok, xT, None, arena_o, arena_s, None, None, wo_hl[1],
                         yT_hl, ident, eps, psum, x2_hl, ff)
        swiglu(nc, d, x_tok, x2_hl, ff, s_gate, s_up, s_down, ones, eps, psum, out)


class Phase:

    def __init__(self, nc, name, recycle=False):
        self.nc, self.name, self.stack, self.sems = nc, name, ExitStack(), []
        self.recycle = recycle

    def __enter__(self):
        return self

    def sem(self, name):
        self.sems.append(self.nc.alloc_semaphore(f"{self.name}_{name}"))
        return self.sems[-1]

    def block(self):
        return self.stack.enter_context(self.nc.Block())

    def __exit__(self, *what):
        self.stack.__exit__(*what)
        if self.recycle and what[0] is None:
            self.nc.clear_and_free_semaphores(self.sems)
            self.nc.all_engine_barrier()


def products(pe, out, lhs, rhs, before=None):
    for k in range(KC):
        if before:
            before(k)
        for n, (i, j) in enumerate(((0, 0), (0, 1), (1, 0))):
            last = pe.matmul(out, lhs[i](k), rhs[j](k), start=k + n == 0, stop=k == KC - 1 and n == 2)
    return last


def load_and_project(nc, d, layer, m):
    nk = 4 if layer == 0 else 1
    n_out = C + nk * P + (C if layer == 0 else P)
    w = view(m["arena_w"], 0, [KC, n_out])
    v_T = view(m["arena_w"], 0, [CH, 512])
    cos = view(m["arena_p"], 0, [T])
    sin = view(m["arena_p"], 4096, [T])
    parts = view(m["arena_p"], 8192, [2, NPART, 512], BF16)
    rot = view(m["arena_p"], 8192 + 6144, [P])
    q_rot = view(m["arena_o"], 0, [KC, T])
    raw = view(m["arena_o"], 16384, [2, 512])
    t_cos = view(m["arena_o"], 20480, [2, 512])
    t_sin = view(m["arena_o"], 24576, [2, 512])
    k_rot = view(m["arena_o"], 28672, [2, 512])
    psum, v_tok, (wh, wl), (xh, xl) = m["psum"], m["v_tok"], m["w_hl"], m["x_hl"]
    x_raw = v_tok[:, :, :].rearrange("p t c -> p (t c)").rearrange("p (k n) -> p k n", k=KC)
    units = [("q", t, c) for c in range(CH) for t in range(KC)]
    keys = [("k", t, c) for c in range(CH) for t in range(nk)]
    units = units + keys if layer == 0 else keys + sorted(units, key=lambda u: u[1])
    pieces = []
    if layer == 0:
        pieces += [(kind, k, 0) for k in range(KC) for kind in "xw"]
        for kind, n0 in (("x", 512), ("w", C), ("w", 2 * C)):
            pieces += [(kind, k, n0) for k in range(KC)]
    batches = [(n, n + 2) for n in range(0, 2 * KC, 2)] \
        + [(n, n + KC) for n in range(2 * KC, len(pieces), KC)]

    def batch_of(n):
        return next(b for b, (first, end) in enumerate(batches) if first <= n < end)

    def cut_of(piece):
        kind, k, n0 = piece
        return [a[:, k, n0:n0 + 512] for a in ((x_raw, xh, xl) if kind == "x" else (w, wh, wl))]

    n_units = len(units)
    ad = m["ad"] if layer == 0 else None

    def rotated(n):
        kind, t, c = units[n]
        return q_rot[:, t, 512 * c:512 * c + 512] if kind == "q" else k_rot[:, n % 2, :]

    with Phase(nc, f"proj{layer}") as ph:
        aux_loaded, tables = ph.sem("aux_loaded"), [ph.sem(f"tables{c}") for c in range(CH)]
        rot_loaded = ph.sem("rot_loaded")
        proj_ready, raw_ready, rot_ready = ph.sem("proj_ready"), ph.sem("raw_ready"), ph.sem("rot_ready")
        cos_ready, sin_ready, sum_ready = ph.sem("cos_ready"), ph.sem("sin_ready"), ph.sem("sum_ready")
        hi_ready, res_ready, mid_ready = ph.sem("hi_ready"), ph.sem("res_ready"), ph.sem("mid_ready")
        lo_ready = ph.sem("lo_ready")
        stored = [ph.sem("stored0"), ph.sem("stored1")]
        v_ready, v_copied, consts = ph.sem("v_ready"), ph.sem("v_copied"), ph.sem("consts")
        ad_loaded, ad_ready, ad_spread = ph.sem("ad_loaded"), ph.sem("ad_ready"), ph.sem("ad_spread")
        arrived = [ph.sem(f"arrived{n}") for n in range(len(batches) if layer == 0 else 0)]
        cut_h, cut_l = ph.sem("cut_h"), ph.sem("cut_l")
        block = ph.block()

        @block.sync
        def _(sp):
            def load_tables(c):
                cs = slice(512 * c, 512 * c + 512)
                sp.dma_start(cos[:, cs], d[f"cos{layer}"][:, cs]).then_inc(tables[c], 16)
                sp.dma_start(sin[:, cs], d[f"sin{layer}"][:, cs]).then_inc(tables[c], 16)

            for n, (kind, k, n0) in enumerate(pieces):
                if n == 2 * KC:
                    sp.dma_start(rot, d["rot"]).then_inc(rot_loaded, 16)
                    load_tables(0)
                src = d["xT"] if kind == "x" else d["w0"]
                sp.dma_start(cut_of(pieces[n])[0], src[P * k:P * k + P, n0:n0 + 512])\
                    .then_inc(arrived[batch_of(n)], 16)
            if layer == 1:
                sp.dma_start(rot, d["rot"]).then_inc(rot_loaded, 16)
                load_tables(0)
            load_tables(1)
            if layer == 0:
                sp.dma_start(ad["a_rep"], d["a_repT"].rearrange("(k p) n -> p k n", p=P))\
                    .then_inc(ad_loaded, 16)
                sp.dma_start(ad["hm_k"], d["hm_k"]).then_inc(ad_loaded, 16)
                sp.dma_start(ad["hm_v"], d["hm_v"]).then_inc(ad_loaded, 16)
                n_aux = 0
                for dst, src in ((m["ident"][:, :], d["ident"]),
                                 (view(m["arena_f"], 0, [KC, C]), d["wo0"].rearrange("(k p) n -> p k n", p=P)),
                                 *m["small_loads"]):
                    if len(dst.shape) == 3 and len(src.shape) == 2:
                        src = src.rearrange("p (k n) -> p k n", k=KC)
                    sp.dma_start(dst, src).then_inc(aux_loaded, 16)
                    n_aux += 1
            for n, (kind, t, c) in enumerate(units):
                sp.wait_ge(lo_ready, n + 1)
                for j in range(NPART):
                    hs, cs = slice(HPT * t, HPT * t + HPT), slice(512 * c, 512 * c + 512)
                    sp.dma_start(m["q_parts"][hs, j, :, cs] if kind == "q" else
                                 m["k_parts"][j, :, hs, cs].rearrange("d h t -> h d t"),
                                 parts[:, n % 2, j, :]).then_inc(stored[n % 2], 16)
                if layer == 1 and n == 6:
                    for side in range(2):
                        sp.wait_ge(stored[side], 16 * NPART * 2)
                    m["stacked"].load_first(sp)
            m["stacked"].stored = [(s, 16 * NPART * (n_units // 2)) for s in stored]
            if layer == 0:
                m["stacked"].wait_stored(sp)
            if layer == 0:
                sp.wait_ge(aux_loaded, 16 * n_aux)

        @block.tensor
        def _(pe):
            def rotate(n):
                pe.wait_ge(raw_ready, n + 1)
                if n == 0:
                    pe.wait_ge(rot_loaded, 16)
                if n >= 2:
                    pe.wait_ge(sin_ready, n - 1)
                pe.matmul(psum[:, 2 + n % 2, :], rot, raw[:, n % 2, :], start=True, stop=True)\
                    .then_inc(rot_ready, 1)

            for n, (kind, t, c) in enumerate(units):
                if n >= 2:
                    pe.wait_ge(raw_ready, n - 1)
                if layer == 0 and n > 0:
                    pe.wait_ge(cut_l, KC * ((2 if c == 0 else 3) if kind == "q" else 4))
                col = (0 if kind == "q" else C) + P * t
                products(pe, psum[:, n % 2, :],
                         [lambda k, a=a: a[:, k, col:col + P] for a in (wh, wl)],
                         [lambda k, a=a: a[:, k, 512 * c:512 * c + 512] for a in (xh, xl)],
                         (lambda k: pe.wait_ge(cut_l, 2 * k + 2)) if layer == 0 and n == 0 else None)\
                    .then_inc(proj_ready, 1)
                if n >= 1:
                    rotate(n - 1)
            rotate(n_units - 1)
            if layer == 0:
                pe.wait_ge(ad_loaded, 48)
                pe.wait_ge(cut_l, len(pieces))
                for t in range(KC):
                    for k in range(KC):
                        pe.matmul(psum[:, 6, ADP * t:ADP * t + ADP],
                                  w[:, k, C + P * t:C + P * t + P], ad["a_rep"][:, k, 0:ADP],
                                  start=k == 0, stop=k == KC - 1)
                for k in range(KC):
                    last = pe.matmul(psum[0:AW, 7, :], ad["a_rep"][:, k, :], w[:, k, 2 * C:3 * C],
                                     start=k == 0, stop=k == KC - 1)
                last.then_inc(ad_ready, 1)
                return
            for c in range(CH):
                products(pe, psum[:, 4 + c, :],
                         [lambda k, a=a: a[:, k, C + nk * P:n_out] for a in (wh, wl)],
                         [lambda k, a=a: a[:, k, 512 * c:512 * c + 512] for a in (xh, xl)])\
                    .then_inc(v_ready, 1)
            for c in range(CH):
                pe.wait_ge(v_copied, c + 1)
                for t in range(4):
                    last = pe.transpose(psum[:, 6 + c, P * t:P * t + P],
                                        v_T[:, c, P * t:P * t + P], m["ident"][:, :])
                last.then_inc(v_ready, 1)

        @block.scalar
        def _(act):
            def high(n):
                act.wait_ge(sum_ready, n + 1)
                if n >= 2:
                    act.wait_ge(stored[n % 2], 16 * NPART * (n // 2))
                act.copy(parts[:, n % 2, 0, :], rotated(n)).then_inc(hi_ready, 1)

            def cut_high(n):
                first, end = batches[batch_of(n)]
                act.wait_ge(arrived[batch_of(n)], 16 * (end - first))
                raw_piece, h, _ = cut_of(pieces[n])
                act.copy(h, raw_piece).then_inc(cut_h, 1)

            for n in range(min(len(pieces), 2 * KC)):
                cut_high(n)
            for n in range(n_units):
                if 2 * KC + 2 * n < len(pieces):
                    cut_high(2 * KC + 2 * n)
                    cut_high(2 * KC + 2 * n + 1)
                act.wait_ge(proj_ready, n + 1)
                if n >= 2:
                    act.wait_ge(rot_ready, n - 1)
                    act.wait_ge(cos_ready, n - 1)
                act.copy(raw[:, n % 2, :], psum[:, n % 2, :]).then_inc(raw_ready, 1)
                if n >= 1:
                    high(n - 1)
            high(n_units - 1)
            for c in range(CH if layer == 1 else 0):
                act.wait_ge(v_ready, c + 1)
                act.copy(v_T[:, c, :], psum[:, 4 + c, :]).then_inc(v_copied, 1)
            for c in range(CH if layer == 1 else 0):
                act.wait_ge(v_ready, CH + c + 1)
                act.copy(v_tok[:, 4 * c:4 * c + 4, 0:P],
                         psum[:, 6 + c, :].rearrange("p (t f) -> p t f", f=P)).then_inc(v_copied, 1)

        @block.vector
        def _(dve):
            def low(n):
                dve.wait_ge(res_ready, n + 1)
                dve.tensor_copy(parts[:, n % 2, 1, :], t_cos[:, n % 2, :]).then_inc(mid_ready, 1)
                dve.wait_ge(mid_ready, n + 1)
                dve.tensor_tensor(parts[:, n % 2, 2, :], t_cos[:, n % 2, :], parts[:, n % 2, 1, :],
                                  ALU.subtract).then_inc(lo_ready, 1)

            def cut_low(n):
                dve.wait_ge(cut_h, n + 1)
                raw_piece, h, lo = cut_of(pieces[n])
                dve.tensor_tensor(lo, raw_piece, h.bitcast(F32), ALU.subtract).then_inc(cut_l, 1)

            for n in range(min(len(pieces), 2 * KC)):
                cut_low(n)
            for n, (kind, t, c) in enumerate(units):
                if c not in [u[2] for u in units[:n]]:
                    dve.wait_ge(tables[c], 32)
                if 2 * KC + 2 * n < len(pieces):
                    cut_low(2 * KC + 2 * n)
                    cut_low(2 * KC + 2 * n + 1)
                dve.wait_ge(raw_ready, n + 1)
                if n >= 2:
                    dve.wait_ge(lo_ready, n - 1)
                dve.tensor_tensor(t_cos[:, n % 2, :], raw[:, n % 2, :],
                                  cos[:, 512 * c:512 * c + 512], ALU.mult).then_inc(cos_ready, 1)
                dve.wait_ge(rot_ready, n + 1)
                if n >= 2:
                    dve.wait_ge(sum_ready, n - 1)
                dve.tensor_tensor(t_sin[:, n % 2, :], psum[:, 2 + n % 2, :],
                                  sin[:, 512 * c:512 * c + 512], ALU.mult).then_inc(sin_ready, 1)
                if n >= 1:
                    low(n - 1)
            low(n_units - 1)
            if layer == 0:
                dve.wait_ge(ad_loaded, 48)
                dve.wait_ge(ad_ready, 1)
                dve.tensor_tensor(
                    ad["ak_bd"].rearrange("p t (h a) -> p t h a", a=ADP),
                    psum[:, 6, 0:KC * ADP].rearrange("p (t o a) -> p t o a", o=1, a=ADP)
                    .broadcast_to([P, KC, HPT, ADP]),
                    ad["hm_k"].rearrange("p (t h a) -> p t h a", t=1, a=1)
                    .broadcast_to([P, KC, HPT, ADP]), ALU.mult).then_inc(ad_spread, 1)
                dve.tensor_tensor(
                    ad["av_bd"].rearrange("p t (h f) -> p t h f", f=D),
                    psum[0:AW, 7, :].rearrange("p (t h f) -> p t h f", h=HPT, f=D),
                    ad["hm_v"].rearrange("p (t h f) -> p t h f", t=1, f=1)
                    .broadcast_to([AW, KC, HPT, D]), ALU.mult).then_inc(ad_spread, 1)
                dve.wait_ge(ad_spread, 2)

        @block.gpsimd
        def _(pool):
            if layer == 0:
                pool.memset(m["v_grp"][:, :, :, :, D:VW], 1.0).then_inc(consts, 1)
                pool.memset(m["ones"], 1.0).then_inc(consts, 1)
                pool.memset(m["eps"], EPS).then_inc(consts, 1)
                pool.memset(m["maskb"][:, :], 0.0).then_inc(consts, 1)
                pool.memset(m["ident_b"][:, :], 0.0).then_inc(consts, 1)
                pool.wait_ge(consts, 5)
                pool.affine_select(out=m["maskb"][:, :], in_=m["maskb"][:, :], compare_op=ALU.is_ge,
                                   fill=-BIG, base=0, pattern=[[-1, P]], channel_multiplier=1)\
                    .then_inc(consts, 1)
                pool.affine_select(out=m["ident_b"][:, :], in_=m["ident_b"][:, :],
                                   compare_op=ALU.not_equal, fill=1.0, base=0, pattern=[[-1, P]],
                                   channel_multiplier=1).then_inc(consts, 1)
                pool.wait_ge(consts, 7)
            for n, (kind, t, c) in enumerate(units):
                s = n % 2
                pool.wait_ge(cos_ready, n + 1)
                pool.wait_ge(sin_ready, n + 1)
                if kind == "k" and n >= 2:
                    pool.wait_ge(hi_ready, n - 1)
                pool.tensor_tensor(rotated(n), t_cos[:, s, :], t_sin[:, s, :], ALU.add)\
                    .then_inc(sum_ready, 1)
                pool.wait_ge(sum_ready, n + 1)
                pool.wait_ge(hi_ready, n + 1)
                pool.tensor_tensor(t_cos[:, s, :], rotated(n), parts[:, s, 0, :], ALU.subtract)\
                    .then_inc(res_ready, 1)


def adapter(nc, d, ad, x_loaded, x_tok, v_tok, w_hl, x_hl, arena_o, ident, gating, psum, stacked,
            wo_raw, wo_hl):
    q_rot = view(arena_o, 0, [KC, T])
    HT = NT // 2
    prob = [view(arena_o, 16384 + 5120 * n, [HT, H * ADP]) for n in range(2)]
    pT = view(arena_o, 16384 + 10240, [2, KC, P], parts=AW)
    mx, y_ad = ad["mx"], ad["y"]
    order = [("scores", 0), ("V", 0), ("V", 1), ("scores", 1)]
    for n in range(NT):
        order.append(("T", n))
        if n < 3:
            order += [("V", 2 * n + 2), ("V", 2 * n + 3), ("y", n)]
        elif n > 3:
            order.append(("y", n - 1))
    order.append(("y", NT - 1))
    turns = [what for what in order if what[0] in "VT"]

    def heads(a):
        return a.rearrange("p t (h a) -> p t h a", a=ADP)

    with Phase(nc, "adapter") as ph:
        wo_cut = ph.sem("wo_cut")
        scores_ready, shifted, exped, prob_ready = (ph.sem(n) for n in
                                                    ("scores_ready", "shifted", "exped", "prob_ready"))
        turn_ready, turn_taken, y_ready, y_copied = (ph.sem(n) for n in
                                                     ("turn_ready", "turn_taken", "y_ready", "y_copied"))
        chain_s = ph.sem("chain")
        block = ph.block()

        @block.sync
        def _(sp):
            sp.wait_ge(turn_ready, turns.index(("V", NT - 1)) + 1)
            stacked.load_first(sp)
            sp.dma_start(x_tok[:, :, :], d["x"].rearrange("(t p) c -> p t c", p=P))\
                .then_inc(x_loaded, 16)

        @block.gpsimd
        def _(pool):
            cut_weights(pool, wo_cut, wo_raw, wo_hl)

        @block.tensor
        def _(pe):
            for what, n in order:
                if what == "scores":
                    if n:
                        pe.wait_ge(shifted, n)
                    for i in range(HT):
                        tok = P * (HT * n + i)
                        for t in range(KC):
                            last = pe.matmul(psum[:, i, AW * t:AW * t + AW], q_rot[:, t, tok:tok + P],
                                             ad["ak_bd"][:, t, :], start=True, stop=True)
                    last.then_inc(scores_ready, 1)
                    continue
                if what == "y":
                    pe.wait_ge(turn_taken, turns.index(("T", n)) + 1)
                    if n >= 2:
                        pe.wait_ge(y_copied, n - 1)
                    for t in range(KC):
                        last = pe.matmul(psum[:, 6 + n % 2, P * t:P * t + P], pT[:, n % 2, t, :],
                                         ad["av_bd"][:, t, :], start=True, stop=True)
                    last.then_inc(y_ready, 1)
                    continue
                turn = turns.index((what, n))
                if turn >= 2:
                    pe.wait_ge(turn_taken, turn - 1)
                bank = 4 + turn % 2
                if what == "V":
                    last = products(pe, psum[:, bank, :],
                                    [lambda k, a=a: a[:, k, P * n:P * n + P] for a in x_hl],
                                    [lambda k, a=a: a[:, k, 2 * C:3 * C] for a in w_hl])
                else:
                    pe.wait_ge(prob_ready, n // HT + 1)
                    for t in range(KC):
                        last = pe.transpose(psum[0:AW, bank, P * t:P * t + P],
                                            prob[n // HT][:, n % HT, AW * t:AW * t + AW], ident[:, :])
                last.then_inc(turn_ready, 1)

        @block.scalar
        def _(act):
            for what, n in order:
                if what == "y":
                    act.wait_ge(y_ready, n + 1)
                    act.copy(y_ad[:, n, :], psum[:, 6 + n % 2, :]).then_inc(y_copied, 1)
                if what in "VT":
                    turn = turns.index((what, n))
                    bank = 4 + turn % 2
                    act.wait_ge(turn_ready, turn + 1)
                    if what == "V":
                        act.copy(v_tok[:, n, :], psum[:, bank, :]).then_inc(turn_taken, 1)
                    else:
                        if n >= 2:
                            act.wait_ge(y_ready, n - 1)
                        act.copy(pT[:, n % 2, :, :], psum[0:AW, bank, :].rearrange(
                            "p (t q) -> p t q", q=P)).then_inc(turn_taken, 1)
                if what == "V" and n in (0, 2):
                    half = n // 2
                    act.wait_ge(shifted, half + 1)
                    act.activation(prob[half], prob[half], ACT.Exp, scale=float(C) ** -0.5)\
                        .then_inc(exped, 1)

        @block.vector
        def _(dve):
            link = Chain(dve, chain_s)
            for half in range(2):
                dve.wait_ge(scores_ready, half + 1)
                if half:
                    dve.wait_ge(prob_ready, half)
                ps = heads(psum[:, 0:HT, 0:H * ADP])
                wide = [P, HT, H, ADP]
                prob_h = heads(prob[half])
                link(dve.tensor_reduce(mx, ps, AX, ALU.max))
                dve.tensor_tensor(prob_h, ps, mx.rearrange("p t (h o) -> p t h o", o=1)
                                  .broadcast_to(wide), ALU.subtract).then_inc(shifted, 1)
                dve.wait_ge(exped, half + 1)
                dve.wait_ge(shifted, half + 1)
                link(dve.tensor_reduce(mx, prob_h, AX, ALU.add))
                link(dve.reciprocal(mx, mx))
                link(dve.tensor_scalar(mx, mx, gating, None, ALU.mult))
                dve.tensor_tensor(prob_h, prob_h, mx.rearrange("p t (h o) -> p t h o", o=1)
                                  .broadcast_to(wide), ALU.mult).then_inc(prob_ready, 1)


def cut_weights(pool, cut, raw, hl):
    for k in range(KC):
        pool.tensor_copy(hl[0][:, k, :], raw[:, k, :]).then_inc(cut, 1)
        pool.wait_ge(cut, 2 * k + 1)
        pool.tensor_tensor(hl[1][:, k, :], raw[:, k, :], hl[0][:, k, :].bitcast(F32), ALU.subtract)\
            .then_inc(cut, 1)


class StackedOperands:

    def __init__(self, ph, layer, arena_s, q_parts, k_parts):
        self.q_parts, self.k_parts = q_parts, k_parts
        self.kr = R if layer == 0 else 1
        self.q = view(arena_s, 0, [2, CH, R * 512], BF16)
        self.k_max = view(arena_s, 16384, [2, R * T], BF16)
        self.k_exp = view(arena_s, 32768, [2, R * T], BF16)
        self.q_loaded = [[ph.sem(f"q_loaded{s}{c}") for c in range(CH)] for s in range(2)]
        self.km_loaded = [ph.sem(f"km_loaded{s}") for s in range(2)]
        self.ke_loaded = [ph.sem(f"ke_loaded{s}") for s in range(2)]

    def wait_stored(self, engine):
        for sem, value in self.stored:
            engine.wait_ge(sem, value)

    def load_q(self, sp, g, s, c):
        for j0, n in ((0, 3), (3, 2), (5, 1)):
            sp.dma_start(
                self.q[D * j0:D * (j0 + n), s, c, :].rearrange("p (h t) -> p h t", h=R),
                self.q_parts[bass.ds(R * g, R), 0:n, :, 512 * c:512 * c + 512]
                .rearrange("h j d t -> j d h t")).then_inc(self.q_loaded[s][c], 16)

    def load_k(self, sp, g, s, dst, sem):
        for kp, (j0, n) in enumerate(((0, 3), (3, 2), (5, 1))):
            sp.dma_start(
                dst[D * j0:D * (j0 + n), s, 0:self.kr * T],
                self.k_parts[kp, :, bass.ds(self.kr * g, self.kr), :]
                .rearrange("(o d) h t -> o d (h t)", o=1).broadcast_to([n, D, self.kr * T]))\
                .then_inc(sem[s], 16)

    def load_first(self, queue):
        self.load_q(queue, 0, 0, 0)
        self.load_k(queue, 0, 0, self.k_max, self.km_loaded)


def attention(nc, layer, phase, stacked, arena_o, arena_p, v_tok, v_grp, ident_b, maskb, psum):
    kr, q_st, k_max, k_exp = stacked.kr, stacked.q, stacked.k_max, stacked.k_exp
    q_loaded, km_loaded, ke_loaded = stacked.q_loaded, stacked.km_loaded, stacked.ke_loaded
    scale = float(D) ** -0.5
    pr = view(arena_p, 0, [NP_RING, 2, 512])
    o_raw = view(arena_o, 0, [NG, T])

    with phase as ph, ExitStack() as own:
        mx = own.enter_context(nc.sbuf_tensor(f"mx{layer}", [P, CH, R * 4], F32))
        md = own.enter_context(nc.sbuf_tensor(f"md{layer}", [P, R * 4], F32))
        mst = own.enter_context(nc.sbuf_tensor(f"mst{layer}", [P, 2, NPART, R * 4], BF16))
        mT = own.enter_context(nc.sbuf_tensor(f"mT{layer}", [NPART * R * 4, 2, P], BF16))
        max_loaded = [[ph.sem(f"max_loaded{s}{c}") for c in range(CH)] for s in range(2)]
        qk_ready, qk_taken = ph.sem("qk_ready"), ph.sem("qk_taken")
        max_ready, dve_link = ph.sem("max_ready"), ph.sem("dve_link")
        scores_ready, exp_ready = ph.sem("scores_ready"), ph.sem("exp_ready")
        masked, pv_done = ph.sem("masked"), ph.sem("pv_done")
        o_copied, vg_ready, rows = ph.sem("o_copied"), ph.sem("vg_ready"), ph.sem("rows")
        passed_pe, passed_pool = ph.sem("passed_pe"), ph.sem("passed_pool")
        block = ph.block()

        n_tiles = [4 * (c + 1) for c in range(CH)]
        first_half = [0, 2 * n_tiles[0]]
        BG = 2 * sum(n_tiles)
        DG = 2 * 4 * CH
        assert BG % NP_RING == 0

        def pieces(c):
            out = []
            for i in range(4):
                for kc in range(c):
                    out += [(i, (r,), kc, 512) for r in range(R)]
                heads = [(0, 1), (2, 3)] if i < 2 else [(r,) for r in range(R)]
                out += [(i, hs, c, P * (i + 1)) for hs in heads]
            return out

        def entries(c, with_pieces=True, with_t=True):
            out = list(pieces(c)) if with_pieces else []
            if with_t:
                out.insert(min(2, len(out)), "T")
            return out

        RING = (4, 5, 7)
        first0 = len(entries(0, with_t=False))
        start = first0 + len(entries(1))
        n_entries = [len(entries(c)) for c in range(CH)]
        EG = sum(n_entries)
        assert EG % len(RING) == 0

        def first_entry(g, c):
            at = start + (n_entries[0] if c else 0)
            return EG * g + at, at

        def first_column(c, kt):
            return max(0, P * kt - 512 * c)

        def pairs(engine, body, first=None):
            if first:
                first()
            with engine.Fori(1 if first else 0, NG // 2 - 1) as pair:
                body(pair, False)
            body(NG // 2 - 1, True)

        @block.sync
        def _(sp):
            def load_max(entry, s, c):
                sp.wait_ge(qk_taken, entry + 1)
                for j in range(NPART):
                    sp.dma_start(q_st[KS + j:KS + j + 1, s, c, :].rearrange("p (i t) -> p i t", t=P),
                                 mT[R * 4 * j:R * 4 * (j + 1), c, :]).then_inc(max_loaded[s][c], 16)

            if layer == 1:
                stacked.wait_stored(sp)
            stacked.load_q(sp, 0, 0, 1)
            stacked.load_k(sp, 0, 0, k_exp, ke_loaded)
            stacked.load_q(sp, 1, 1, 0)
            stacked.load_k(sp, 1, 1, k_max, km_loaded)
            load_max(first0 + 2, 0, 0)

            def body(pair, last):
                for a in range(2):
                    g = 2 * pair + a
                    alone = last and a == 1
                    load_max(first_entry(g, 0)[0] + (0 if alone else 2), a, 1)
                    if alone:
                        break
                    sp.wait_ge(scores_ready, BG * g + 1)
                    stacked.load_q(sp, g + 1, 1 - a, 1)
                    stacked.load_k(sp, g + 1, 1 - a, k_exp, ke_loaded)
                    load_max(first_entry(g, 1)[0] + 2, 1 - a, 0)
                    if last:
                        continue
                    sp.wait_ge(scores_ready, BG * g + first_half[1])
                    stacked.load_q(sp, g + 2, a, 0)
                    sp.wait_ge(qk_ready, first_entry(g, 0)[0])
                    stacked.load_k(sp, g + 2, a, k_max, km_loaded)

            pairs(sp, body)

        @block.tensor
        def _(pe):
            def entry(number, at, what, pair, s, c, first):
                if at >= len(RING):
                    pe.wait_ge(qk_taken, number - len(RING) + 1)
                bank = RING[at % len(RING)]
                if what == "T":
                    tc = 1 - c
                    pe.wait_ge(max_ready, 2 * (2 * pair + s) + c)
                    pe.sem_inc(passed_pe, 1)
                    pe.transpose(psum[0:NPART * R * 4, bank, 0:P // 2].bitcast(BF16),
                                 mst[:, tc, :, :].rearrange("p j i -> p (j i)"), ident_b[:, :])\
                        .then_inc(qk_ready, 1)
                    return
                i, heads, kc, width = what
                if first:
                    pe.wait_ge(q_loaded[s][c], 48 * pair + 48)
                    if c == 0:
                        pe.wait_ge(km_loaded[s], 48 * pair + 48)
                for n, r in enumerate(heads):
                    kh = r if layer == 0 else 0
                    last = pe.matmul(psum[:, bank, width * n:width * n + width],
                                     q_st[0:KS, s, c, 512 * r + P * i:512 * r + P * i + P],
                                     k_max[0:KS, s, T * kh + 512 * kc:T * kh + 512 * kc + width],
                                     start=True, stop=kc < c)
                    if kc == c:
                        last = pe.matmul(psum[:, bank, width * (n + 1) - P:width * (n + 1)],
                                         ident_b[:, :], maskb[:, :], start=False, stop=True)
                last.then_inc(qk_ready, 1)

            def scores(pair, s, c, kt, hp):
                n = first_half[c] + 2 * kt + hp
                o = first_column(c, kt)
                if kt == 0 and hp == 0:
                    pe.wait_ge(max_loaded[s][c], 48 * pair + 48)
                    if c == 0:
                        pe.wait_ge(ke_loaded[s], 48 * pair + 48)
                if not (isinstance(pair, int) and 2 * pair + s == 0 and n < 2):
                    pe.wait_ge(exp_ready, BG * (2 * pair + s) + n - 1)
                for h in range(2):
                    r = 2 * hp + h
                    kh = r if layer == 0 else 0
                    last = pe.matmul(psum[:, 2 * hp + h, o:512],
                                     k_exp[0:KM, s, T * kh + P * kt:T * kh + P * kt + P],
                                     q_st[0:KM, s, c, 512 * r + o:512 * r + 512],
                                     start=True, stop=True)
                last.then_inc(scores_ready, 1)

            def values(pair, s, c, kt):
                g = 2 * pair + s
                n = first_half[c] + 2 * kt
                o = first_column(c, kt)
                if kt >= 4 * c:
                    pe.wait_ge(masked, DG * g + 2 * kt + 2)
                else:
                    pe.wait_ge(exp_ready, BG * g + n + 2)
                if kt == 0:
                    if c == 0:
                        pe.wait_ge(vg_ready, g + 1)
                    pe.wait_ge(o_copied, 2 * g + c + 1)
                for r in range(R):
                    last = pe.matmul(psum[32 * r:32 * r + VW, 6, o:512],
                                     v_grp[:, s, kt, r if layer == 0 else 0, :],
                                     pr[:, (n + r // 2) % NP_RING, r % 2, o:512],
                                     start=kt == 0, stop=kt == 4 * c + 3, tile_position=(0, 32 * r))
                last.then_inc(pv_done, 2)

            pe.sem_inc(pv_done, NP_RING)

            def step(pair, a, c, alone, todo, n_slots):
                issued = [0]

                def slot(n):
                    while issued[0] < min(len(todo), len(todo) * n // n_slots):
                        entry(*todo[issued[0]])
                        issued[0] += 1

                for kt in range(n_tiles[c]):
                    if kt + 1 < n_tiles[c]:
                        ahead = (pair, a, c, kt + 1)
                    elif c == 0:
                        ahead = (pair, a, 1, 0)
                    else:
                        ahead = None if alone else (*((pair, 1) if a == 0 else (pair + 1, 0)), 0, 0)
                    for hp in range(2):
                        if ahead:
                            scores(*ahead, hp)
                        slot(4 * kt + hp + 1)
                    slot(4 * kt + 3)
                    values(pair, a, c, kt)
                    slot(4 * kt + 4)

            def listed(number, at, todo, pair, s, c):
                return [(number + n, at + n, what, pair, s, c, n == 0) for n, what in enumerate(todo)]

            def body(pair, last):
                for a in range(2):
                    alone = last and a == 1
                    nxt = (pair, 1) if a == 0 else (pair + 1, 0)
                    for c in range(CH):
                        todo = listed(*first_entry(2 * pair + a, c),
                                      entries(c, not alone, not (alone and c == 1)), *nxt, c)
                        step(pair, a, c, alone, todo, 1 if alone else 4 * n_tiles[c])

            def first():
                for e in listed(0, 0, entries(0, with_t=False), 0, 0, 0):
                    entry(*e)
                todo = listed(first0, first0, entries(1), 0, 0, 1) \
                    + listed(*first_entry(0, 0), entries(0), 0, 1, 0) \
                    + listed(*first_entry(0, 1), entries(1), 0, 1, 1)
                for e in todo[:12]:
                    entry(*e)
                pe.wait_ge(rows, 2)
                scores(0, 0, 0, 0, 0)
                scores(0, 0, 0, 0, 1)
                to = n_entries[1] + 3
                step(0, 0, 0, False, todo[12:to], 12)
                step(0, 0, 1, False, todo[to:], 4 * n_tiles[1])
                for c in range(CH):
                    step(0, 1, c, False, listed(*first_entry(1, c), entries(c), 1, 0, c),
                         4 * n_tiles[c])

            pairs(pe, body, first)

        @block.scalar
        def _(act):
            def exp(g, c, b):
                n = first_half[c] + b
                o = first_column(c, b // 2)
                act.wait_ge(scores_ready, BG * g + n + 1)
                act.wait_ge(pv_done, BG * g + n + 1)
                act.activation(pr[:, n % NP_RING, :, o:512],
                               psum[:, 2 * (b % 2):2 * (b % 2) + 2, o:512],
                               ACT.Exp, scale=scale).then_inc(exp_ready, 1)

            def copy_o(g, c):
                act.wait_ge(pv_done, NP_RING + BG * g + first_half[c] + 2 * n_tiles[c])
                act.copy(o_raw[:, bass.ds(g, 1), 512 * c:512 * c + 512], psum[:, 6, :])\
                    .then_inc(o_copied, 1)

            act.sem_inc(o_copied, 1)
            if layer == 1:
                stacked.wait_stored(act)
            exp(0, 0, 0)
            exp(0, 0, 1)

            def body(pair, last):
                for a in range(2):
                    g = 2 * pair + a
                    for b in range(2, 2 * n_tiles[0]):
                        exp(g, 0, b)
                    for b in range(2):
                        exp(g, 1, b)
                    copy_o(g, 0)
                    for b in range(2, 2 * n_tiles[1]):
                        exp(g, 1, b)
                    if not (last and a == 1):
                        for b in range(2):
                            exp(g + 1, 0, b)
                    copy_o(g, 1)

            pairs(act, body)

        @block.vector
        def _(dve):
            LINKS = [3, 4]

            def unit(number, at, todo, G, c):
                for n, what in enumerate(todo):
                    bank = RING[(at + n) % len(RING)]
                    dve.wait_ge(qk_ready, number + n + 1)
                    if what == "T":
                        dve.tensor_copy(mT[:, 1 - c, :],
                                        psum[0:NPART * R * 4, bank, 0:P // 2].bitcast(BF16))\
                            .then_inc(qk_taken, 1)
                        continue
                    i, heads, kc, width = what
                    if n == 0 and not (isinstance(G, int) and G == 0 and c == 0):
                        dve.wait_ge(max_ready, 2 * G + c)
                    src = psum[:, bank, 0:width * len(heads)]
                    if len(heads) > 1:
                        src = src.rearrange("p (h k) -> p h k", h=len(heads))
                    col = 4 * heads[0] + i
                    dve.tensor_reduce(mx[:, kc, col:col + 4 * len(heads) - 3:4], src, AX, ALU.max)\
                        .then_inc(qk_taken, 1)
                if len(todo) == 1:
                    return
                base = sum(LINKS) * G + (LINKS[0] if c else 0)
                dve.wait_ge(qk_taken, number + len(todo))
                if c == 1:
                    dve.tensor_tensor(mx[:, 0, :], mx[:, 0, :], mx[:, 1, :], ALU.max)\
                        .then_inc(dve_link, 1)
                    dve.wait_ge(dve_link, base + 1)
                    base = base + 1
                dve.tensor_copy(mst[:, c, 0, :], mx[:, 0, :]).then_inc(dve_link, 1)
                dve.wait_ge(dve_link, base + 1)
                dve.tensor_tensor(md[:, :], mx[:, 0, :], mst[:, c, 0, :], ALU.subtract)\
                    .then_inc(dve_link, 1)
                dve.wait_ge(dve_link, base + 2)
                dve.tensor_copy(mst[:, c, 1, :], md[:, :]).then_inc(dve_link, 1)
                dve.wait_ge(dve_link, base + 3)
                dve.tensor_tensor(mst[:, c, 2, :], md[:, :], mst[:, c, 1, :], ALU.subtract)\
                    .then_inc(max_ready, 1)

            unit(0, 0, entries(0, with_t=False), 0, 0)
            unit(first0, first0, entries(1), 0, 1)

            def body(pair, last):
                for a in range(2):
                    alone = last and a == 1
                    for c in range(CH):
                        if not (alone and c == 1):
                            unit(*first_entry(2 * pair + a, c), entries(c, not alone),
                                 2 * pair + a + 1, c)

            pairs(dve, body)

        @block.gpsimd
        def _(pool):
            pool.memset(k_exp[KS:KM, 0, :], -1.0).then_inc(rows, 1)
            pool.memset(k_exp[KS:KM, 1, :], -1.0).then_inc(rows, 1)
            vgw = kr * D

            def load_v(g, s):
                pool.wait_ge(pv_done, NP_RING + BG * g - BG)
                pool.tensor_copy(v_grp[:, s, :, 0:kr, 0:D],
                                 v_tok[:, :, bass.ds(vgw * g, vgw)]
                                 .rearrange("p t (r f) -> p t r f", f=D)).then_inc(vg_ready, 1)

            pool.wait_ge(rows, 2)
            pool.tensor_copy(v_grp[:, 0, :, 0:kr, 0:D],
                             v_tok[:, :, 0:vgw].rearrange("p t (r f) -> p t r f", f=D))\
                .then_inc(vg_ready, 1)

            def body(pair, last):
                for a in range(2):
                    g = 2 * pair + a
                    for c in range(CH):
                        for b in range(8 * c, 8 * c + 8):
                            n = first_half[c] + b
                            o = first_column(c, b // 2)
                            pool.wait_ge(exp_ready, BG * g + n + 1)
                            pool.sem_inc(passed_pool, 1)
                            tri = pr[:, n % NP_RING, :, o:o + P]
                            pool.affine_select(out=tri, in_=tri, compare_op=ALU.is_ge, fill=0.0,
                                               base=0, pattern=[[0, 2], [1, P]],
                                               channel_multiplier=-1).then_inc(masked, 1)
                        if c == 0 and not (last and a == 1):
                            load_v(g + 1, 1 - a)

            pairs(pool, body)


def norm_stats(dve, link, src, stats):
    link(dve.bn_stats(stats[:, 0:6], src))
    return dve.bn_aggr(stats[:, 6:8], stats[:, 0:6])


def norm_root(act, stats, eps):
    return act.activation(stats[:, 8:9], stats[:, 7:8], ACT.Sqrt, bias=eps)


def norm_apply(dve, link, dst, src, stats):
    link(dve.reciprocal(stats[:, 8:9], stats[:, 8:9]))
    return dve.tensor_scalar(dst, src, stats[:, 6:7], stats[:, 8:9], ALU.subtract, ALU.mult)


def finish_attention(nc, layer, d, x_loaded, x_tok, xT, y_ad, arena_o, arena_s, w_next, wo_next,
                     w_out, yT_hl, ident, eps, psum, x_hl, ff):
    o_raw = view(arena_o, 0, [NG, T])
    y = view(arena_s, 0, [2, C])
    h = view(arena_s, 8192, [2, C])
    rec = view(arena_s, 12288, [H])
    stats = view(arena_s, 12416, [2, 9])
    with Phase(nc, f"fin{layer}") as ph:
        chain_s, next_loaded = ph.sem("chain"), ph.sem("next_loaded")
        oT_ready, y_ready, yT_ready, yT_copied = (ph.sem(n) for n in
                                                  ("oT_ready", "y_ready", "yT_ready", "yT_copied"))
        z_ready, x_ready, xT_ready, xT_copied = (ph.sem(n) for n in
                                                 ("z_ready", "x_ready", "xT_ready", "xT_copied"))
        xT_cut, yT_cut = ph.sem("xT_cut"), ph.sem("yT_cut")
        z_added, var_ready, dev_ready = ph.sem("z_added"), ph.sem("var_ready"), ph.sem("dev_ready")
        block = ph.block()

        @block.sync
        def _(sp):
            if layer == 1:
                ff.prefetch(sp, d)
            if layer == 0:
                sp.dma_start(w_next, d["w1"].rearrange("(k p) n -> p k n", p=P)).then_inc(next_loaded, 16)
                sp.dma_start(wo_next, d["wo1"].rearrange("(k p) n -> p k n", p=P))\
                    .then_inc(next_loaded, 16)
                sp.wait_ge(next_loaded, 32)

        if layer == 1:
            @block.gpsimd
            def _(pool):
                for i in range(2):
                    ff.cut_high(pool, pool.tensor_copy, i)
                    ff.cut_low(pool, i)

        @block.tensor
        def _(pe):
            for s in range(NT + 4):
                if s < NT:
                    t = s
                    if t >= 2:
                        pe.wait_ge(y_ready, t - 1)
                    for g in range(NG):
                        last = pe.transpose(psum[:, 2 * (t % 2) + g // 4, P * (g % 4):P * (g % 4) + P],
                                            o_raw[:, g, P * t:P * t + P], ident[:, :])
                    last.then_inc(oT_ready, 1)
                if 0 <= s - 1 < NT:
                    t = s - 1
                    pe.wait_ge(y_ready, t + 1)
                    if t >= 1:
                        pe.wait_ge(yT_cut, t)
                    for k in range(KC):
                        last = pe.transpose(psum[:, 4, P * k:P * k + P],
                                            y[:, t % 2, P * k:P * k + P], ident[:, :])
                    last.then_inc(yT_ready, 1)
                if 0 <= s - 2 < NT:
                    t = s - 2
                    pe.wait_ge(yT_cut, t + 1)
                    if t >= 1:
                        pe.wait_ge(z_added, t)
                    for k in range(KC):
                        for n, (i, j) in enumerate(((0, 0), (0, 1), (1, 0))):
                            last = pe.matmul(psum[:, 5, :], yT_hl[i][:, t % 2, k, :], w_out[j][:, k, :],
                                             start=k + n == 0, stop=k == KC - 1 and n == 2)
                    last.then_inc(z_ready, 1)
                if 0 <= s - 4 < NT:
                    t = s - 4
                    pe.wait_ge(x_ready, t + 1)
                    if t >= 2:
                        pe.wait_ge(xT_copied if layer == 0 else xT_cut, t - 1)
                    for k in range(KC):
                        last = pe.transpose(psum[:, 6 + t % 2, P * k:P * k + P],
                                            x_tok[:, t, P * k:P * k + P], ident[:, :])
                    last.then_inc(xT_ready, 1)

        @block.scalar
        def _(act):
            for s in range(NT + 4):
                if 0 <= s - 1 < NT:
                    t = s - 1
                    act.wait_ge(yT_ready, t + 1)
                    if t >= 2:
                        act.wait_ge(z_ready, t - 1)
                    act.copy(yT_hl[0][:, t % 2, :, :], psum[:, 4, :].rearrange("p (k q) -> p k q", q=P))\
                        .then_inc(yT_copied, 1)
                if 0 <= s - 2 < NT:
                    t = s - 2
                    act.wait_ge(var_ready, t + 1)
                    norm_root(act, stats[:, t % 2, :], eps).then_inc(dev_ready, 1)
                if 0 <= s - 4 < NT:
                    t = s - 4
                    act.wait_ge(xT_ready, t + 1)
                    dst = xT if layer == 0 else x_hl[0]
                    act.copy(dst[:, :, P * t:P * t + P], psum[:, 6 + t % 2, :].rearrange("p (k q) -> p k q", q=P))\
                        .then_inc(xT_copied, 1)
                    if layer == 1 and t in (3, 5):
                        ff.weigh(act, (t - 3) // 2)

        @block.vector
        def _(dve):
            link = Chain(dve, chain_s)
            for s in range(NT + 5):
                if s < NT:
                    t = s
                    dve.wait_ge(oT_ready, t + 1)
                    if t >= 2:
                        dve.wait_ge(yT_ready, t - 1)
                    o = psum[:, 2 * (t % 2):2 * (t % 2) + 2, :].rearrange("p b (h f) -> p (b h) f", f=VW)
                    if t >= 1:
                        dve.wait_ge(y_ready, t)
                    link(dve.reciprocal(rec, o[:, :, D]))
                    out_y = y[:, t % 2, :].rearrange("p (h f) -> p h f", f=D)
                    mul = dve.tensor_tensor(out_y, o[:, :, 0:D], rec.rearrange("p (h o) -> p h o", o=1)
                                            .broadcast_to([P, H, D]), ALU.mult)
                    if layer == 0:
                        link(mul)
                        mul = dve.tensor_tensor(y[:, t % 2, :], y[:, t % 2, :], y_ad[:, t, :], ALU.add)
                    mul.then_inc(y_ready, 1)
                if 0 <= s - 1 < NT:
                    t = s - 1
                    dve.wait_ge(yT_copied, t + 1)
                    if t >= 2:
                        dve.wait_ge(z_ready, t - 1)
                    dve.tensor_tensor(yT_hl[1][:, t % 2, :, :],
                                      psum[:, 4, :].rearrange("p (k q) -> p k q", q=P),
                                      yT_hl[0][:, t % 2, :, :].bitcast(F32), ALU.subtract)\
                        .then_inc(yT_cut, 1)
                if 0 <= s - 2 < NT:
                    t = s - 2
                    dve.wait_ge(z_ready, t + 1)
                    dve.wait_ge(y_ready, t + 1)
                    if t >= 2:
                        dve.wait_ge(x_ready, t - 1)
                    if layer == 0 and t == 0:
                        dve.wait_ge(x_loaded, 16)
                    dve.tensor_tensor(h[:, t % 2, :], psum[:, 5, :], x_tok[:, t, :], ALU.add).then_inc(z_added, 1)
                    dve.wait_ge(z_added, t + 1)
                    norm_stats(dve, link, h[:, t % 2, :], stats[:, t % 2, :]).then_inc(var_ready, 1)
                if 0 <= s - 3 < NT:
                    t = s - 3
                    dve.wait_ge(dev_ready, t + 1)
                    norm_apply(dve, link, x_tok[:, t, :], h[:, t % 2, :], stats[:, t % 2, :])\
                        .then_inc(x_ready, 1)
                if layer == 1 and 0 <= s - 5 < NT:
                    t = s - 5
                    dve.wait_ge(xT_copied, t + 1)
                    dve.tensor_tensor(x_hl[1][:, :, P * t:P * t + P],
                                      psum[:, 6 + t % 2, :].rearrange("p (k q) -> p k q", q=P),
                                      x_hl[0][:, :, P * t:P * t + P].bitcast(F32), ALU.subtract)\
                        .then_inc(xT_cut, 1)


def lookup(nc, x_tok, xT, arena_o, arena_s, arena_p, w_raw, w_hl, x_hl, ident, ones, eps, psum,
           wq, wr, akey, av, wvd, wvu,
           wu1, wu2, bu1, logrel, bu2, gate_w1, gate_bias, wo_raw, wo_hl):
    hid = view(arena_o, 0, [T])
    query = view(arena_o, 4096, [T], parts=BOT)
    rq = view(arena_o, 8192, [T], parts=RDIM)
    rs = view(arena_o, 12288, [NT, NSLOT])
    at = view(arena_o, 16384, [NT, NSLOT])
    rest = view(arena_o, 20480, [NT, NSLOT])
    wT = view(arena_o, 24576, [T])
    aux = view(arena_o, 28672, [2, C])
    rk = view(arena_s, 0, [NSLOT], parts=RDIM)
    dn = view(arena_s, 512, [NSLOT], parts=VB)
    vals = view(arena_s, 1024, [C])
    top = view(arena_s, 3072, [NT, 8])
    n8 = [view(arena_s, 3328 + 32 * n, [NT]) for n in range(8)]
    mxs, sums, _, lv, learned, gate, tmp, tmp2 = n8
    lvs = view(arena_s, 3584, [1])
    stats2 = view(arena_s, 3712, [2, 9])
    row_stats = view(arena_p, 4096, [NT, 6])
    var2 = view(arena_p, 4288, [NT, 2])
    x_T = view(arena_p, 0, [2, KC, P])
    h = view(arena_s, 4096, [2, C])
    last_exp = float(BOT) ** -0.5
    with Phase(nc, "lookup") as ph:
        pre, pre_copied = ph.sem("pre"), ph.sem("pre_copied")
        q_ready, q_copied, s_ready, s_read = (ph.sem(n) for n in
                                              ("q_ready", "q_copied", "s_ready", "s_read"))
        hid_ready, hid_copied, mean_read = (ph.sem(n) for n in
                                            ("hid_ready", "hid_copied", "mean_read"))
        shifted, exped, wT_ready, wT_copied = (ph.sem(n) for n in
                                               ("shifted", "exped", "wT_ready", "wT_copied"))
        lv_done, lvs_ready, mean_ready, lin_ready = (ph.sem(n) for n in
                                                     ("lv_done", "lvs_ready", "mean_ready", "lin_ready"))
        sig_in, sig_out, gate_ready, var_ready = (ph.sem(n) for n in
                                                  ("sig_in", "sig_out", "gate_ready", "var_ready"))
        z_ready, aux_ready, x_ready, xT_ready, xT_copied = (ph.sem(n) for n in
                                                            ("z_ready", "aux_ready", "x_ready", "xT_ready", "xT_copied"))
        chain_s, g_in, g_out = ph.sem("chain"), ph.sem("g_in"), ph.sem("g_out")
        row_var, dev_ready = ph.sem("row_var"), ph.sem("dev_ready")
        xT_cut, w_cut, wo_cut = ph.sem("xT_cut"), ph.sem("w_cut"), ph.sem("wo_cut")
        block = ph.block()

        @block.gpsimd
        def _(pool):
            cut_weights(pool, w_cut, w_raw, w_hl)
            cut_weights(pool, wo_cut, wo_raw, wo_hl)
            for t in range(NT):
                pool.wait_ge(xT_copied, 2 * t + 2)
                pool.tensor_tensor(x_hl[1][:, :, P * t:P * t + P], x_T[:, t % 2, :, :],
                                   x_hl[0][:, :, P * t:P * t + P].bitcast(F32), ALU.subtract)\
                    .then_inc(xT_cut, 1)

        @block.tensor
        def _(pe):
            pe.matmul(psum[0:RDIM, 4, 0:NSLOT], wr, akey, start=True, stop=True)
            for k in range(KC):
                last = pe.matmul(psum[0:VB, 5, 0:NSLOT], wvd[:, k, :], av[:, k, :],
                                 start=k == 0, stop=k == KC - 1)
            last.then_inc(pre, 1)
            for c in range(CH):
                for k in range(KC):
                    last = pe.matmul(psum[0:BOT, 6 + c, :], wq[:, k, :], xT[:, k, 512 * c:512 * c + 512],
                                     start=k == 0, stop=k == KC - 1)
                last.then_inc(q_ready, 1)
            pe.wait_ge(pre_copied, 2)
            for c in range(CH):
                pe.wait_ge(q_copied, c + 1)
                last = pe.matmul(psum[0:RDIM, 4 + c, :], wr, query[:, 512 * c:512 * c + 512],
                                 start=True, stop=True)
            last.then_inc(q_ready, 1)
            pe.wait_ge(lvs_ready, 1)
            pe.matmul(psum[:, 6, 0:1], ones, lvs, start=True, stop=True).then_inc(mean_ready, 1)
            pe.wait_ge(q_copied, 3)
            for t in range(NT):
                pe.matmul(psum[:, t // 4, P * (t % 4):P * (t % 4) + NSLOT], rq[:, P * t:P * t + P], rk,
                          start=True, stop=True)
                last = pe.matmul(psum[:, 2 + t // 4, P * (t % 4):P * (t % 4) + NSLOT],
                                 query[:, P * t:P * t + P], akey, start=True, stop=True)
            last.then_inc(s_ready, 1)
            for c in range(CH):
                for k in range(KC):
                    last = pe.matmul(psum[:, 4 + c, :], wu1[:, k, :], xT[:, k, 512 * c:512 * c + 512],
                                     start=k == 0, stop=k == KC - 1)
                last.then_inc(hid_ready, 1)
            pe.matmul(psum[:, 7, :], dn, wvu, start=True, stop=True).then_inc(pre, 1)
            pe.wait_ge(mean_read, 1)
            pe.wait_ge(hid_copied, CH)
            for t in range(NT):
                last = pe.matmul(psum[:, 6, t:t + 1], hid[:, P * t:P * t + P], wu2, start=True, stop=True)
            last.then_inc(lin_ready, 1)
            pe.wait_ge(pre_copied, 3)
            pe.wait_ge(exped, 1)
            pe.wait_ge(s_read, 1)
            for t in range(NT):
                last = pe.transpose(psum[:, t // 4, P * (t % 4):P * (t % 4) + P], at[:, t, :], ident[:, :])
            last.then_inc(wT_ready, 1)
            pe.wait_ge(wT_copied, 1)
            for s in range(NT + 3):
                if s < NT:
                    t = s
                    if t >= 2:
                        pe.wait_ge(aux_ready, t - 1)
                    pe.matmul(psum[:, 2 + t % 2, :], wT[:, P * t:P * t + P], vals, start=True, stop=True)\
                        .then_inc(z_ready, 1)
                if s >= 3:
                    t = s - 3
                    pe.wait_ge(x_ready, t + 1)
                    if t >= 2:
                        pe.wait_ge(xT_copied, 2 * t - 2)
                    for k in range(KC):
                        last = pe.transpose(psum[:, 6 + t % 2, P * k:P * k + P],
                                            x_tok[:, t, P * k:P * k + P], ident[:, :])
                    last.then_inc(xT_ready, 1)

        @block.scalar
        def _(act):
            act.wait_ge(pre, 1)
            act.copy(rk, psum[0:RDIM, 4, 0:NSLOT]).then_inc(pre_copied, 1)
            act.copy(dn, psum[0:VB, 5, 0:NSLOT]).then_inc(pre_copied, 1)
            for c in range(CH):
                act.wait_ge(q_ready, c + 1)
                act.copy(query[:, 512 * c:512 * c + 512], psum[0:BOT, 6 + c, :]).then_inc(q_copied, 1)
            act.wait_ge(var_ready, 1)
            act.activation(lv, var2[:, :, 1], ACT.Ln, bias=1.0).then_inc(lv_done, 1)
            act.wait_ge(q_ready, 3)
            act.copy(rq.rearrange("p (c t) -> p c t", c=CH), psum[0:RDIM, 4:6, :]).then_inc(q_copied, 1)
            for c in range(CH):
                act.wait_ge(hid_ready, c + 1)
                act.activation(hid[:, 512 * c:512 * c + 512], psum[:, 4 + c, :], ACT.Gelu_apprx_tanh,
                               bias=bu1[:, :]).then_inc(hid_copied, 1)
            act.wait_ge(pre, 2)
            act.copy(vals, psum[:, 7, :]).then_inc(pre_copied, 1)
            act.wait_ge(shifted, 1)
            act.activation(at, rest, ACT.Exp).then_inc(exped, 1)
            act.wait_ge(sig_in, 1)
            act.activation(learned, tmp, ACT.Sigmoid).then_inc(sig_out, 1)
            act.wait_ge(wT_ready, 1)
            act.copy(wT.rearrange("p (c t) -> p c t", c=CH), psum[:, 0:2, :]).then_inc(wT_copied, 1)
            act.wait_ge(g_in, 1)
            act.activation(tmp, gate, ACT.Sigmoid).then_inc(g_out, 1)
            act.wait_ge(gate_ready, 1)
            for s in range(NT + 3):
                if s < NT:
                    t = s
                    act.wait_ge(z_ready, t + 1)
                    if t >= 2:
                        act.wait_ge(row_var, t - 1)
                    act.activation(aux[:, t % 2, :], psum[:, 2 + t % 2, :], ACT.Copy,
                                   scale=gate[:, t:t + 1]).then_inc(aux_ready, 1)
                if 1 <= s <= NT:
                    t = s - 1
                    act.wait_ge(row_var, t + 1)
                    norm_root(act, stats2[:, t % 2, :], eps).then_inc(dev_ready, 1)
                if s >= 3:
                    t = s - 3
                    act.wait_ge(xT_ready, t + 1)
                    src = psum[:, 6 + t % 2, :].rearrange("p (k q) -> p k q", q=P)
                    if t >= 2:
                        act.wait_ge(xT_cut, t - 1)
                    act.copy(x_T[:, t % 2, :, :], src).then_inc(xT_copied, 1)
                    act.copy(x_hl[0][:, :, P * t:P * t + P], src).then_inc(xT_copied, 1)

        @block.vector
        def _(dve):
            link = Chain(dve, chain_s)
            for t in range(NT):
                link.later(dve.bn_stats(row_stats[:, t, :], x_tok[:, t, :]))
            link.all()
            for t in range(NT):
                link.later(dve.bn_aggr(var2[:, t, :], row_stats[:, t, :]))
            link.all()
            dve.sem_inc(var_ready, 1)
            dve.wait_ge(lv_done, 1)
            dve.tensor_reduce(lvs, lv, AX, ALU.add).then_inc(lvs_ready, 1)
            dve.wait_ge(mean_ready, 1)
            dve.tensor_scalar(lvs, psum[:, 6, 0:1], 1.0 / T, 1e-6, ALU.mult, ALU.add)\
                .then_inc(mean_read, 1)
            dve.wait_ge(mean_read, 1)
            link(dve.reciprocal(lvs, lvs))
            link(dve.tensor_scalar(tmp2, lv, lvs, 0.5, ALU.mult, ALU.mult))
            dve.wait_ge(s_ready, 1)
            lr = logrel.rearrange("p (o n) -> p o n", o=1).broadcast_to([P, NT, NSLOT])
            ps = [psum[:, 2 * n:2 * n + 2, :].rearrange("p b (t n) -> p (b t) n", n=NSLOT) for n in range(2)]
            link(dve.scalar_tensor_tensor(out=rs, in0=ps[0], scalar=float(1 / np.sqrt(RDIM)), in1=lr,
                                          op0=ALU.mult, op1=ALU.add))
            dve.scalar_tensor_tensor(out=at, in0=ps[1], scalar=last_exp, in1=lr,
                                     op0=ALU.mult, op1=ALU.add).then_inc(s_read, 1)
            dve.wait_ge(s_read, 1)
            for t in range(NT):
                link.later(dve.max(top[:, t, :], rs[:, t, :]))
            link.all()
            for t in range(NT):
                link.later(dve.match_replace(out=rest[:, t, :], in_to_replace=top[:, t, :],
                                             in_values=rs[:, t, :], imm_value=-3e38))
            link.all()
            link(dve.tensor_tensor(rs, rs, rest, ALU.is_equal))
            link(dve.scalar_tensor_tensor(out=at, in0=rs, scalar=-BIG, in1=at,
                                          op0=ALU.mult, op1=ALU.add))
            link(dve.tensor_reduce(mxs, at, AX, ALU.max))
            dve.tensor_tensor(rest, at, mxs.rearrange("p (t o) -> p t o", o=1)
                              .broadcast_to([P, NT, NSLOT]), ALU.subtract).then_inc(shifted, 1)
            dve.wait_ge(lin_ready, 1)
            dve.tensor_scalar(tmp, psum[:, 6, 0:NT], bu2, None, ALU.add).then_inc(sig_in, 1)
            dve.wait_ge(exped, 1)
            link(dve.tensor_reduce(sums, at, AX, ALU.add))
            link(dve.reciprocal(sums, sums))
            dve.wait_ge(sig_out, 1)
            link(dve.scalar_tensor_tensor(out=gate, in0=learned, scalar=2.5, in1=tmp2,
                                          op0=ALU.mult, op1=ALU.add))
            link(dve.tensor_scalar(gate, gate, 0.0, 5.0, ALU.max, ALU.min))
            link(dve.tensor_scalar(gate, gate, 0.5, 1.0 / 1.5, ALU.subtract, ALU.mult))
            link(dve.tensor_scalar(gate, gate, 0.0, 1.0, ALU.max, ALU.min))
            dve.tensor_scalar(gate, gate, gate_w1, gate_bias, ALU.mult, ALU.add).then_inc(g_in, 1)
            dve.wait_ge(g_out, 1)
            link(dve.tensor_scalar(learned, tmp, 0.05, None, ALU.is_ge))
            link(dve.tensor_tensor(gate, tmp, learned, ALU.mult))
            dve.tensor_tensor(gate, gate, sums, ALU.mult).then_inc(gate_ready, 1)
            for s in range(NT + 1):
                if s < NT:
                    t = s
                    dve.wait_ge(aux_ready, t + 1)
                    if t >= 2:
                        dve.wait_ge(x_ready, t - 1)
                    link(dve.scalar_tensor_tensor(out=h[:, t % 2, :], in0=x_tok[:, t, :], scalar=2.0,
                                                  in1=aux[:, t % 2, :], op0=ALU.mult, op1=ALU.add))
                    norm_stats(dve, link, h[:, t % 2, :], stats2[:, t % 2, :]).then_inc(row_var, 1)
                if 1 <= s <= NT:
                    t = s - 1
                    dve.wait_ge(dev_ready, t + 1)
                    norm_apply(dve, link, x_tok[:, t, :], h[:, t % 2, :], stats2[:, t % 2, :])\
                        .then_inc(x_ready, 1)


class SwigluArrays:

    def __init__(self, nc, at):
        self.nc = nc
        self.raw = at("ff_raw", M_RAW, [P, 2, 2 * KC * P])
        self.w_hl = [at(f"ff_w{n}", M_WIN + 8192 * n, [P, 2, 2 * KC * P], F32R) for n in range(2)]
        self.g_hl = [at(f"ff_g{n}", m, [P, NI, T], F32R) for n, m in enumerate((M_GH, M_GL))]
        self.wd_raw = at("ff_wd_raw", M_WD, [P, NI, C])
        self.wd_hl = [at(f"ff_wd{n}", M_XT + NI * C * 4 * n, [P, NI, C], F32R) for n in range(2)]
        self.silu = at("ff_silu", M_TMP, [P, 2, 512])
        self.h = at("ff_h", M_ROWS, [P, 2, C])
        self.prod = at("ff_prod", M_TMP + 4096, [P, 2, 512])
        self.stats = at("ff_stats", M_ROWS + 4096, [P, 2, 9])
        self.w_high, self.w_low = nc.alloc_semaphore("ff_w_high"), nc.alloc_semaphore("ff_w_low")
        self.arrived = [nc.alloc_semaphore(f"ff_arrived{n}") for n in range(2)]
        self.wd_arrived = nc.alloc_semaphore("ff_wd_arrived")
        self.in_weighed = nc.alloc_semaphore("ff_in_weighed")
        self.low_in = at("ff_low_in", M_ROWS + 4224, [P, NI])
        self.low_out = at("ff_low_out", M_ROWS + 4288, [P, NI])
        self.low_all = at("ff_low_all", M_ROWS + 4352, [P, 1])
        self.flags = at("ff_flags", M_ROWS + 4384, [1, NI + 1])
        self.probe = at("ff_probe", M_TMP + 8192, [P, 512], F32R)
        self.probe_low = [at(f"ff_probe_low{n}", m, [P, 512])
                          for n, m in enumerate((M_TMP + 10240, M_ROWS + 4608))]

    def load_in(self, sp, d, i):
        sp.dma_start(self.raw[:, i % 2, :], d["w_in"][i]).then_inc(self.arrived[i % 2], 16)

    def prefetch(self, sp, d):
        self.load_in(sp, d, 0)
        self.load_in(sp, d, 1)

    def cut_high(self, engine, copy, i):
        engine.wait_ge(self.arrived[i % 2], 16 * (i // 2 + 1))
        copy(self.w_hl[0][:, i % 2, :], self.raw[:, i % 2, :]).then_inc(self.w_high, 1)

    def cut_low(self, engine, i):
        engine.wait_ge(self.w_high, i + 1)
        engine.tensor_tensor(self.w_hl[1][:, i % 2, :], self.raw[:, i % 2, :],
                           self.w_hl[0][:, i % 2, :].bitcast(F32), ALU.subtract)\
            .then_inc(self.w_low, 1)

    def weigh(self, act, i):
        act.wait_ge(self.w_low, i + 1)
        if i:
            act.wait_ge(self.in_weighed, i)
        act.activation(self.h[:, :, :].rearrange("p b n -> p (b n)"),
                       self.w_hl[1][:, i % 2, :].bitcast(F32), ACT.Abs,
                       accum_out=self.low_in[:, i:i + 1]).then_inc(self.in_weighed, 1)

    def load_out(self, sp, d):
        full = P * (NI - 1)
        sp.dma_start(self.wd_raw[:, 0:NI - 1, :], d["w_down"][0:full, :]
                     .rearrange("(i p) n -> p i n", p=P)).then_inc(self.wd_arrived, 16)
        sp.dma_start(self.wd_raw[0:INTER - full, NI - 1, :], d["w_down"][full:, :])\
            .then_inc(self.wd_arrived, 16)


def swiglu(nc, d, x_tok, x_hl, ff, s_gate, s_up, s_down, ones, eps, psum, out):
    rows = [min(P, INTER - P * i) for i in range(NI)]
    with Phase(nc, "swiglu") as ph:
        chain_s, stored = ph.sem("chain"), ph.sem("stored")
        w_low = ff.w_low
        gu_ready, silu_ready, prod_ready = ph.sem("gu_ready"), ph.sem("silu_ready"), ph.sem("prod_ready")
        g_high, g_low = ph.sem("g_high"), ph.sem("g_low")
        wd_high, wd_low = ph.sem("wd_high"), ph.sem("wd_low")
        z_ready, z_scaled, x_ready = ph.sem("z_ready"), ph.sem("z_scaled"), ph.sem("x_ready")
        var_ready, dev_ready = ph.sem("var_ready"), ph.sem("dev_ready")
        in_weighed, out_weighed, all_weighed = ff.in_weighed, ph.sem("out_weighed"), ph.sem("all_weighed")
        summed, flagged, probed = ph.sem("summed"), ph.sem("flagged"), ph.sem("probed")
        cleared = ph.sem("cleared")
        FIRST = CH * NI - NI - 3
        block = ph.block()

        @block.sync
        def _(sp):
            for i in range(2, NI):
                sp.wait_ge(w_low, i - 1)
                ff.load_in(sp, d, i)
                if i == 3:
                    ff.load_out(sp, d)
            for t in range(NT):
                sp.wait_ge(x_ready, t + 1)
                sp.dma_start(out[P * t:P * t + P, :], x_tok[:, t, :]).then_inc(stored, 16)
            sp.wait_ge(stored, 16 * NT)

        @block.tensor
        def _(pe):
            flag = pe.alloc_register("has_low_parts")

            def sum_flag(i):
                if i < NI:
                    pe.wait_ge(in_weighed, i + 1)
                else:
                    pe.wait_ge(all_weighed, 1)
                if i:
                    pe.wait_ge(flagged, i)
                pe.matmul(psum[0:1, 6, 0:1], ff.low_in[:, i:i + 1] if i < NI else ff.low_all[:, :],
                          ones[:, 0:1], start=True, stop=True).then_inc(summed, 1)

            sum_flag(0)
            for i in range(NI):
                pe.wait_ge(w_low, i + 1)
                pe.wait_ge(flagged, i + 1)
                pe.reg_load(flag, ff.flags[0:1, i:i + 1].bitcast(mybir.dt.int32))
                for c in range(CH):
                    n = CH * i + c
                    if n >= 3:
                        pe.wait_ge(prod_ready, n - 2)

                    def products(a, b, ks):
                        for u in range(2):
                            for k in ks:
                                col = P * (KC * u + k)
                                last = pe.matmul(psum[0:rows[i], 2 * (n % 3) + u, :],
                                                 ff.w_hl[a][:, i % 2, col:col + rows[i]],
                                                 x_hl[b][:, k, 512 * c:512 * c + 512],
                                                 start=(a, b, k) == (0, 0, 0),
                                                 stop=(a, b, k) == (0, 1, KC - 1))
                        return last

                    products(0, 0, range(KC))
                    with pe.If(flag):
                        products(1, 0, range(KC))
                    if c == CH - 1:
                        sum_flag(i + 1)
                    products(0, 1, range(KC)).then_inc(gu_ready, 1)
            pe.wait_ge(flagged, NI + 1)
            pe.reg_load(flag, ff.flags[0:1, NI:NI + 1].bitcast(mybir.dt.int32))
            for t in range(NT):
                if t >= 2:
                    pe.wait_ge(z_scaled, t - 1)

                def product(a, b, i):
                    return pe.matmul(psum[:, 4 + t % 2, :],
                                     ff.g_hl[a][0:rows[i], i, P * t:P * t + P],
                                     ff.wd_hl[b][0:rows[i], i, :],
                                     start=(a, b, i) == (0, 0, 0), stop=(a, i) == (1, NI - 1))

                for i in range(NI):
                    if t == 0:
                        pe.wait_ge(wd_high, i + 1)
                        pe.wait_ge(g_low, CH * (i + 1))
                    product(0, 0, i)
                    if i < NI - 1:
                        product(1, 0, i)
                with pe.If(flag):
                    if t == 0:
                        pe.wait_ge(wd_low, NI)
                    for i in range(NI):
                        product(0, 1, i)
                product(1, 0, NI - 1).then_inc(z_ready, 1)

        def product(n):
            i, c = n // CH, n % CH
            return (ff.prod[0:rows[i], n % 2, :],
                    *[a[0:rows[i], i, 512 * c:512 * c + 512] for a in ff.g_hl])

        @block.scalar
        def _(act):
            def high(n):
                act.wait_ge(prod_ready, n + 1)
                src, h, _ = product(n)
                act.copy(h, src).then_inc(g_high, 1)

            def cut_out(i):
                act.copy(ff.wd_hl[0][0:rows[i], i, :], ff.wd_raw[0:rows[i], i, :]).then_inc(wd_high, 1)

            def copy_flag(i):
                act.wait_ge(summed, i + 1)
                act.copy(ff.flags[0:1, i:i + 1], psum[0:1, 6, 0:1]).then_inc(flagged, 1)

            def weigh_out(k):
                act.wait_ge(probed, 2 * k + 2)
                if k == 0:
                    act.wait_ge(cleared, 1)
                low = ff.probe_low[k % 2][0:rows[k], :]
                act.activation(low, low, ACT.Abs,
                               accum_out=ff.low_out[0:rows[k], k:k + 1]).then_inc(out_weighed, 1)

            copy_flag(0)
            for n in range(CH * NI):
                i = n // CH
                act.wait_ge(gu_ready, n + 1)
                if n >= 2:
                    act.wait_ge(prod_ready, n - 1)
                act.activation(ff.silu[0:rows[i], n % 2, :], psum[0:rows[i], 2 * (n % 3), :], ACT.Silu,
                               scale=s_gate[0:rows[i], :]).then_inc(silu_ready, 1)
                if n % CH == CH - 1 and i + 2 < NI:
                    ff.cut_high(act, act.copy, i + 2)
                if n == CH * NI - 1:
                    act.wait_ge(ff.wd_arrived, 32)
                    cut_out(0)
                    cut_out(1)
                high(n)
                if n % CH == CH - 1 and i + 2 < NI:
                    ff.weigh(act, i + 2)
                if 0 <= n - FIRST < NI:
                    weigh_out(n - FIRST)
                if n % CH == 0:
                    copy_flag(i + 1)
            for i in range(2, NI):
                cut_out(i)
            for t in range(NT):
                act.wait_ge(var_ready, t + 1)
                norm_root(act, ff.stats[:, t % 2, :], eps).then_inc(dev_ready, 1)

        @block.vector
        def _(dve):
            link = Chain(dve, chain_s)
            dve.memset(ff.low_out[:, :], 0.0).then_inc(cleared, 1)
            for n in range(CH * NI):
                i = n // CH
                dve.wait_ge(silu_ready, n + 1)
                if n >= 2:
                    dve.wait_ge(g_low, n - 1)
                src, h, lo = product(n)
                dve.scalar_tensor_tensor(out=src, in0=psum[0:rows[i], 2 * (n % 3) + 1, :],
                                         scalar=s_up[0:rows[i], :], in1=ff.silu[0:rows[i], n % 2, :],
                                         op0=ALU.mult, op1=ALU.mult).then_inc(prod_ready, 1)
                if n % CH == CH - 1 and i + 2 < NI:
                    ff.cut_low(dve, i + 2)
                dve.wait_ge(g_high, n + 1)
                dve.tensor_tensor(lo, src, h.bitcast(F32), ALU.subtract).then_inc(g_low, 1)
                if n == FIRST + NI:
                    dve.wait_ge(out_weighed, NI)
                    dve.tensor_reduce(ff.low_all[:, :], ff.low_out[:, :], AX, ALU.add)\
                        .then_inc(all_weighed, 1)
            dve.wait_ge(gu_ready, CH * NI)
            dve.wait_ge(g_low, CH * NI)
            for i in range(NI):
                dve.wait_ge(wd_high, i + 1)
                dve.tensor_tensor(ff.wd_hl[1][0:rows[i], i, :], ff.wd_raw[0:rows[i], i, :],
                                  ff.wd_hl[0][0:rows[i], i, :].bitcast(F32), ALU.subtract)\
                    .then_inc(wd_low, 1)
            for t in range(NT):
                dve.wait_ge(z_ready, t + 1)
                if t >= 2:
                    dve.wait_ge(x_ready, t - 1)
                dve.scalar_tensor_tensor(out=ff.h[:, t % 2, :], in0=psum[:, 4 + t % 2, :],
                                         scalar=s_down, in1=x_tok[:, t, :], op0=ALU.mult,
                                         op1=ALU.add).then_inc(z_scaled, 1)
                dve.wait_ge(z_scaled, t + 1)
                norm_stats(dve, link, ff.h[:, t % 2, :], ff.stats[:, t % 2, :]).then_inc(var_ready, 1)
                dve.wait_ge(dev_ready, t + 1)
                norm_apply(dve, link, x_tok[:, t, :], ff.h[:, t % 2, :], ff.stats[:, t % 2, :])\
                    .then_inc(x_ready, 1)

        @block.gpsimd
        def _(pool):
            pool.wait_ge(ff.wd_arrived, 32)
            for i in range(NI):
                if i:
                    pool.wait_ge(probed, 2 * i)
                pool.tensor_copy(ff.probe[0:rows[i], :], ff.wd_raw[0:rows[i], i, :]).then_inc(probed, 1)
                pool.wait_ge(probed, 2 * i + 1)
                if i >= 2:
                    pool.wait_ge(out_weighed, i - 1)
                pool.tensor_tensor(ff.probe_low[i % 2][0:rows[i], :], ff.wd_raw[0:rows[i], i, :],
                                   ff.probe[0:rows[i], :].bitcast(F32), ALU.subtract).then_inc(probed, 1)


def _rope(base):
    theta = (1.0 / np.float32(base) ** (np.arange(0, D, 2, dtype=np.float32) / np.float32(D))).astype(np.float32)
    angle = np.outer(np.arange(T, dtype=np.float32), theta).astype(np.float32)
    angle = np.concatenate([angle, angle], axis=1).T
    return (np.tile(np.cos(angle), (HPT, 1)).astype(np.float32),
            np.tile(np.sin(angle), (HPT, 1)).astype(np.float32))


def _constants():
    cos0, sin0 = _rope(10000.0)
    cos1, sin1 = _rope(500000.0)
    rot = np.zeros((P, P), np.float32)
    for h in range(HPT):
        for i in range(D // 2):
            rot[D * h + D // 2 + i, D * h + i] = -1.0
            rot[D * h + i, D * h + D // 2 + i] = 1.0
    eye = np.eye(P, dtype=np.float32)
    hm_k = (np.arange(P)[:, None] // D == np.arange(HPT)[None]).astype(np.float32)
    hm_v = (np.arange(HPT * ADP)[:, None] // ADP == np.arange(HPT)[None]).astype(np.float32)
    return dict(cos0=cos0, sin0=sin0, cos1=cos1, sin1=sin1, rot=rot, ident=eye, hm_k=hm_k, hm_v=hm_v)


def kernel(**inputs):
    import concourse.bacc as bacc
    from concourse.bass_utils import run_bass_kernel_spmd as run

    a = {k: np.asarray(v) for k, v in inputs.items()}
    tiles = lambda w: np.ascontiguousarray(w.reshape(KC, P, -1).transpose(1, 0, 2).reshape(P, -1))
    col = lambda v: np.broadcast_to(np.asarray(v).reshape(1, -1), (P, np.asarray(v).size)).copy()
    w_in = np.zeros((NI, P, 2, KC, P), np.float32)
    for u, name in enumerate(["L1_ffn_gate_w", "L1_ffn_up_w"]):
        wT = a[name].T.reshape(KC, P, INTER)
        for i in range(NI):
            n = min(P, INTER - P * i)
            w_in[i, :, u, :, 0:n] = wT[:, :, P * i:P * i + n].transpose(1, 0, 2)
    x0 = a["L0_attn_x"][0]
    d = dict(
        x=x0, xT=x0.T, w0=a["L0_attn_w_attn"].T, wo0=a["L0_attn_w_proj"].T,
        a_repT=np.tile(a["L0_attn_adapter_wte"].T, (1, HPT)), gating=col(a["L0_attn_gating"]),
        f_wqT=tiles(a["L0_ffn_Wq"].T), f_wrT=a["L0_ffn_Wr"].T, f_akeyT=a["L0_ffn_aux_keys"].T,
        f_avT=tiles(a["L0_ffn_aux_values"].T), f_wvdT=tiles(a["L0_ffn_Wvd"].T),
        f_wvuT=a["L0_ffn_Wvu"].T, f_wu1T=tiles(a["L0_ffn_Wu1"].T), f_wu2T=a["L0_ffn_Wu2"].T,
        f_bu1=a["L0_ffn_bu1"].reshape(HU, 1), f_logrel=col(a["L0_ffn_log_rel"]),
        f_bu2=col(a["L0_ffn_bu2"]), f_gate_w1=col(a["L0_ffn_gate_w1"]),
        f_gate_bias=col(a["L0_ffn_gate_bias"]),
        w1=np.concatenate([a["L1_attn_Wq"], a["L1_attn_Wk"], a["L1_attn_Wv"]], axis=1),
        wo1=a["L1_attn_Wo"], w_in=w_in.reshape(NI, P, -1), w_down=a["L1_ffn_down_w"].T,
        s_gate=col(a["L1_ffn_gate_scale"]), s_up=col(a["L1_ffn_up_scale"]),
        s_down=col(a["L1_ffn_down_scale"]), **_constants())
    nc = bacc.Bacc("TRN2", target_bir_lowering=False, num_devices=1)
    arrays, aps = {}, {}
    for name, v in d.items():
        v = np.ascontiguousarray(v)
        arrays[f"in_{name}"] = v
        aps[name] = nc.dram_tensor(f"in_{name}", v.shape, mybir.dt.from_np(v.dtype),
                                   kind="ExternalInput").ap()
    out = nc.dram_tensor("out", [T, C], F32, kind="ExternalOutput").ap()
    build(nc, aps, out)
    r = run(nc, [arrays], core_ids=[0])
    return np.asarray(r.results[0]["out"]).reshape(1, T, C)
```
